# Optimizing a Trainium2 kernel written in Bass

```python
import numpy as np
import jax
import jax.numpy as jnp

def _softmax(x, axis=-1):
    return jax.nn.softmax(x, axis=axis)

def _gelu(x):
    return jax.nn.gelu(x, approximate=True)

def _silu(x):
    return jax.nn.silu(x)

def _sigmoid(x):
    return jax.nn.sigmoid(x)

def _layernorm(x, axis=-1, eps=1e-05):
    m = jnp.mean(x, axis=axis, keepdims=True)
    v = jnp.var(x, axis=axis, keepdims=True)
    return (x - m) / jnp.sqrt(v + eps)

def _scatter_add(tgt, idx, src, axis=0):
    return tgt.at[idx].add(src)

def _segment_sum(src, seg, n):
    return jax.ops.segment_sum(src, seg, n)
kernel_name = 'mk_adaln_d1_jaxref_r8_87807a'

def setup_inputs(seed: int=0):
    np.random.seed(seed)
    _w = jnp.asarray

    def _L0_attn_setup():
        import jax, jax.numpy as jnp
        import numpy as np
        D_MODEL, EXPAND, D_STATE, D_CONV, HEADDIM = (128, 2, 64, 4, 64)
        D_INNER = EXPAND * D_MODEL
        NHEADS = D_INNER // HEADDIM
        CONV_DIM = D_INNER + 2 * D_STATE
        D_IN_PROJ = 2 * D_INNER + 2 * D_STATE + NHEADS
        EPS = 1e-05

        def _layernorm(x, w, b):
            mu = jnp.mean(x, axis=-1, keepdims=True)
            var = jnp.mean(jnp.square(x - mu), axis=-1, keepdims=True)
            return (x - mu) * jax.lax.rsqrt(var + EPS) * w + b

        def _mamba2(x, in_proj_w, conv_w, conv_b, dt_bias, A_log, D, norm_w, out_proj_w):
            Bt, L, _ = x.shape
            zxbcdt = x @ in_proj_w.T
            z = zxbcdt[..., :D_INNER]
            xBC = zxbcdt[..., D_INNER:D_INNER + CONV_DIM]
            dt = jax.nn.softplus(zxbcdt[..., D_INNER + CONV_DIM:] + dt_bias)
            xp = jnp.pad(xBC, ((0, 0), (D_CONV - 1, 0), (0, 0)))
            conv = conv_b
            for k in range(D_CONV):
                conv = conv + xp[:, k:k + L, :] * conv_w[:, k]
            xBC = jax.nn.silu(conv)
            xs = xBC[..., :D_INNER].reshape(Bt, L, NHEADS, HEADDIM)
            Bm = xBC[..., D_INNER:D_INNER + D_STATE]
            Cm = xBC[..., D_INNER + D_STATE:]
            A = -jnp.exp(A_log)

            def step(h, inp):
                x_t, dt_t, B_t, C_t = inp
                dA = jnp.exp(dt_t * A)
                h = h * dA[:, :, None, None] + (dt_t[:, :, None] * x_t)[..., None] * B_t[:, None, None, :]
                y = jnp.einsum('bhpn,bn->bhp', h, C_t)
                return (h, y)
            h0 = jnp.zeros((Bt, NHEADS, HEADDIM, D_STATE), x.dtype)
            xsT = jnp.moveaxis(xs, 1, 0)
            dtT = jnp.moveaxis(dt, 1, 0)
            BT = jnp.moveaxis(Bm, 1, 0)
            CT = jnp.moveaxis(Cm, 1, 0)
            _, ys = jax.lax.scan(step, h0, (xsT, dtT, BT, CT))
            y = jnp.moveaxis(ys, 0, 1) + xs * D[None, None, :, None]
            y = y.reshape(Bt, L, D_INNER)
            y = y * jax.nn.silu(z)
            y = y * jax.lax.rsqrt(jnp.mean(jnp.square(y), axis=-1, keepdims=True) + EPS) * norm_w
            return y @ out_proj_w.T
        key = jax.random.key(seed)
        ks = jax.random.split(key, 16)
        s = 0.02
        inp = {'x': jax.random.normal(ks[0], (2, 256, D_MODEL), jnp.float32), 'ln1_w': jnp.ones((D_MODEL,), jnp.float32), 'ln1_b': jnp.zeros((D_MODEL,), jnp.float32), 'in_proj_w': jax.random.normal(ks[1], (D_IN_PROJ, D_MODEL), jnp.float32) * s, 'conv_w': jax.random.normal(ks[2], (CONV_DIM, D_CONV), jnp.float32) * 0.3, 'conv_b': jnp.zeros((CONV_DIM,), jnp.float32), 'dt_bias': jnp.log(jnp.expm1(jnp.exp(jax.random.uniform(ks[3], (NHEADS,), jnp.float32, jnp.log(0.001), jnp.log(0.1))))), 'A_log': jnp.log(jax.random.uniform(ks[4], (NHEADS,), jnp.float32, 1.0, 16.0)), 'D': jnp.ones((NHEADS,), jnp.float32), 'norm_w': jnp.ones((D_INNER,), jnp.float32), 'out_proj_w': jax.random.normal(ks[5], (D_MODEL, D_INNER), jnp.float32) * s, 'ln2_w': jnp.ones((D_MODEL,), jnp.float32), 'ln2_b': jnp.zeros((D_MODEL,), jnp.float32), 'mlp_w1': jax.random.normal(ks[6], (4 * D_MODEL, D_MODEL), jnp.float32) * s, 'mlp_b1': jnp.zeros((4 * D_MODEL,), jnp.float32), 'mlp_w2': jax.random.normal(ks[7], (D_MODEL, 4 * D_MODEL), jnp.float32) * s, 'mlp_b2': jnp.zeros((D_MODEL,), jnp.float32)}
        return inp
    _L0_attn_in = _L0_attn_setup()

    def _L0_ffn_setup():
        import jax, jax.numpy as jnp
        import numpy as np
        TOP_K = 2
        EPS = 1e-09
        key = jax.random.key(seed)
        ks = jax.random.split(key, 6)
        B, T, D, H, E = (4, 256, 128, 256, 8)
        x = jax.random.normal(ks[0], (B, T, D), dtype=jnp.float32)
        Wg = jax.random.normal(ks[1], (E, D), dtype=jnp.float32) * 0.02
        W1 = jax.random.normal(ks[2], (E, 2 * H, D), dtype=jnp.float32) * 0.02
        b1 = jax.random.normal(ks[3], (E, 2 * H), dtype=jnp.float32) * 0.02
        Wo = jax.random.normal(ks[4], (D, H), dtype=jnp.float32) * 0.02
        bo = jax.random.normal(ks[5], (D,), dtype=jnp.float32) * 0.02
        return {'x': x, 'Wg': Wg, 'W1': W1, 'b1': b1, 'Wo': Wo, 'bo': bo}
    _L0_ffn_in = _L0_ffn_setup()
    _L0_c = _w((lambda *s: np.random.randn(*s).astype(np.float32) * 0.05)(4, 128))
    _L0_wmod = _w((lambda *s: np.random.randn(*s).astype(np.float32) * 0.05)(128, 6 * 128) * 128 ** (-0.5))
    _d = {'L0_attn_x': _L0_attn_in['x'], 'L0_attn_ln1_w': _L0_attn_in['ln1_w'], 'L0_attn_ln1_b': _L0_attn_in['ln1_b'], 'L0_attn_in_proj_w': _L0_attn_in['in_proj_w'], 'L0_attn_conv_w': _L0_attn_in['conv_w'], 'L0_attn_conv_b': _L0_attn_in['conv_b'], 'L0_attn_dt_bias': _L0_attn_in['dt_bias'], 'L0_attn_A_log': _L0_attn_in['A_log'], 'L0_attn_D': _L0_attn_in['D'], 'L0_attn_norm_w': _L0_attn_in['norm_w'], 'L0_attn_out_proj_w': _L0_attn_in['out_proj_w'], 'L0_attn_ln2_w': _L0_attn_in['ln2_w'], 'L0_attn_ln2_b': _L0_attn_in['ln2_b'], 'L0_attn_mlp_w1': _L0_attn_in['mlp_w1'], 'L0_attn_mlp_b1': _L0_attn_in['mlp_b1'], 'L0_attn_mlp_w2': _L0_attn_in['mlp_w2'], 'L0_attn_mlp_b2': _L0_attn_in['mlp_b2'], 'L0_ffn_Wg': _L0_ffn_in['Wg'], 'L0_ffn_W1': _L0_ffn_in['W1'], 'L0_ffn_b1': _L0_ffn_in['b1'], 'L0_ffn_Wo': _L0_ffn_in['Wo'], 'L0_ffn_bo': _L0_ffn_in['bo'], 'L0_c': _L0_c, 'L0_wmod': _L0_wmod}
    _x0 = _d['L0_attn_x']
    _d['L0_attn_x'] = jax.random.normal(jax.random.fold_in(jax.random.key(seed), 1), (4, 1024, 128), dtype=_x0.dtype)
    del _x0
    return _d

def reference(L0_attn_x, L0_attn_ln1_w, L0_attn_ln1_b, L0_attn_in_proj_w, L0_attn_conv_w, L0_attn_conv_b, L0_attn_dt_bias, L0_attn_A_log, L0_attn_D, L0_attn_norm_w, L0_attn_out_proj_w, L0_attn_ln2_w, L0_attn_ln2_b, L0_attn_mlp_w1, L0_attn_mlp_b1, L0_attn_mlp_w2, L0_attn_mlp_b2, L0_ffn_Wg, L0_ffn_W1, L0_ffn_b1, L0_ffn_Wo, L0_ffn_bo, L0_c, L0_wmod):

    def _L0_attn_ref(x, ln1_w, ln1_b, in_proj_w, conv_w, conv_b, dt_bias, A_log, D, norm_w, out_proj_w, ln2_w, ln2_b, mlp_w1, mlp_b1, mlp_w2, mlp_b2):
        import jax, jax.numpy as jnp
        import numpy as np
        D_MODEL, EXPAND, D_STATE, D_CONV, HEADDIM = (128, 2, 64, 4, 64)
        D_INNER = EXPAND * D_MODEL
        NHEADS = D_INNER // HEADDIM
        CONV_DIM = D_INNER + 2 * D_STATE
        D_IN_PROJ = 2 * D_INNER + 2 * D_STATE + NHEADS
        EPS = 1e-05

        def _layernorm(x, w, b):
            mu = jnp.mean(x, axis=-1, keepdims=True)
            var = jnp.mean(jnp.square(x - mu), axis=-1, keepdims=True)
            return (x - mu) * jax.lax.rsqrt(var + EPS) * w + b

        def _mamba2(x, in_proj_w, conv_w, conv_b, dt_bias, A_log, D, norm_w, out_proj_w):
            Bt, L, _ = x.shape
            zxbcdt = x @ in_proj_w.T
            z = zxbcdt[..., :D_INNER]
            xBC = zxbcdt[..., D_INNER:D_INNER + CONV_DIM]
            dt = jax.nn.softplus(zxbcdt[..., D_INNER + CONV_DIM:] + dt_bias)
            xp = jnp.pad(xBC, ((0, 0), (D_CONV - 1, 0), (0, 0)))
            conv = conv_b
            for k in range(D_CONV):
                conv = conv + xp[:, k:k + L, :] * conv_w[:, k]
            xBC = jax.nn.silu(conv)
            xs = xBC[..., :D_INNER].reshape(Bt, L, NHEADS, HEADDIM)
            Bm = xBC[..., D_INNER:D_INNER + D_STATE]
            Cm = xBC[..., D_INNER + D_STATE:]
            A = -jnp.exp(A_log)

            def step(h, inp):
                x_t, dt_t, B_t, C_t = inp
                dA = jnp.exp(dt_t * A)
                h = h * dA[:, :, None, None] + (dt_t[:, :, None] * x_t)[..., None] * B_t[:, None, None, :]
                y = jnp.einsum('bhpn,bn->bhp', h, C_t)
                return (h, y)
            h0 = jnp.zeros((Bt, NHEADS, HEADDIM, D_STATE), x.dtype)
            xsT = jnp.moveaxis(xs, 1, 0)
            dtT = jnp.moveaxis(dt, 1, 0)
            BT = jnp.moveaxis(Bm, 1, 0)
            CT = jnp.moveaxis(Cm, 1, 0)
            _, ys = jax.lax.scan(step, h0, (xsT, dtT, BT, CT))
            y = jnp.moveaxis(ys, 0, 1) + xs * D[None, None, :, None]
            y = y.reshape(Bt, L, D_INNER)
            y = y * jax.nn.silu(z)
            y = y * jax.lax.rsqrt(jnp.mean(jnp.square(y), axis=-1, keepdims=True) + EPS) * norm_w
            return y @ out_proj_w.T
        res = x
        h = _layernorm(x, ln1_w, ln1_b)
        h = _mamba2(h, in_proj_w, conv_w, conv_b, dt_bias, A_log, D, norm_w, out_proj_w)
        x = res + h
        res = x
        h = _layernorm(x, ln2_w, ln2_b)
        h = jax.nn.gelu(h @ mlp_w1.T + mlp_b1, approximate=False) @ mlp_w2.T + mlp_b2
        return res + h

    def _L0_ffn_ref(x, Wg, W1, b1, Wo, bo):
        import jax, jax.numpy as jnp
        import numpy as np
        TOP_K = 2
        EPS = 1e-09
        E = Wg.shape[0]
        gate_logits = jnp.einsum('btd,ed->bte', x, Wg)
        gate_scores = jax.nn.softmax(gate_logits, axis=-1)
        topk_val, topk_idx = jax.lax.top_k(gate_scores, TOP_K)
        topk_val = topk_val / (topk_val.sum(axis=-1, keepdims=True) + EPS)
        comb = (jax.nn.one_hot(topk_idx, E, dtype=x.dtype) * topk_val[..., None]).sum(axis=-2)
        out = jnp.zeros_like(x)
        for e in range(E):
            h = jnp.einsum('btd,hd->bth', x, W1[e]) + b1[e]
            a, b = jnp.split(h, 2, axis=-1)
            g = a * jax.nn.sigmoid(b)
            eo = jnp.einsum('bth,dh->btd', g, Wo) + bo
            out = out + eo * comb[..., e:e + 1]
        return out
    x = L0_attn_x
    mod = (_silu(L0_c) @ L0_wmod).reshape(L0_c.shape[0], 6, 1, -1)
    sa, ca, ga, sb, cb, gb = (mod[:, 0], mod[:, 1], mod[:, 2], mod[:, 3], mod[:, 4], mod[:, 5])
    ga = (2 * (ga >= 0) - 1) * jnp.maximum(jnp.abs(ga), 0.25)
    gb = (2 * (gb >= 0) - 1) * jnp.maximum(jnp.abs(gb), 0.25)
    h = _layernorm(x, axis=-1) * (1 + ca) + sa
    x = x + ga * _L0_attn_ref(h, L0_attn_ln1_w, L0_attn_ln1_b, L0_attn_in_proj_w, L0_attn_conv_w, L0_attn_conv_b, L0_attn_dt_bias, L0_attn_A_log, L0_attn_D, L0_attn_norm_w, L0_attn_out_proj_w, L0_attn_ln2_w, L0_attn_ln2_b, L0_attn_mlp_w1, L0_attn_mlp_b1, L0_attn_mlp_w2, L0_attn_mlp_b2)
    h = _layernorm(x, axis=-1) * (1 + cb) + sb
    x = x + gb * _L0_ffn_ref(h, L0_ffn_Wg, L0_ffn_W1, L0_ffn_b1, L0_ffn_Wo, L0_ffn_bo)
    return x

_drawn_inputs = setup_inputs


def setup_inputs(seed=0):
    import zlib

    import numpy as np

    out = dict(_drawn_inputs(seed))
    spreads = {'L0_attn_ln1_w': (1.0, 0.6),
     'L0_attn_ln1_b': (0.0, 0.8),
     'L0_attn_conv_b': (0.0, 0.1),
     'L0_attn_D': (1.0, 0.6),
     'L0_attn_norm_w': (1.0, 0.6),
     'L0_attn_ln2_w': (1.0, 0.6),
     'L0_attn_ln2_b': (0.0, 0.8),
     'L0_attn_mlp_b1': (0.0, 0.8),
     'L0_attn_mlp_b2': (0.0, 0.303)}
    factors = {'L0_attn_dt_bias': 8.0,
     'L0_attn_A_log': 8.0,
     'L0_attn_mlp_w1': 4.051,
     'L0_attn_mlp_w2': 3.649,
     'L0_ffn_Wg': 8.0,
     'L0_ffn_W1': 8.0,
     'L0_ffn_b1': 8.0,
     'L0_ffn_Wo': 8.0,
     'L0_ffn_bo': 8.0}
    for name, (base, spread) in spreads.items():
        noise = np.random.default_rng([zlib.crc32(name.encode()), seed]).standard_normal(out[name].shape)
        drawn = base * np.exp(spread * noise) if base else spread * noise
        out[name] = jnp.asarray(drawn.astype(out[name].dtype))
    for name, factor in factors.items():
        out[name] = (out[name] * factor).astype(out[name].dtype)
    return out
```

```python
from contextlib import ExitStack

import concourse.bass as bass
from concourse import mybir

F32 = mybir.dt.float32
F32R = mybir.dt.float32r
ALU = mybir.AluOpType
ACT = mybir.ActivationFunctionType
AX = mybir.AxisListType

P = 128
LN_EPS = 1e-5
TOPK_EPS = 1e-9
PAD = -3.0e38
TAKEN = 3.0e38
ATANH = (13, 11, 9, 7, 5, 3)
DT_STEPS = 8 + len(ATANH)
GATE_STEPS = 9
GATE_EXP = 3

EVENTS = """
x_loaded xa_stats xa_mv xa_var xa_rstd xa_norm xa_scaled h_ready
h_stats h_mv h_var h_rstd n1_ready n1T_ps u_ready uhi_ready ulo_ready
dt_ps dt_chain dt_exp a_ready xbc_ps xbc_read conv_tap halo_saved z_ps z_silu xs_silu bc_silu
xtm_ps xdt_ready btm_ps btm_ready cum_ps ecs_ready g_ps gm_ready
m1a_ready seg_ps L_ready W_ready int_ps yt_ready yi_ps y_ready yz_ready
ssq_ready y_var y_rstd xde_ready st_ps Hd_ready H_ready
yzT_ps yzT_ready op_ps x2_ready
x2_stats x2_mv x2_var x2_rstd n2_ready n2T_ps v_ready vhi_ready vlo_ready x2b_ready
hid_ps gelu_ready mlp_ps x3_ready x3_scaled x4_ready
x4_stats x4_mv x4_var x4_rstd n4_ready n4T_ps w_ready whi_ready wlo_ready
logit_ps logit_ready gate_chain ex_ready comb_ready combT_ps combT_hi combT_lo
kept combB_ps combB_ready ab_ps tanh_ready aw_ready g_ready acc_added
wo_ps o_bias o_scaled o_ready stored
""".split()
SETUP = "loads silu_c_ready silu_rows_ready mod_ps mod_read masks_filled masks_made split_hi vector_ready scalar_ready gpsimd_ready A_exp setup_chain".split()
N_LOADS = 24


def bcast(ap, where, shape):
    return ap.unsqueeze(where).to_broadcast(shape)


def build(nc, d, out):
    B, T, D = d["x"].shape
    NT = T // P
    E = d["moe_b1"].shape[1]
    DI = d["out_projT"].shape[0]
    NH = d["A_log"].shape[0]
    HD = DI // NH
    NS = (d["conv_w"].shape[1] * P - DI) // 2
    MH = d["mlp_w1T"].shape[1]
    MQ = MH // P
    H2 = d["moe_woT"].shape[0]
    HK = H2 // P
    CB = d["conv_w"].shape[1]
    TAPS = d["conv_w"].shape[2]
    HALO = TAPS - 1
    NU = E * HK
    DP = d["in_projT"].shape[1]
    ZX = DP - NH
    W4 = B * P
    assert D == P and B == 4 and NH == 4 and E == 8 and CB == 3 and HK == 2

    with ExitStack() as ctx:
        def sb(name, shape, dt=F32):
            return ctx.enter_context(nc.sbuf_tensor(name, shape, dt))

        wdt = sb("wdt", [P, NH]); wp_hi = sb("wp_hi", [P, ZX], F32R); wp_lo = sb("wp_lo", [P, ZX], F32R)
        w1m_hi = sb("w1m_hi", [P, MH], F32R); w1m_lo = sb("w1m_lo", [P, MH], F32R)
        w2m = sb("w2m", [P, MQ, D])
        wexp_hi = sb("wexp_hi", [P, E * 2 * H2], F32R); wexp_lo = sb("wexp_lo", [P, E * 2 * H2], F32R)
        wo = sb("wo", [P, HK, D]); wout = sb("wout", [P, DI // P, D]); wg = sb("wg", [P, E])
        ln1w = sb("ln1w", [P, 1]); ln1b = sb("ln1b", [P, 1]); ln2w = sb("ln2w", [P, 1]); ln2b = sb("ln2b", [P, 1])
        convw = sb("convw", [P, CB, TAPS]); convb = sb("convb", [P, CB])
        dtb = sb("dtb", [P, NH]); A_row = sb("A_row", [P, NH]); A_neg = sb("A_neg", [P, NH])
        Dcol = sb("Dcol", [P, DI // P]); Ddiag = sb("Ddiag", [P, DI // P, P])
        normw = sb("normw", [P, DI // P]); b1m = sb("b1m", [P, MQ]); b2row = sb("b2row", [P, D])
        b1e = sb("b1e", [P, E, 2 * HK]); b1e_half = sb("b1e_half", [P, E, 2 * HK]); borow = sb("borow", [P, D])
        cT = sb("cT", [P, B]); silu_c = sb("silu_c", [P, B])
        ones = sb("ones", [P, P]); ident = sb("ident", [P, P])
        upto = sb("upto", [P, P])
        after = sb("after", [P, P])
        pick_r = sb("pick_r", [64, E, P], F32R)
        minus_half = sb("minus_half", [P, B])
        sa = sb("sa", [P, B, D]); ca1 = sb("ca1", [P, B, D]); ga = sb("ga", [P, B, D]); gb = sb("gb", [P, B, D])
        sbT = sb("sbT", [P, B]); cb1T = sb("cb1T", [P, B])

        xt = sb("xt", [P, B, D]); stats = sb("stats", [P, 4, B, 6])
        mva = sb("mva", [P, B, 2]); mvh = sb("mvh", [P, B, 2]); mv2 = sb("mv2", [P, B, 2]); mv4 = sb("mv4", [P, B, 2])
        var_e = sb("var_e", [P, 5, B]); ra = sb("ra", [P, B]); rh = sb("rh", [P, B]); r2 = sb("r2", [P, B]); r4 = sb("r4", [P, B])
        na = sb("na", [P, B, D]); h = sb("h", [P, B, D]); nrm = sb("nrm", [P, B, D])
        u = sb("u", [P, W4]); u_hi = sb("u_hi", [P, W4], F32R); u_lo = sb("u_lo", [P, W4], F32R)
        dtv = sb("dtv", [P, B, NH]); nab = sb("nab", [P, B, NH]); ew = sb("ew", [P, B, NH]); den = sb("den", [P, B, NH])
        rden = sb("rden", [P, B, NH]); sw = sb("sw", [P, B, NH]); s2 = sb("s2", [P, B, NH]); pl = sb("pl", [P, B, NH])
        relu = sb("relu", [P, B, NH]); dt = sb("dt", [P, B, NH]); a = sb("a", [P, B, NH])
        xbc = sb("xbc", [P, CB, B, HALO + P]); cv = sb("cv", [P, CB, B, P])
        xs = sb("xs", [P, DI // P, W4]); Bc = sb("Bc", [NS, W4]); Cc = sb("Cc", [NS, W4])
        sz = sb("sz", [P, B, DI]); xdt = sb("xdt", [P, B, DI]); xde = sb("xde", [P, B, DI]); Btm = sb("Btm", [P, B, NS])
        ecs = sb("ecs", [P, 3, B, NH])
        gm = sb("gm", [P, B, P]); m1a = sb("m1a", [P, 2, NH, P]); L = sb("L", [P, 2, NH, P]); Wt = sb("Wt", [P, 2, NH, P])
        yt = sb("yt", [P, B, DI]); yz = sb("yz", [P, B, DI])
        ssq = sb("ssq", [P, B]); ry = sb("ry", [P, B])
        H = sb("H", [NS, B, DI]); Hd = sb("Hd", [NS, B, DI])
        yzT = sb("yzT", [P, DI // P, W4]); x2 = sb("x2", [P, B, D]); x2b = sb("x2b", [P, B, D])
        v, v_hi, v_lo = u, u_hi, u_lo
        gl = sb("gl", [P, MQ, W4]); x3 = sb("x3", [P, B, D]); x4 = sb("x4", [P, B, D])
        w = sb("w", [P, W4]); w_hi = sb("w_hi", [P, W4], F32R); w_lo = sb("w_lo", [P, W4], F32R)
        NP_ = E + 6
        lg = sb("lg", [P, B, NP_]); mx = sb("mx", [P, B, 8]); top = sb("top", [P, B, 8]); rep = sb("rep", [P, B, NP_])
        exs = sb("exs", [P, B, E]); ex = sb("ex", [P, B, E]); Z = sb("Z", [P, B]); sel = sb("sel", [P, B, E])
        dsum = sb("dsum", [P, B]); deps = sb("deps", [P, B]); rinv = sb("rinv", [P, B]); csum = sb("csum", [P, B])
        comb = sb("comb", [P, B, E]); combT = sb("combT", [64, W4], F32R)
        csumk = sb("csumk", [P, B]); combB = sb("combB", [P, 2, W4])
        tg = sb("tg", [P, 2, W4]); aw = sb("aw", [P, 2, W4]); acc = sb("acc", [P, HK, W4])
        late = sb("late", [P, 8 * W4])
        gg = late[:, 0:4 * W4].rearrange("p (q w) -> p q w", q=4)
        x4k, o1, o2, ot = (late[:, (4 + q) * W4:(5 + q) * W4].rearrange("p (b d) -> p b d", b=B) for q in range(4))
        wexp = late
        raw = gl[:, :, :].rearrange("p q w -> p (q w)")
        wp, w1m = raw[:, 0:ZX], raw[:, ZX:ZX + MH]
        wmod = xde[:, :, :].rearrange("p b c -> p (b c)")[:, 0:6 * D]
        silu_row, gsign = yz[:, 0:2, :].rearrange("p b (c d) -> p (b c) d", d=D), x2
        pick = combB[0:64, :, :].rearrange("p a (e w) -> p (a e) w", w=P)

        ring = [ctx.enter_context(nc.psum_tensor(f"ring{i}", [P, W4], F32)) for i in range(3)]
        ab = [ctx.enter_context(nc.psum_tensor(f"ab{i}", [P, W4], F32)) for i in range(4)]
        cbps = ctx.enter_context(nc.psum_tensor("cbps", [P, W4], F32))
        S = {e: ctx.enter_context(nc.semaphore(e)) for e in SETUP + EVENTS}
        block = ctx.enter_context(nc.Block())

        R_N1T, R_DT, R_XBC, R_Z, R_XTM, R_BTM, R_CUM, R_G = 0, 1, 2, 5, 7, 9, 10, 11
        R_PAIR = (12, 16)
        R_ST, R_YZT, R_OP, R_N2T, R_HID, R_MLP, R_N4T, R_LOGIT, R_COMBT, R_OUT = 20, 22, 24, 25, 26, 30, 31, 32, 33, 35
        TURN = 36
        readers = {
            0: (S["u_ready"], 1, 1), 1: (S["dt_chain"], DT_STEPS, 1),
            2: (S["xbc_read"], CB, 1), 3: (S["xbc_read"], CB, 2), 4: (S["xbc_read"], CB, 3),
            5: (S["z_silu"], 2, 1), 6: (S["z_silu"], 2, 2), 7: (S["xdt_ready"], 2, 1), 8: (S["xdt_ready"], 2, 2),
            9: (S["btm_ready"], 1, 1), 10: (S["ecs_ready"], 1, 1), 11: (S["gm_ready"], 1, 1),
            12: (S["L_ready"], 4, 1), 13: (S["L_ready"], 4, 2), 14: (S["yt_ready"], 2, 1), 15: (S["y_ready"], 2, 1),
            16: (S["L_ready"], 4, 3), 17: (S["L_ready"], 4, 4), 18: (S["yt_ready"], 2, 2), 19: (S["y_ready"], 2, 2),
            20: (S["H_ready"], 2, 1), 21: (S["H_ready"], 2, 2), 22: (S["yzT_ready"], 2, 1), 23: (S["yzT_ready"], 2, 2),
            24: (S["x2_ready"], 1, 1), 25: (S["v_ready"], 1, 1),
            26: (S["gelu_ready"], 4, 1), 27: (S["gelu_ready"], 4, 2), 28: (S["gelu_ready"], 4, 3), 29: (S["gelu_ready"], 4, 4),
            30: (S["x3_ready"], 1, 1), 31: (S["w_ready"], 1, 1), 32: (S["logit_ready"], 1, 1), 33: (S["combT_lo"], 1, 1),
        }

        bt = lambda b: slice(b * P, (b + 1) * P)
        slot = lambda k: ring[k % 3]
        tok4 = lambda t: t[:, :].rearrange("p (b d) -> p b d", b=B)
        heads = lambda t: t.rearrange("p b (h q) -> p b h q", h=NH)
        over_q = lambda t: t.unsqueeze(3).to_broadcast([t.shape[0], t.shape[1], NH, HD])

        def wait_before(eng, *waits):
            waits = [(sem, value if isinstance(value, int) else eng.to_reg(value)) for sem, value in waits]
            eng.wait_ge(S["vector_ready"], 1)
            for sem, value in waits:
                eng.wait_ge(sem, value)

        def x_tile(t, n):
            return t[:, bass.ds(n * P, P), :].rearrange("b t d -> t b d")

        @block.sync
        def _(sp):
            loads = [
                (cT[:, :], d["cT"]), (wmod, d["wmod"]), (ln1w[:, :], d["ln1_w"]), (ln1b[:, :], d["ln1_b"]),
                (wp, d["in_projT"][:, 0:ZX]), (wdt[:, :], d["in_projT"][:, ZX:DP]), (convw[:, :, :], d["conv_w"]), (convb[:, :], d["conv_b"]),
                (dtb[:, :], d["dt_bias"].unsqueeze(0).to_broadcast([P, NH])),
                (A_row[:, :], d["A_log"].unsqueeze(0).to_broadcast([P, NH])),
                (Dcol[:, :], d["D_col"]), (normw[:, :], d["norm_w"]),
                (wout[:, :, :], d["out_projT"].rearrange("(j p) n -> p j n", p=P)),
                (ln2w[:, :], d["ln2_w"]), (ln2b[:, :], d["ln2_b"]), (w1m, d["mlp_w1T"]), (b1m[:, :], d["mlp_b1"]),
                (w2m[:, :, :], d["mlp_w2T"].rearrange("(q p) n -> p q n", p=P)),
                (b2row[:, :], d["mlp_b2"].unsqueeze(0).to_broadcast([P, D])),
                (wg[:, :], d["gateT"]), (wexp[:, :], d["moe_w1T"]), (b1e[:, :, :], d["moe_b1"]),
                (wo[:, :, :], d["moe_woT"].rearrange("(k p) n -> p k n", p=P)),
                (borow[:, :], d["moe_bo"].unsqueeze(0).to_broadcast([P, D])),
            ]
            assert len(loads) == N_LOADS
            for dst, src in loads:
                sp.dma_start(dst, src).then_inc(S["loads"], 16)

            def load(n):
                sp.wait_ge(S["x4_ready"], n)
                sp.dma_start(xt[:, :, :], x_tile(d["x"], n)).then_inc(S["x_loaded"], 16)

            def store(n):
                sp.wait_ge(S["o_ready"], n + 1)
                sp.dma_start(x_tile(out, n), ot[:, :, :]).then_inc(S["stored"], 16)

            load(0)
            load(1)
            store(0)
            with sp.Fori(1, NT - 1) as i:
                load(i + 1)
                store(i)
            store(NT - 1)
            sp.wait_ge(S["stored"], 16 * NT)

        @block.tensor
        def _(pe):
            def split3(o, ahi, alo, bhi, blo, start=True):
                pe.matmul(o, ahi, bhi, start=start, stop=False, skip_group_check=True)
                pe.matmul(o, ahi, blo, start=False, stop=False, skip_group_check=True)
                return pe.matmul(o, alo, bhi, start=False, stop=True, skip_group_check=True)

            def ring_free(k, n):
                before, tile = k - 3, n
                if before < 0:
                    before, tile = before + TURN, n - 1
                    if isinstance(n, int) and n == 0:
                        return
                    if before == R_OUT:
                        pe.wait_ge(S["o_bias"], tile)
                        return
                    if before == 34:
                        before = R_N4T
                sem, per, at = readers[before]
                pe.wait_ge(sem, per * tile + at)

            def setup():
                pe.wait_ge(S["silu_rows_ready"], 1)
                for b in range(B):
                    for part, (c0, cols) in enumerate(((0, 3 * D), (5 * D, D))):
                        k = 2 * b + part
                        if k >= 3:
                            pe.wait_ge(S["mod_read"], k - 2)
                        pe.matmul(slot(k)[:, 0:cols], silu_row[:, b, :], wmod[:, c0:c0 + cols],
                                  start=True, stop=True).then_inc(S["mod_ps"], 1)
                pe.wait_ge(S["mod_read"], 2 * B - 2)
                for j in range(2):
                    m = pe.matmul(slot(2 * B)[:, j * B:(j + 1) * B], wmod[:, (3 + j) * D:(4 + j) * D], silu_c[:, :],
                                  start=(j == 0), stop=True, skip_group_check=True)
                m.then_inc(S["mod_ps"], 1)
                pe.wait_ge(S["mod_read"], 2 * B + 1)
                pe.wait_ge(S["gpsimd_ready"], 1)
                pe.wait_ge(S["scalar_ready"], 1)
                pe.wait_ge(S["vector_ready"], 1)

            def transposes(k, src):
                for b in range(B):
                    m = pe.transpose(slot(k)[:, bt(b)], src[:, b, :], ident[:, :])
                return m

            def front(n, s):
                if s == 1:
                    ring_free(R_N1T, n)
                    pe.wait_ge(S["n1_ready"], n + 1)
                    transposes(R_N1T, nrm).then_inc(S["n1T_ps"], 1)
                if s == 2:
                    ring_free(R_DT, n)
                    pe.wait_ge(S["u_ready"], n + 1)
                    for b in range(B):
                        m = pe.matmul(slot(R_DT)[:, b * NH:(b + 1) * NH], u[:, bt(b)], wdt[:, :],
                                      start=(b == 0), stop=True, skip_group_check=True)
                    m.then_inc(S["dt_ps"], 1)
                    pe.wait_ge(S["ulo_ready"], n + 1)
                    for j in range(CB):
                        ring_free(R_XBC + j, n)
                        cols = slice(DI + j * P, DI + (j + 1) * P)
                        split3(slot(R_XBC + j)[:, :], wp_hi[:, cols], wp_lo[:, cols], u_hi[:, :], u_lo[:, :])\
                            .then_inc(S["xbc_ps"], 1)
                if s == 3:
                    for pair in range(2):
                        ring_free(R_Z + pair, n)
                        for q in range(2):
                            m = split3(slot(R_Z + pair)[:, q * DI:(q + 1) * DI], u_hi[:, bt(2 * pair + q)],
                                       u_lo[:, bt(2 * pair + q)], wp_hi[:, 0:DI], wp_lo[:, 0:DI], start=(q == 0))
                        m.then_inc(S["z_ps"], 1)
                if s == 5:
                    pe.wait_ge(S["xs_silu"], n + 1)
                    for pair in range(2):
                        ring_free(R_XTM + pair, n)
                        for q in range(2):
                            for j in range(DI // P):
                                m = pe.transpose(slot(R_XTM + pair)[:, q * DI + j * P:q * DI + (j + 1) * P],
                                                 xs[:, j, bt(2 * pair + q)], ident[:, :])
                        m.then_inc(S["xtm_ps"], 1)
                    sem, per, at = readers[R_BTM - 3]
                    wait_before(pe, (S["bc_silu"], n + 1), (sem, per * n + at))
                    for b in range(B):
                        m = pe.transpose(slot(R_BTM)[:, b * NS:(b + 1) * NS], Bc[:, bt(b)], ident[0:NS, 0:NS])
                    m.then_inc(S["btm_ps"], 1)
                    pe.wait_ge(S["a_ready"], n + 1)
                    ring_free(R_CUM, n)
                    av = a[:, :, :].rearrange("p b h -> p (b h)")
                    for k, mask in enumerate((upto, after, ones)):
                        m = pe.matmul(slot(R_CUM)[:, k * B * NH:(k + 1) * B * NH], mask[:, :], av, start=(k == 0),
                                      stop=True, skip_group_check=True)
                    m.then_inc(S["cum_ps"], 1)
                if s == 6:
                    ring_free(R_G, n)
                    for b in range(B):
                        m = pe.matmul(slot(R_G)[:, bt(b)], Bc[:, bt(b)], Cc[:, bt(b)], start=(b == 0), stop=True,
                                      skip_group_check=True)
                    m.then_inc(S["g_ps"], 1)
                if s in (6, 8):
                    pair = (s - 6) // 2
                    for q in range(2):
                        b = 2 * pair + q
                        ring_free(R_PAIR[pair] + q, n)
                        pe.wait_ge(S["m1a_ready"], 4 * n + b + 1)
                        pe.matmul(slot(R_PAIR[pair] + q)[:, :], after[:, :],
                                  m1a[:, q, :, :].rearrange("p h t -> p (h t)"), start=True, stop=True).then_inc(S["seg_ps"], 1)
                if s in (7, 9):
                    pair = (s - 7) // 2
                    inter, intra = slot(R_PAIR[pair] + 2), slot(R_PAIR[pair] + 3)
                    ring_free(R_PAIR[pair] + 2, n)
                    pe.wait_ge(S["H_ready"], 2 * n)
                    for q in range(2):
                        b = 2 * pair + q
                        m = pe.matmul(inter[:, q * DI:(q + 1) * DI], Cc[:, bt(b)], H[:, b, :], start=(q == 0), stop=True,
                                      skip_group_check=True)
                    m.then_inc(S["int_ps"], 1)
                    ring_free(R_PAIR[pair] + 3, n)
                    for q in range(2):
                        b = 2 * pair + q
                        for j in range(DI // P):
                            pe.matmul(intra[:, q * DI + j * P:q * DI + (j + 1) * P], xs[:, j, bt(b)], Ddiag[:, j, :],
                                      start=(q == 0 and j == 0), stop=False, skip_group_check=True)
                        pe.wait_ge(S["W_ready"], 4 * n + b + 1)
                        pe.wait_ge(S["xdt_ready"], 2 * n + pair + 1)
                        for hh in range(NH):
                            m = pe.matmul(intra[:, q * DI + hh * HD:q * DI + (hh + 1) * HD], Wt[:, q, hh, :],
                                          xdt[:, b, hh * HD:(hh + 1) * HD], start=False, stop=True,
                                          skip_group_check=True)
                    m.then_inc(S["yi_ps"], 1)
                if s == 10:
                    pe.wait_ge(S["btm_ready"], n + 1)
                    for pair in range(2):
                        ring_free(R_ST + pair, n)
                        pe.wait_ge(S["xde_ready"], 2 * n + pair + 1)
                        for q in range(2):
                            b = 2 * pair + q
                            m = pe.matmul(slot(R_ST + pair)[0:NS, q * DI:(q + 1) * DI], Btm[:, b, :], xde[:, b, :],
                                          start=(q == 0), stop=True, skip_group_check=True)
                        m.then_inc(S["st_ps"], 1)
                    pe.wait_ge(S["yz_ready"], 2 * n + 2)
                    for j in range(DI // P):
                        ring_free(R_YZT + j, n)
                        for b in range(B):
                            m = pe.transpose(slot(R_YZT + j)[:, bt(b)], yz[:, b, j * P:(j + 1) * P], ident[:, :])
                        m.then_inc(S["yzT_ps"], 1)
                if s == 11:
                    ring_free(R_OP, n)
                    pe.wait_ge(S["yzT_ready"], 2 * n + 2)
                    for b in range(B):
                        for j in range(DI // P):
                            m = pe.matmul(slot(R_OP)[:, bt(b)], yzT[:, j, bt(b)], wout[:, j, :],
                                          start=(b == 0 and j == 0), stop=(j == 1), skip_group_check=True)
                    m.then_inc(S["op_ps"], 1)
                if s == 12:
                    ring_free(R_N2T, n)
                    pe.wait_ge(S["n2_ready"], n + 1)
                    transposes(R_N2T, nrm).then_inc(S["n2T_ps"], 1)
                if s == 13:
                    pe.wait_ge(S["vhi_ready"], n + 1)
                    pe.wait_ge(S["vlo_ready"], n + 1)
                    for q in range(MQ):
                        ring_free(R_HID + q, n)
                        cols = slice(q * P, (q + 1) * P)
                        split3(slot(R_HID + q)[:, :], w1m_hi[:, cols], w1m_lo[:, cols], v_hi[:, :], v_lo[:, :])\
                            .then_inc(S["hid_ps"], 1)
                    ring_free(R_MLP, n)
                    pe.wait_ge(S["gelu_ready"], 4 * n + 4)
                    for b in range(B):
                        for q in range(MQ):
                            m = pe.matmul(slot(R_MLP)[:, bt(b)], gl[:, q, bt(b)], w2m[:, q, :],
                                          start=(b == 0 and q == 0), stop=(q == MQ - 1), skip_group_check=True)
                    m.then_inc(S["mlp_ps"], 1)
                if s == 14:
                    ring_free(R_N4T, n)
                    pe.wait_ge(S["n4_ready"], n + 1)
                    transposes(R_N4T, nrm).then_inc(S["n4T_ps"], 1)
                if s == 15:
                    ring_free(R_LOGIT, n)
                    pe.wait_ge(S["w_ready"], n + 1)
                    for b in range(B):
                        m = pe.matmul(slot(R_LOGIT)[:, b * E:(b + 1) * E], w[:, bt(b)], wg[:, :], start=(b == 0), stop=True,
                                      skip_group_check=True)
                    m.then_inc(S["logit_ps"], 1)
                    ring_free(R_COMBT, n)
                    pe.wait_ge(S["comb_ready"], n + 1)
                    for b in range(B):
                        m = pe.transpose(slot(R_COMBT)[0:E, bt(b)], comb[:, b, :], ident[:, :])
                    m.then_inc(S["combT_ps"], 1)

            def expert_unit(n, un):
                e, k = divmod(un, HK)
                if un == 0:
                    pe.wait_ge(S["whi_ready"], n + 1)
                    pe.wait_ge(S["wlo_ready"], n + 1)
                pe.wait_ge(S["tanh_ready"], NU * n + max(un - 1, 0))
                pe.wait_ge(S["aw_ready"], NU * n + max(un - 1, 0))
                for half in range(2):
                    c0 = e * 2 * H2 + half * H2 + k * P
                    m = split3(ab[2 * (un % 2) + half][:, :], wexp_hi[:, c0:c0 + P], wexp_lo[:, c0:c0 + P],
                               w_hi[:, :], w_lo[:, :])
                m.then_inc(S["ab_ps"], 1)
                if k == 0:
                    if e == 0:
                        pe.wait_ge(S["combT_hi"], n + 1)
                        pe.wait_ge(S["combT_lo"], n + 1)
                    pe.wait_ge(S["combB_ready"], E * n + e)
                    pe.matmul(cbps[:, :], pick_r[:, e, :], combT[:, :], start=True, stop=True).then_inc(S["combB_ps"], 1)

            def expert_out(n, last):
                pe.wait_ge(S["acc_added"], (NU - HK) * n + NU - HK)
                if last:
                    pe.wait_ge(S["o_bias"], n)
                else:
                    pe.wait_ge(S["logit_ready"], n + 2)
                for b in range(B):
                    for k in range(HK):
                        m = pe.matmul(slot(R_OUT)[:, bt(b)], acc[:, k, bt(b)], wo[:, k, :], start=(b == 0 and k == 0),
                                      stop=(k == 1), skip_group_check=True)
                m.then_inc(S["wo_ps"], 1)

            def between(i):
                for s in range(NU):
                    expert_unit(i, s)
                    front(i + 1, s)
                expert_out(i, False)

            setup()
            for s in range(NU):
                front(0, s)
            between(0)
            with pe.Fori(1, NT - 1) as i:
                between(i)
            for un in range(NU):
                expert_unit(NT - 1, un)
            expert_out(NT - 1, True)

        @block.scalar
        def _(act):
            f = act.activation

            def setup():
                act.wait_ge(S["loads"], 16 * N_LOADS)
                f(silu_c[:, :], cT[:, :], ACT.Silu).then_inc(S["silu_c_ready"], 1)
                f(wp_hi[:, :], wp[:, 0:ZX], ACT.Copy).then_inc(S["split_hi"], 1)
                f(w1m_hi[:, :], w1m[:, :], ACT.Copy).then_inc(S["split_hi"], 1)
                f(wexp_hi[:, :], wexp[:, :], ACT.Copy).then_inc(S["split_hi"], 1)
                f(A_neg[:, :], A_row[:, :], ACT.Exp).then_inc(S["A_exp"], 1)
                act.wait_ge(S["split_hi"], 3)
                f(b1e_half[:, :, :], b1e[:, :, :], ACT.Copy, scale=0.5).then_inc(S["scalar_ready"], 1)
                act.wait_ge(S["scalar_ready"], 1)
                act.wait_ge(S["gpsimd_ready"], 1)
                act.wait_ge(S["vector_ready"], 1)

            def front(n, s):
                if s == 1:
                    act.wait_ge(S["n1T_ps"], n + 1)
                    act.wait_ge(S["vlo_ready"], n)
                    f(u[:, :], slot(R_N1T)[:, :], ACT.Identity, bias=ln1b[:, 0:1], scale=ln1w[:, 0:1]).then_inc(S["u_ready"], 1)
                    act.wait_ge(S["u_ready"], n + 1)
                    act.wait_ge(S["hid_ps"], 4 * n)
                    f(u_hi[:, :], u[:, :], ACT.Copy).then_inc(S["uhi_ready"], 1)
                if s == 2:
                    act.wait_ge(S["halo_saved"], n)
                    for j in range(CB):
                        act.wait_ge(S["xbc_ps"], CB * n + j + 1)
                        src = slot(R_XBC + j)[:, :].rearrange("p (b t) -> p b t", b=B)
                        f(xbc[:, j, :, HALO:HALO + P], src, ACT.Copy)
                        f(cv[:, j, :, :], src, ACT.Identity, bias=convb[:, j:j + 1], scale=convw[:, j, HALO:HALO + 1])\
                            .then_inc(S["xbc_read"], 1)
                if s == 4:
                    act.wait_ge(S["yz_ready"], 2 * n)
                    for pair in range(2):
                        act.wait_ge(S["z_ps"], 2 * n + pair + 1)
                        f(sz[:, 2 * pair:2 * pair + 2, :], slot(R_Z + pair)[:, :].rearrange("p (b c) -> p b c", b=2),
                          ACT.Silu).then_inc(S["z_silu"], 1)
                    act.wait_ge(S["yi_ps"], 2 * n)
                    for j in range(CB - 1):
                        act.wait_ge(S["conv_tap"], CB * HALO * n + HALO * (j + 1))
                        m = f(xs[:, j, :].rearrange("p (b t) -> p b t", b=B), cv[:, j, :, :], ACT.Silu)
                    m.then_inc(S["xs_silu"], 1)
                    act.wait_ge(S["conv_tap"], CB * HALO * (n + 1))
                    f(tok4(Bc), cv[0:NS, CB - 1, :, :], ACT.Silu)
                    f(tok4(Cc), cv[NS:2 * NS, CB - 1, :, :], ACT.Silu).then_inc(S["bc_silu"], 1)
                    act.wait_ge(S["dt_chain"], DT_STEPS * n + 2)
                    f(ew[:, :, :], nab[:, :, :], ACT.Exp).then_inc(S["dt_exp"], 1)
                if s == 5:
                    act.wait_ge(S["btm_ps"], n + 1)
                    act.wait_ge(S["st_ps"], 2 * n)
                    f(Btm[:, :, :], slot(R_BTM)[:, 0:B * NS].rearrange("p (b s) -> p b s", b=B), ACT.Copy)\
                        .then_inc(S["btm_ready"], 1)
                    act.wait_ge(S["cum_ps"], n + 1)
                    act.wait_ge(S["yt_ready"], 2 * n)
                    act.wait_ge(S["xde_ready"], 2 * n)
                    act.wait_ge(S["Hd_ready"], 2 * n)
                    f(ecs[:, :, :, :].rearrange("p k b h -> p (k b h)"), slot(R_CUM)[:, 0:3 * B * NH], ACT.Exp)\
                        .then_inc(S["ecs_ready"], 1)
                if s in (6, 8):
                    pair = (s - 6) // 2
                    for q in range(2):
                        b = 2 * pair + q
                        act.wait_ge(S["seg_ps"], 4 * n + b + 1)
                        act.wait_ge(S["W_ready"], 4 * n + max(b - 1, 0))
                        f(L[:, q, :, :].rearrange("p h t -> p (h t)"), slot(R_PAIR[pair] + q)[:, :], ACT.Exp)\
                            .then_inc(S["L_ready"], 1)
                if s == 10:
                    act.wait_ge(S["yz_ready"], 2 * n + 2)
                    for b in range(B):
                        m = f(yt[:, b, :], yz[:, b, :], ACT.Square, accum_out=ssq[:, b:b + 1])
                    m.then_inc(S["ssq_ready"], 1)
                    act.wait_ge(S["op_ps"], n)
                    for j in range(DI // P):
                        act.wait_ge(S["yzT_ps"], 2 * n + j + 1)
                        f(yzT[:, j, :], slot(R_YZT + j)[:, :], ACT.Copy).then_inc(S["yzT_ready"], 1)
                if s == 12:
                    act.wait_ge(S["n2T_ps"], n + 1)
                    act.wait_ge(S["ulo_ready"], n + 1)
                    act.wait_ge(S["dt_ps"], n + 1)
                    f(v[:, :], slot(R_N2T)[:, :], ACT.Identity, bias=ln2b[:, 0:1], scale=ln2w[:, 0:1]).then_inc(S["v_ready"], 1)
                    act.wait_ge(S["v_ready"], n + 1)
                    act.wait_ge(S["z_ps"], 2 * n + 2)
                    f(v_hi[:, :], v[:, :], ACT.Copy).then_inc(S["vhi_ready"], 1)
                if s == 13:
                    act.wait_ge(S["mlp_ps"], n)
                    for q in range(MQ):
                        act.wait_ge(S["hid_ps"], 4 * n + q + 1)
                        f(gl[:, q, :], slot(R_HID + q)[:, :], ACT.Gelu, bias=b1m[:, q:q + 1]).then_inc(S["gelu_ready"], 1)
                if s == 15:
                    act.wait_ge(S["n4T_ps"], n + 1)
                    act.wait_ge(S["wlo_ready"], n)
                    act.wait_ge(S["logit_ps"], n)
                    for b in range(B):
                        m = f(w[:, bt(b)], slot(R_N4T)[:, bt(b)], ACT.Identity, bias=sbT[:, b:b + 1], scale=cb1T[:, b:b + 1])
                    m.then_inc(S["w_ready"], 1)
                    act.wait_ge(S["w_ready"], n + 1)
                    act.wait_ge(S["ab_ps"], NU * n)
                    f(w_hi[:, :], w[:, :], ACT.Copy).then_inc(S["whi_ready"], 1)
                    act.wait_ge(S["gate_chain"], GATE_STEPS * n + GATE_EXP)
                    f(ex[:, :, :], exs[:, :, :], ACT.Exp).then_inc(S["ex_ready"], 1)
                    act.wait_ge(S["combT_ps"], n + 1)
                    act.wait_ge(S["combB_ps"], E * n)
                    f(combT[0:E, :], slot(R_COMBT)[0:E, :], ACT.Copy).then_inc(S["combT_hi"], 1)

            def expert_unit(n, un):
                e, k = divmod(un, HK)
                if un == 0:
                    act.wait_ge(S["x4_ready"], n + 1)
                    act.wait_ge(S["comb_ready"], n + 1)
                    act.wait_ge(S["o_ready"], n)
                    act.wait_ge(S["o_bias"], n)
                    f(x4k[:, :, :], x4[:, :, :], ACT.Copy)
                    f(csumk[:, :], csum[:, :], ACT.Copy).then_inc(S["kept"], 1)
                if k == 0:
                    act.wait_ge(S["combB_ps"], E * n + e + 1)
                    act.wait_ge(S["aw_ready"], NU * n + HK * max(e - 1, 0))
                    f(combB[:, e % 2, :], cbps[:, :], ACT.Copy).then_inc(S["combB_ready"], 1)
                act.wait_ge(S["ab_ps"], NU * n + un + 1)
                act.wait_ge(S["g_ready"], NU * n + max(un - 1, 0))
                f(tg[:, un % 2, :], ab[2 * (un % 2) + 1][:, :], ACT.Tanh, bias=b1e_half[:, e, HK + k:HK + k + 1], scale=0.5)\
                    .then_inc(S["tanh_ready"], 1)

            def between(i):
                for s in range(NU):
                    expert_unit(i, s)
                    front(i + 1, s)

            setup()
            for s in range(NU):
                front(0, s)
            between(0)
            with act.Fori(1, NT - 1) as i:
                between(i)
            for un in range(NU):
                expert_unit(NT - 1, un)

        @block.vector
        def _(dve):
            tt, ts, stt = dve.tensor_tensor, dve.tensor_scalar, dve.scalar_tensor_tensor

            def setup():
                dve.memset(xbc[:, :, :, 0:HALO], 0.0)
                dve.memset(H[:, :, :], 0.0)
                dve.memset(top[:, :, :], PAD)
                dve.memset(lg[:, :, :], PAD)
                dve.memset(minus_half[:, :], -0.5)
                dve.wait_ge(S["silu_c_ready"], 1)
                dve.tensor_copy(silu_row[:, :, :], bcast(silu_c[:, :], 2, [P, B, P])).then_inc(S["silu_rows_ready"], 1)
                dve.wait_ge(S["gpsimd_ready"], 1)
                dve.tensor_copy(pick_r[:, :, :], pick[:, :, :])
                ts(combT[:, :], wexp[0:64, 0:W4], 0.0, None, ALU.mult)
                for j in range(DI // P):
                    ts(Ddiag[:, j, :], ident[:, :], Dcol[:, j:j + 1], None, ALU.mult)
                    ts(wout[:, j, :], wout[:, j, :], normw[:, j:j + 1], None, ALU.mult)
                for b in range(B):
                    dve.wait_ge(S["mod_ps"], 2 * b + 1)
                    dve.tensor_copy(sa[:, b, :], slot(2 * b)[:, 0:D])
                    ts(ca1[:, b, :], slot(2 * b)[:, D:2 * D], 1.0, None, ALU.add)
                    dve.tensor_copy(ga[:, b, :], slot(2 * b)[:, 2 * D:3 * D]).then_inc(S["mod_read"], 1)
                    dve.wait_ge(S["mod_ps"], 2 * b + 2)
                    dve.tensor_copy(gb[:, b, :], slot(2 * b + 1)[:, 0:D]).then_inc(S["mod_read"], 1)
                dve.wait_ge(S["mod_ps"], 2 * B + 1)
                dve.tensor_copy(sbT[:, :], slot(2 * B)[:, 0:B])
                ts(cb1T[:, :], slot(2 * B)[:, B:2 * B], 1.0, None, ALU.add).then_inc(S["mod_read"], 1)
                dve.wait_ge(S["split_hi"], 3)
                tt(wp_lo[:, :], wp[:, 0:ZX], wp_hi[:, :].bitcast(F32), ALU.subtract)
                tt(w1m_lo[:, :], w1m[:, :], w1m_hi[:, :].bitcast(F32), ALU.subtract)
                tt(wexp_lo[:, :], wexp[:, :], wexp_hi[:, :].bitcast(F32), ALU.subtract)
                steps = 0
                for g in (ga, gb):
                    dve.wait_ge(S["mod_read"], 2 * B + 1)
                    if steps:
                        dve.wait_ge(S["setup_chain"], steps)
                    ts(gsign[:, :, :], g[:, :, :], 0.0, 2.0, ALU.is_ge, ALU.mult).then_inc(S["setup_chain"], 1)
                    dve.wait_ge(S["setup_chain"], steps + 1)
                    stt(g[:, :, :], g[:, :, :], -1.0, g[:, :, :], ALU.mult, ALU.max).then_inc(S["setup_chain"], 1)
                    ts(gsign[:, :, :], gsign[:, :, :], -1.0, None, ALU.add).then_inc(S["setup_chain"], 1)
                    dve.wait_ge(S["setup_chain"], steps + 3)
                    stt(g[:, :, :], g[:, :, :], 0.25, gsign[:, :, :], ALU.max, ALU.mult).then_inc(S["setup_chain"], 1)
                    steps += 4
                dve.wait_ge(S["setup_chain"], steps)
                dve.wait_ge(S["A_exp"], 1)
                ts(A_neg[:, :], A_neg[:, :], -1.0, None, ALU.mult).then_inc(S["vector_ready"], 1)
                dve.wait_ge(S["vector_ready"], 1)
                dve.wait_ge(S["scalar_ready"], 1)

            def ln_stats(src, which, mv, n, stats_done, mv_done):
                for b in range(B):
                    m = dve.bn_stats(stats[:, which, b, :], src[:, b, :])
                m.then_inc(stats_done, 1)
                wait_before(dve, (stats_done, n + 1))
                for b in range(B):
                    m = dve.bn_aggr(mv[:, b, :], stats[:, which, b, :])
                m.then_inc(mv_done, 1)

            def ln_norm(src, mv, r):
                for b in range(B):
                    m = ts(nrm[:, b, :], src[:, b, :], mv[:, b, 0:1], r[:, b:b + 1], ALU.subtract, ALU.mult)
                return m

            def softplus_and_a(n):
                base = DT_STEPS * n
                dve.wait_ge(S["dt_exp"], n + 1)
                ts(den[:, :, :], ew[:, :, :], 2.0, None, ALU.add).then_inc(S["dt_chain"], 1)
                dve.wait_ge(S["dt_chain"], base + 3)
                dve.reciprocal(rden[:, :, :], den[:, :, :]).then_inc(S["dt_chain"], 1)
                dve.wait_ge(S["dt_chain"], base + 4)
                tt(sw[:, :, :], ew[:, :, :], rden[:, :, :], ALU.mult).then_inc(S["dt_chain"], 1)
                dve.wait_ge(S["dt_chain"], base + 5)
                tt(s2[:, :, :], sw[:, :, :], sw[:, :, :], ALU.mult).then_inc(S["dt_chain"], 1)
                dve.wait_ge(S["dt_chain"], base + 6)
                ts(pl[:, :, :], s2[:, :, :], 2.0 / ATANH[0], None, ALU.mult).then_inc(S["dt_chain"], 1)
                at = base + 7
                for c in ATANH[1:]:
                    dve.wait_ge(S["dt_chain"], at)
                    stt(pl[:, :, :], pl[:, :, :], 2.0 / c, s2[:, :, :], ALU.add, ALU.mult).then_inc(S["dt_chain"], 1)
                    at = at + 1
                dve.wait_ge(S["dt_chain"], at)
                stt(pl[:, :, :], pl[:, :, :], 2.0, sw[:, :, :], ALU.add, ALU.mult).then_inc(S["dt_chain"], 1)
                dve.wait_ge(S["dt_chain"], at + 1)
                dve.wait_ge(S["xdt_ready"], 2 * n)
                tt(dt[:, :, :], pl[:, :, :], relu[:, :, :], ALU.add).then_inc(S["dt_chain"], 1)
                dve.wait_ge(S["dt_chain"], at + 2)
                dve.wait_ge(S["m1a_ready"], 4 * n)
                dve.wait_ge(S["cum_ps"], n)
                tt(a[:, :, :], dt[:, :, :], bcast(A_neg[:, :], 1, [P, B, NH]), ALU.mult).then_inc(S["a_ready"], 1)

            def gate(n):
                base = GATE_STEPS * n
                wait_before(dve, (S["logit_ready"], n + 1))
                for b in range(B):
                    m = dve.max(mx[:, b, :], lg[:, b, 0:E])
                m.then_inc(S["gate_chain"], 1)
                dve.wait_ge(S["gate_chain"], base + 1)
                dve.tensor_copy(top[:, :, 0:2], mx[:, :, 0:2]).then_inc(S["gate_chain"], 1)
                tt(exs[:, :, :], lg[:, :, 0:E], mx[:, :, 0:1].to_broadcast([P, B, E]), ALU.subtract).then_inc(S["gate_chain"], 1)
                wait_before(dve, (S["gate_chain"], base + 3))
                for b in range(B):
                    m = dve.match_replace(rep[:, b, :], top[:, b, :], lg[:, b, :], TAKEN)
                m.then_inc(S["gate_chain"], 1)
                dve.wait_ge(S["ex_ready"], n + 1)
                dve.tensor_reduce(Z[:, :], ex[:, :, :], AX.X, ALU.add).then_inc(S["gate_chain"], 1)
                dve.wait_ge(S["gate_chain"], base + 5)
                stt(sel[:, :, :], rep[:, :, 0:E], TAKEN / 2, ex[:, :, :], ALU.is_gt, ALU.mult).then_inc(S["gate_chain"], 1)
                dve.wait_ge(S["gate_chain"], base + 6)
                dve.tensor_reduce(dsum[:, :], sel[:, :, :], AX.X, ALU.add).then_inc(S["gate_chain"], 1)
                dve.wait_ge(S["gate_chain"], base + 7)
                stt(deps[:, :], Z[:, :], TOPK_EPS, dsum[:, :], ALU.mult, ALU.add).then_inc(S["gate_chain"], 1)
                dve.wait_ge(S["gate_chain"], base + 8)
                dve.reciprocal(rinv[:, :], deps[:, :]).then_inc(S["gate_chain"], 1)
                dve.wait_ge(S["gate_chain"], base + 9)
                dve.wait_ge(S["kept"], n)
                dve.wait_ge(S["combT_ps"], n)
                tt(csum[:, :], dsum[:, :], rinv[:, :], ALU.mult)
                stt(comb[:, :, :], sel[:, :, :], 0.5, bcast(rinv[:, :], 2, [P, B, E]), ALU.mult, ALU.mult)\
                    .then_inc(S["comb_ready"], 1)

            def front(n, s):
                if s == 0:
                    dve.wait_ge(S["x_loaded"], 16 * (n + 1))
                    ln_stats(xt, 0, mva, n, S["xa_stats"], S["xa_mv"])
                if s == 1:
                    dve.wait_ge(S["h_ready"], n + 1)
                    ln_stats(h, 1, mvh, n, S["h_stats"], S["h_mv"])
                    dve.wait_ge(S["h_rstd"], n + 1)
                    dve.wait_ge(S["n4T_ps"], n)
                    ln_norm(h, mvh, rh).then_inc(S["n1_ready"], 1)
                if s == 2:
                    dve.wait_ge(S["uhi_ready"], n + 1)
                    dve.wait_ge(S["hid_ps"], 4 * n)
                    tt(u_lo[:, :], u[:, :], u_hi[:, :].bitcast(F32), ALU.subtract).then_inc(S["ulo_ready"], 1)
                    dve.wait_ge(S["dt_ps"], n + 1)
                    tt(dtv[:, :, :], slot(R_DT)[:, 0:B * NH].rearrange("p (b h) -> p b h", b=B),
                       bcast(dtb[:, :], 1, [P, B, NH]), ALU.add).then_inc(S["dt_chain"], 1)
                    dve.wait_ge(S["dt_chain"], DT_STEPS * n + 1)
                    ts(relu[:, :, :], dtv[:, :, :], 0.0, None, ALU.max)
                    stt(nab[:, :, :], dtv[:, :, :], -1.0, dtv[:, :, :], ALU.mult, ALU.min).then_inc(S["dt_chain"], 1)
                if s == 3:
                    for j in range(CB):
                        dve.wait_ge(S["xbc_read"], CB * n + j + 1)
                        for k in range(HALO):
                            if k > 0:
                                dve.wait_ge(S["conv_tap"], CB * HALO * n + HALO * j + k)
                            stt(cv[:, j, :, :], xbc[:, j, :, k:k + P], convw[:, j, k:k + 1], cv[:, j, :, :],
                                ALU.mult, ALU.add).then_inc(S["conv_tap"], 1)
                if s == 4:
                    softplus_and_a(n)
                if s == 5:
                    dve.wait_ge(S["yi_ps"], 2 * n)
                    dve.wait_ge(S["xde_ready"], 2 * n)
                    dve.wait_ge(S["dt_chain"], DT_STEPS * (n + 1))
                    for pair in range(2):
                        bb = slice(2 * pair, 2 * pair + 2)
                        dve.wait_ge(S["xtm_ps"], 2 * n + pair + 1)
                        tt(heads(xdt[:, bb, :]), heads(slot(R_XTM + pair)[:, :].rearrange("p (b c) -> p b c", b=2)),
                           over_q(dt[:, bb, :]), ALU.mult).then_inc(S["xdt_ready"], 1)
                if s == 6:
                    dve.wait_ge(S["g_ps"], n + 1)
                    tt(gm[:, :, :], tok4(slot(R_G)), bcast(upto[:, :], 1, [P, B, P]), ALU.mult).then_inc(S["gm_ready"], 1)
                    dve.wait_ge(S["gm_ready"], n + 1)
                if s in (6, 8):
                    pair = (s - 6) // 2
                    dve.wait_ge(S["yi_ps"], 2 * n + pair)
                    for q in range(2):
                        b = 2 * pair + q
                        dve.wait_ge(S["L_ready"], 4 * n + b + 1)
                        tt(Wt[:, q, :, :], L[:, q, :, :], bcast(gm[:, b, :], 1, [P, NH, P]), ALU.mult).then_inc(S["W_ready"], 1)
                if s in (7, 9):
                    pair = (s - 7) // 2
                    bb = slice(2 * pair, 2 * pair + 2)
                    dve.wait_ge(S["int_ps"], 2 * n + pair + 1)
                    dve.wait_ge(S["ecs_ready"], n + 1)
                    dve.wait_ge(S["ssq_ready"], n)
                    tt(heads(yt[:, bb, :]), heads(slot(R_PAIR[pair] + 2)[:, :].rearrange("p (b c) -> p b c", b=2)),
                       over_q(ecs[:, 0, bb, :]), ALU.mult).then_inc(S["yt_ready"], 1)
                    dve.wait_ge(S["yt_ready"], 2 * n + pair + 1)
                    dve.wait_ge(S["yi_ps"], 2 * n + pair + 1)
                    tt(yt[:, bb, :], slot(R_PAIR[pair] + 3)[:, :].rearrange("p (b c) -> p b c", b=2), yt[:, bb, :], ALU.add)\
                        .then_inc(S["y_ready"], 1)
                    dve.wait_ge(S["y_ready"], 2 * n + pair + 1)
                    dve.wait_ge(S["z_silu"], 2 * n + pair + 1)
                    dve.wait_ge(S["yzT_ps"], 2 * n)
                    tt(yz[:, bb, :], yt[:, bb, :], sz[:, bb, :], ALU.mult).then_inc(S["yz_ready"], 1)
                if s == 10:
                    for pair in range(2):
                        bb = slice(2 * pair, 2 * pair + 2)
                        dve.wait_ge(S["st_ps"], 2 * n + pair + 1)
                        dve.wait_ge(S["Hd_ready"], 2 * n + pair + 1)
                        tt(H[:, bb, :], slot(R_ST + pair)[0:NS, :].rearrange("p (b c) -> p b c", b=2), Hd[:, bb, :], ALU.add)\
                            .then_inc(S["H_ready"], 1)
                if s == 11:
                    dve.wait_ge(S["op_ps"], n + 1)
                    dve.wait_ge(S["y_rstd"], n + 1)
                    dve.wait_ge(S["x2b_ready"], n)
                    for b in range(B):
                        m = stt(x2[:, b, :], slot(R_OP)[:, bt(b)], ry[:, b:b + 1], h[:, b, :], ALU.mult, ALU.add)
                    m.then_inc(S["x2_ready"], 1)
                    dve.wait_ge(S["x2_ready"], n + 1)
                    ln_stats(x2, 2, mv2, n, S["x2_stats"], S["x2_mv"])
                    dve.wait_ge(S["x2_rstd"], n + 1)
                    dve.wait_ge(S["n1T_ps"], n + 1)
                    ln_norm(x2, mv2, r2).then_inc(S["n2_ready"], 1)
                if s == 12:
                    dve.wait_ge(S["vhi_ready"], n + 1)
                    dve.wait_ge(S["z_ps"], 2 * n + 2)
                    tt(v_lo[:, :], v[:, :], v_hi[:, :].bitcast(F32), ALU.subtract).then_inc(S["vlo_ready"], 1)
                if s == 13:
                    dve.wait_ge(S["mlp_ps"], n + 1)
                    dve.wait_ge(S["x2b_ready"], n + 1)
                    dve.wait_ge(S["x3_scaled"], n)
                    tt(x3[:, :, :], tok4(slot(R_MLP)), x2b[:, :, :], ALU.add).then_inc(S["x3_ready"], 1)
                if s == 14:
                    dve.wait_ge(S["x4_ready"], n + 1)
                    ln_stats(x4, 3, mv4, n, S["x4_stats"], S["x4_mv"])
                    dve.wait_ge(S["x4_rstd"], n + 1)
                    dve.wait_ge(S["n2T_ps"], n + 1)
                    ln_norm(x4, mv4, r4).then_inc(S["n4_ready"], 1)
                if s == 15:
                    dve.wait_ge(S["whi_ready"], n + 1)
                    dve.wait_ge(S["ab_ps"], NU * n)
                    tt(w_lo[:, :], w[:, :], w_hi[:, :].bitcast(F32), ALU.subtract).then_inc(S["wlo_ready"], 1)
                    dve.wait_ge(S["logit_ps"], n + 1)
                    dve.tensor_copy(lg[:, :, 0:E], slot(R_LOGIT)[:, 0:B * E].rearrange("p (b e) -> p b e", b=B))\
                        .then_inc(S["logit_ready"], 1)
                    gate(n)
                    dve.wait_ge(S["combT_hi"], n + 1)
                    dve.wait_ge(S["combB_ps"], E * n)
                    tt(combT[32:32 + E, :], slot(R_COMBT)[0:E, :], combT[0:E, :].bitcast(F32), ALU.subtract)\
                        .then_inc(S["combT_lo"], 1)

            def expert_unit(n, un):
                e, k = divmod(un, HK)
                added = (NU - HK) * n
                dve.wait_ge(S["ab_ps"], NU * n + un + 1)
                dve.wait_ge(S["combB_ready"], E * n + e + 1)
                stt(aw[:, un % 2, :], ab[2 * (un % 2)][:, :], b1e[:, e, k:k + 1], combB[:, e % 2, :], ALU.add, ALU.mult)\
                    .then_inc(S["aw_ready"], 1)
                dve.wait_ge(S["aw_ready"], NU * n + un + 1)
                dve.wait_ge(S["tanh_ready"], NU * n + un + 1)
                if e == 0:
                    dve.wait_ge(S["wo_ps"], n)
                    dst = acc[:, k, :]
                else:
                    dve.wait_ge(S["acc_added"], added + max(un - 5, 0))
                    dst = gg[:, un % 4, :]
                stt(dst, tg[:, un % 2, :], 1.0, aw[:, un % 2, :], ALU.add, ALU.mult).then_inc(S["g_ready"], 1)

            def expert_out(n):
                dve.wait_ge(S["wo_ps"], n + 1)
                dve.wait_ge(S["kept"], n + 1)
                dve.wait_ge(S["o_scaled"], n)
                for b in range(B):
                    m = stt(o1[:, b, :], borow[:, :], csumk[:, b:b + 1], slot(R_OUT)[:, bt(b)], ALU.mult, ALU.add)
                m.then_inc(S["o_bias"], 1)

            def between(i):
                for s in range(NU):
                    expert_unit(i, s)
                    front(i + 1, s)
                expert_out(i)

            setup()
            for s in range(NU):
                front(0, s)
            between(0)
            with dve.Fori(1, NT - 1) as i:
                between(i)
            for un in range(NU):
                expert_unit(NT - 1, un)
            expert_out(NT - 1)

        @block.gpsimd
        def _(pool):
            tt, ts = pool.tensor_tensor, pool.tensor_scalar

            def setup():
                pool.memset(ones[:, :], 1.0).then_inc(S["masks_filled"], 1)
                pool.memset(ident[:, :], 0.0).then_inc(S["masks_filled"], 1)
                pool.memset(pick[:, :, :], 0.0).then_inc(S["masks_filled"], 1)
                pool.wait_ge(S["masks_filled"], 3)
                pool.affine_select(out=ident[:, :], in_=ident[:, :], pattern=[[-1, P]], compare_op=ALU.not_equal, fill=1.0,
                                   base=0, channel_multiplier=1)
                pool.affine_select(out=upto[:, :], in_=ones[:, :], pattern=[[1, P]], compare_op=ALU.is_ge, fill=0.0,
                                   base=0, channel_multiplier=-1)
                pool.affine_select(out=after[:, :], in_=ones[:, :], pattern=[[-1, P]], compare_op=ALU.is_gt, fill=0.0,
                                   base=0, channel_multiplier=1)
                pool.affine_select(out=pick[:, :, :], in_=pick[:, :, :], pattern=[[-1, E], [0, P]],
                                   compare_op=ALU.not_equal, fill=1.0, base=0, channel_multiplier=1).then_inc(S["masks_made"], 1)
                pool.wait_ge(S["masks_made"], 1)
                pool.affine_select(out=pick[:, :, :], in_=pick[:, :, :], pattern=[[-1, E], [0, P]],
                                   compare_op=ALU.not_equal, fill=1.0, base=-32, channel_multiplier=1)\
                    .then_inc(S["gpsimd_ready"], 1)
                pool.wait_ge(S["gpsimd_ready"], 1)
                pool.wait_ge(S["vector_ready"], 1)

            def rstd(dst, which, var, scale, eps, var_done, rstd_done, n):
                ts(var_e[:, which, :], var, scale, eps, ALU.mult, ALU.add).then_inc(var_done, 1)
                pool.wait_ge(var_done, n + 1)
                tt(dst[:, :], var_e[:, which, :], minus_half[:, :], ALU.pow).then_inc(rstd_done, 1)

            def front(n, s):
                if s == 0:
                    wait_before(pool, (S["xa_mv"], n + 1))
                    rstd(ra, 0, mva[:, :, 1], 1.0, LN_EPS, S["xa_var"], S["xa_rstd"], n)
                    wait_before(pool, (S["xa_rstd"], n + 1))
                    for b in range(B):
                        m = ts(na[:, b, :], xt[:, b, :], mva[:, b, 0:1], ra[:, b:b + 1], ALU.subtract, ALU.mult)
                    m.then_inc(S["xa_norm"], 1)
                    pool.wait_ge(S["xa_norm"], n + 1)
                    tt(na[:, :, :], na[:, :, :], ca1[:, :, :], ALU.mult).then_inc(S["xa_scaled"], 1)
                    pool.wait_ge(S["xa_scaled"], n + 1)
                    pool.wait_ge(S["x2_ready"], n)
                    tt(h[:, :, :], na[:, :, :], sa[:, :, :], ALU.add).then_inc(S["h_ready"], 1)
                if s == 1:
                    wait_before(pool, (S["h_mv"], n + 1))
                    rstd(rh, 1, mvh[:, :, 1], 1.0, LN_EPS, S["h_var"], S["h_rstd"], n)
                if s == 4:
                    wait_before(pool, (S["conv_tap"], CB * HALO * (n + 1)))
                    pool.tensor_copy(xbc[:, :, :, 0:HALO], xbc[:, :, :, P:P + HALO]).then_inc(S["halo_saved"], 1)
                if s in (5, 7):
                    pair = (s - 5) // 2
                    pool.wait_ge(S["a_ready"], n + 1)
                    for q in range(2):
                        b = 2 * pair + q
                        pool.wait_ge(S["seg_ps"], 4 * n + max(b - 1, 0))
                        tt(m1a[:, q, :, :], bcast(upto[:, :], 1, [P, NH, P]), bcast(a[:, b, :], 2, [P, NH, P]), ALU.mult)\
                            .then_inc(S["m1a_ready"], 1)
                if s == 8:
                    pool.wait_ge(S["ecs_ready"], n + 1)
                    pool.wait_ge(S["xdt_ready"], 2 * n + 2)
                    pool.wait_ge(S["st_ps"], 2 * n)
                    for pair in range(2):
                        bb = slice(2 * pair, 2 * pair + 2)
                        tt(heads(xde[:, bb, :]), heads(xdt[:, bb, :]), over_q(ecs[:, 1, bb, :]), ALU.mult)\
                            .then_inc(S["xde_ready"], 1)
                if s == 9:
                    pool.wait_ge(S["H_ready"], 2 * n)
                    for pair in range(2):
                        bb = slice(2 * pair, 2 * pair + 2)
                        tt(heads(Hd[:, bb, :]), heads(H[:, bb, :]), over_q(ecs[0:NS, 2, bb, :]), ALU.mult)\
                            .then_inc(S["Hd_ready"], 1)
                if s == 10:
                    wait_before(pool, (S["ssq_ready"], n + 1))
                    rstd(ry, 4, ssq[:, :], 1.0 / DI, LN_EPS, S["y_var"], S["y_rstd"], n)
                if s == 11:
                    wait_before(pool, (S["x2_mv"], n + 1))
                    rstd(r2, 2, mv2[:, :, 1], 1.0, LN_EPS, S["x2_var"], S["x2_rstd"], n)
                    pool.wait_ge(S["x3_ready"], n)
                    tt(x2b[:, :, :], x2[:, :, :], bcast(b2row[:, :], 1, [P, B, D]), ALU.add).then_inc(S["x2b_ready"], 1)
                if s == 13:
                    pool.wait_ge(S["x3_ready"], n + 1)
                    tt(x3[:, :, :], x3[:, :, :], ga[:, :, :], ALU.mult).then_inc(S["x3_scaled"], 1)
                    pool.wait_ge(S["x3_scaled"], n + 1)
                    pool.wait_ge(S["kept"], n)
                    pool.wait_ge(S["n4_ready"], n)
                    tt(x4[:, :, :], x3[:, :, :], xt[:, :, :], ALU.add).then_inc(S["x4_ready"], 1)
                if s == 14:
                    wait_before(pool, (S["x4_mv"], n + 1))
                    rstd(r4, 3, mv4[:, :, 1], 1.0, LN_EPS, S["x4_var"], S["x4_rstd"], n)

            def expert_unit(n, un):
                e, k = divmod(un, HK)
                if e == 0:
                    return
                pool.wait_ge(S["g_ready"], NU * n + un + 1)
                pool.wait_ge(S["acc_added"], (NU - HK) * n + max(un - 3, 0))
                tt(acc[:, k, :], acc[:, k, :], gg[:, un % 4, :], ALU.add).then_inc(S["acc_added"], 1)

            def expert_out(n):
                pool.wait_ge(S["o_bias"], n + 1)
                tt(o2[:, :, :], o1[:, :, :], gb[:, :, :], ALU.mult).then_inc(S["o_scaled"], 1)
                pool.wait_ge(S["o_scaled"], n + 1)
                pool.wait_ge(S["kept"], n + 1)
                pool.wait_ge(S["stored"], 16 * n)
                tt(ot[:, :, :], o2[:, :, :], x4k[:, :, :], ALU.add).then_inc(S["o_ready"], 1)

            def between(i):
                for s in range(NU):
                    expert_unit(i, s)
                    front(i + 1, s)
                expert_out(i)

            setup()
            for s in range(NU):
                front(0, s)
            between(0)
            with pool.Fori(1, NT - 1) as i:
                between(i)
            for un in range(NU):
                expert_unit(NT - 1, un)
            expert_out(NT - 1)


def kernel(**inputs):
    import numpy as np
    import concourse.bacc as bacc
    from concourse.bass_utils import run_bass_kernel_spmd

    def per_partition(v, rows=1):
        return np.moveaxis(v.reshape(v.shape[:-1] + (rows, P)), -1, 0)

    L = {k: np.asarray(v) for k, v in inputs.items()}
    n_heads = L["L0_attn_D"].shape[0]
    inner = L["L0_attn_norm_w"].shape[0]
    arrays = {
        "x": L["L0_attn_x"], "ln1_w": per_partition(L["L0_attn_ln1_w"]), "ln1_b": per_partition(L["L0_attn_ln1_b"]),
        "ln2_w": per_partition(L["L0_attn_ln2_w"]), "ln2_b": per_partition(L["L0_attn_ln2_b"]),
        "in_projT": L["L0_attn_in_proj_w"].T,
        "conv_w": np.moveaxis(L["L0_attn_conv_w"].reshape(-1, P, 4), 0, 1),
        "conv_b": per_partition(L["L0_attn_conv_b"], 3),
        "dt_bias": L["L0_attn_dt_bias"], "A_log": L["L0_attn_A_log"],
        "D_col": per_partition(np.repeat(L["L0_attn_D"], inner // n_heads), inner // P),
        "norm_w": per_partition(L["L0_attn_norm_w"], inner // P), "out_projT": L["L0_attn_out_proj_w"].T,
        "mlp_w1T": L["L0_attn_mlp_w1"].T, "mlp_b1": per_partition(L["L0_attn_mlp_b1"], 4),
        "mlp_w2T": L["L0_attn_mlp_w2"].T, "mlp_b2": L["L0_attn_mlp_b2"], "gateT": L["L0_ffn_Wg"].T,
        "moe_w1T": np.moveaxis(L["L0_ffn_W1"], 2, 0).reshape(P, -1), "moe_b1": per_partition(L["L0_ffn_b1"], 4),
        "moe_woT": L["L0_ffn_Wo"].T, "moe_bo": L["L0_ffn_bo"], "cT": L["L0_c"].T, "wmod": L["L0_wmod"],
    }
    arrays = {k: np.ascontiguousarray(v) for k, v in arrays.items()}
    nc = bacc.Bacc("TRN2", target_bir_lowering=False, num_devices=1)
    d = {k: nc.dram_tensor("in_" + k, v.shape, mybir.dt.from_np(v.dtype), kind="ExternalInput").ap() for k, v in arrays.items()}
    out = nc.dram_tensor("out", arrays["x"].shape, F32, kind="ExternalOutput").ap()
    build(nc, d, out)
    r = run_bass_kernel_spmd(nc, [{"in_" + k: v for k, v in arrays.items()}], core_ids=[0])
    return r.results[0]["out"]
```

```python
from contextlib import ExitStack

import concourse.bass as bass
from concourse import mybir

F32 = mybir.dt.float32
F32R = mybir.dt.float32r
ALU = mybir.AluOpType
ACT = mybir.ActivationFunctionType
AX = mybir.AxisListType

P = 128
LN_EPS = 1e-5
TOPK_EPS = 1e-9
PAD = -3.0e38
TAKEN = 3.0e38
ATANH = (13, 11, 9, 7, 5, 3)
DT_STEPS = 8 + len(ATANH)
GATE_STEPS = 9
GATE_EXP = 3

EVENTS = """
x_loaded xa_stats xa_mv xa_var xa_rstd xa_norm xa_scaled h_ready xr_loaded h_kept
h_stats h_mv h_var h_rstd n1_ready n1T_ps u_ready uhi_ready ulo_ready
dt_ps dt_chain dt_exp a_ready xbc_ps xbc_read conv_tap halo_saved z_ps z_silu xs_silu bc_silu
xtm_ps xdt_ready btm_ps btm_ready cum_ps ecs_ready g_ps gm_ready
m1a_ready seg_ps L_ready W_ready int_ps yt_ready yi_ps yi_read yz_ready
ssq_ready y_var y_rstd xde_ready st_ps Hd_ready H_ready
yzT_ps yzT_ready op_ps x2_ready
x2_stats x2_mv x2_var x2_rstd n2_ready n2T_ps v_ready vhi_ready vlo_ready x2b_ready
hid_ps gelu_ready mlp_ps x3_ready x3_scaled x4_ready
x4_stats x4_mv x4_var x4_rstd n4_ready n4T_ps w_ready whi_ready wlo_ready
logit_ps logit_ready gate_chain ex_ready comb_ready combT_ps combT_hi combT_lo
kept combB_ps combB_ready ab_ps tanh_ready aw_ready g_ready acc_added
wo_ps o_bias o_scaled o_ready stored
""".split()
SETUP = "loads silu_c_ready silu_rows_ready mod_ps mod_read masks_filled masks_made split_hi vector_ready scalar_ready gpsimd_ready A_exp setup_chain".split()
N_LOADS = 24


def bcast(ap, where, shape):
    return ap.unsqueeze(where).to_broadcast(shape)


def build(nc, d, out):
    B, T, D = d["x"].shape
    NT = T // P
    E = d["moe_b1"].shape[1]
    DI = d["out_projT"].shape[0]
    NH = d["A_log"].shape[0]
    HD = DI // NH
    NS = (d["conv_w"].shape[1] * P - DI) // 2
    MH = d["mlp_w1T"].shape[1]
    MQ = MH // P
    H2 = d["moe_woT"].shape[0]
    HK = H2 // P
    CB = d["conv_w"].shape[1]
    TAPS = d["conv_w"].shape[2]
    HALO = TAPS - 1
    NU = E * HK
    DP = d["in_projT"].shape[1]
    ZX = DP - NH
    W4 = B * P
    assert D == P and B == 4 and NH == 4 and E == 8 and CB == 3 and HK == 2

    with ExitStack() as ctx:
        def sb(name, shape, dt=F32):
            return ctx.enter_context(nc.sbuf_tensor(name, shape, dt))

        wdt = sb("wdt", [P, NH]); wp_hi = sb("wp_hi", [P, ZX], F32R); wp_lo = sb("wp_lo", [P, ZX], F32R)
        w1m_hi = sb("w1m_hi", [P, MH], F32R); w1m_lo = sb("w1m_lo", [P, MH], F32R)
        w2m = sb("w2m", [P, MQ, D])
        wexp_hi = sb("wexp_hi", [P, E * 2 * H2], F32R); wexp_lo = sb("wexp_lo", [P, E * 2 * H2], F32R)
        wo = sb("wo", [P, HK, D]); wout = sb("wout", [P, DI // P, D]); wg = sb("wg", [P, E])
        ln1w = sb("ln1w", [P, 1]); ln1b = sb("ln1b", [P, 1]); ln2w = sb("ln2w", [P, 1]); ln2b = sb("ln2b", [P, 1])
        convw = sb("convw", [P, CB, TAPS]); convb = sb("convb", [P, CB])
        dtb = sb("dtb", [P, NH]); A_row = sb("A_row", [P, NH]); A_neg = sb("A_neg", [P, NH])
        Dcol = sb("Dcol", [P, DI // P]); Ddiag = sb("Ddiag", [P, DI // P, P])
        normw = sb("normw", [P, DI // P]); b1m = sb("b1m", [P, MQ]); b2row = sb("b2row", [P, D])
        b1e = sb("b1e", [P, E, 2 * HK]); b1e_half = sb("b1e_half", [P, E, 2 * HK]); borow = sb("borow", [P, D])
        cT = sb("cT", [P, B]); silu_c = sb("silu_c", [P, B])
        ones = sb("ones", [P, P]); ident = sb("ident", [P, P])
        upto = sb("upto", [P, P])
        after = sb("after", [P, P])
        pick_r = sb("pick_r", [64, E, P], F32R)
        minus_half = sb("minus_half", [P, B])
        sa = sb("sa", [P, B, D]); ca1 = sb("ca1", [P, B, D]); ga = sb("ga", [P, B, D]); gb = sb("gb", [P, B, D])
        sbT = sb("sbT", [P, B]); cb1T = sb("cb1T", [P, B])

        xt = sb("xt", [P, B, D]); xr = sb("xr", [P, B, D]); stats = sb("stats", [P, 4, B, 6])
        mva = sb("mva", [P, B, 2]); mvh = sb("mvh", [P, B, 2]); mv2 = sb("mv2", [P, B, 2]); mv4 = sb("mv4", [P, B, 2])
        var_e = sb("var_e", [P, 5, B]); ra = sb("ra", [P, B]); rh = sb("rh", [P, B]); r2 = sb("r2", [P, B]); r4 = sb("r4", [P, B])
        h = sb("h", [P, B, D]); hk = sb("hk", [P, B, D]); nrm = sb("nrm", [P, B, D]); nrm4 = sb("nrm4", [P, B, D])
        u = sb("u", [P, W4]); u_hi = sb("u_hi", [P, W4], F32R); u_lo = sb("u_lo", [P, W4], F32R)
        dtv = sb("dtv", [P, B, NH]); nab = sb("nab", [P, B, NH]); ew = sb("ew", [P, B, NH]); den = sb("den", [P, B, NH])
        rden = sb("rden", [P, B, NH]); sw = sb("sw", [P, B, NH]); s2 = sb("s2", [P, B, NH]); pl = sb("pl", [P, B, NH])
        relu = sb("relu", [P, B, NH]); dt = sb("dt", [P, B, NH]); a = sb("a", [P, B, NH])
        xbc = sb("xbc", [P, CB, B, HALO + P]); cv = sb("cv", [P, CB, B, P])
        xs = sb("xs", [P, DI // P, W4]); Bc = sb("Bc", [NS, W4]); Cc = sb("Cc", [NS, W4])
        sz = sb("sz", [P, B, DI]); xdt = sb("xdt", [P, B, DI]); xde = sb("xde", [P, B, DI]); Btm = sb("Btm", [P, B, NS])
        ecs = sb("ecs", [P, 3, B, NH])
        gm = sb("gm", [P, B, P]); m1a = sb("m1a", [P, 2, NH, P]); L = sb("L", [P, 2, NH, P]); Wt = sb("Wt", [P, 2, NH, P])
        yt = sb("yt", [P, B, DI]); yz = sb("yz", [P, B, DI])
        ssq = sb("ssq", [P, B]); ry = sb("ry", [P, B])
        H = sb("H", [NS, B, DI]); Hd = sb("Hd", [NS, B, DI])
        yzT = sb("yzT", [P, DI // P, W4]); x2 = sb("x2", [P, B, D]); x2b = sb("x2b", [P, B, D]); x3 = x2b
        v = sb("v", [P, W4]); v_hi = sb("v_hi", [P, W4], F32R); v_lo = sb("v_lo", [P, W4], F32R)
        gl = sb("gl", [P, MQ, W4]); x4 = sb("x4", [P, B, D])
        w = sb("w", [P, W4]); w_hi = sb("w_hi", [P, W4], F32R); w_lo = sb("w_lo", [P, W4], F32R)
        NP_ = E + 6
        lg = sb("lg", [P, B, NP_]); mx = sb("mx", [P, B, 8]); top = sb("top", [P, B, 8]); rep = sb("rep", [P, B, NP_])
        exs = sb("exs", [P, B, E]); ex = sb("ex", [P, B, E]); Z = sb("Z", [P, B]); sel = sb("sel", [P, B, E])
        dsum = sb("dsum", [P, B]); deps = sb("deps", [P, B]); rinv = sb("rinv", [P, B]); csum = sb("csum", [P, B])
        comb = sb("comb", [P, B, E]); combT = sb("combT", [64, W4], F32R)
        csumk = sb("csumk", [P, B]); combB = sb("combB", [P, 2, W4])
        aw = sb("aw", [P, 2, W4]); acc = sb("acc", [P, HK, W4])
        late = sb("late", [P, 8 * W4])
        gg = late[:, 0:4 * W4].rearrange("p (q w) -> p q w", q=4)
        tg = late[:, 4 * W4:6 * W4].rearrange("p (q w) -> p q w", q=2)
        x4k, o = (late[:, (6 + q) * W4:(7 + q) * W4].rearrange("p (b d) -> p b d", b=B) for q in range(2))
        wexp = late
        raw = gl[:, :, :].rearrange("p q w -> p (q w)")
        wp, w1m = raw[:, 0:ZX], raw[:, ZX:ZX + MH]
        wmod = xde[:, :, :].rearrange("p b c -> p (b c)")[:, 0:6 * D]
        silu_row, gsign = yz[:, 0:2, :].rearrange("p b (c d) -> p (b c) d", d=D), x2
        pick = combB[0:64, :, :].rearrange("p a (e w) -> p (a e) w", w=P)

        ring = [ctx.enter_context(nc.psum_tensor(f"ring{i}", [P, W4], F32)) for i in range(3)]
        ab = [ctx.enter_context(nc.psum_tensor(f"ab{i}", [P, W4], F32)) for i in range(4)]
        cbps = ctx.enter_context(nc.psum_tensor("cbps", [P, W4], F32))
        S = {e: ctx.enter_context(nc.semaphore(e)) for e in SETUP + EVENTS}
        block = ctx.enter_context(nc.Block())

        uses = {
            "xtm0": (2, "xdt_ready", 2, 1), "xtm1": (2, "xdt_ready", 2, 2), "btm": (2, "btm_ready", 1, 1),
            "cum": (2, "ecs_ready", 1, 1), "g": (2, "gm_ready", 1, 1),
            "n2T": (1, "v_ready", 1, 1), "seg0": (2, "L_ready", 4, 1), "seg1": (2, "L_ready", 4, 2),
            "int0": (2, "yt_ready", 2, 1), "n1T": (3, "u_ready", 1, 1), "intra0": (2, "yi_read", 2, 1),
            "seg2": (2, "L_ready", 4, 3), "seg3": (2, "L_ready", 4, 4),
            "dt": (3, "dt_chain", DT_STEPS, 1), "int1": (2, "yt_ready", 2, 2),
            "xbc0": (3, "xbc_read", CB, 1), "xbc1": (3, "xbc_read", CB, 2), "xbc2": (3, "xbc_read", CB, 3),
            "intra1": (2, "yi_read", 2, 2),
            "hid0": (1, "gelu_ready", 4, 1), "hid1": (1, "gelu_ready", 4, 2), "hid2": (1, "gelu_ready", 4, 3),
            "hid3": (1, "gelu_ready", 4, 4), "st0": (2, "H_ready", 2, 1), "st1": (2, "H_ready", 2, 2),
            "mlp": (1, "x3_ready", 1, 1), "yzT0": (2, "yzT_ready", 2, 1), "yzT1": (2, "yzT_ready", 2, 2),
            "op": (2, "x2_ready", 1, 1), "z0": (3, "z_silu", 2, 1), "z1": (3, "z_silu", 2, 2),
            "n4T": (1, "w_ready", 1, 1), "logit": (1, "logit_ready", 1, 1), "combT": (1, "combT_lo", 1, 1),
            "out": (0, "o_bias", 1, 1), "spare": None,
        }
        order = list(uses)
        assert len(order) % 3 == 0
        slot = lambda name: ring[order.index(name) % 3]

        def ring_reader(name, n):
            t, at, first = n - uses[name][0], order.index(name), isinstance(n, int)
            while True:
                at -= 3
                if at < 0:
                    at, t = at + len(order), t - 1
                if uses[order[at]] is None:
                    continue
                ahead, sem, per, count = uses[order[at]]
                if not first or 0 <= t + ahead < NT:
                    return S[sem], per * (t + ahead) + count
                if t < -4:
                    return None

        bt = lambda b: slice(b * P, (b + 1) * P)
        tok4 = lambda t: t[:, :].rearrange("p (b d) -> p b d", b=B)
        heads = lambda t: t.rearrange("p b (h q) -> p b h q", h=NH)
        over_q = lambda t: t.unsqueeze(3).to_broadcast([t.shape[0], t.shape[1], NH, HD])

        def wait_before(eng, *waits):
            waits = [(sem, value if isinstance(value, int) else eng.to_reg(value)) for sem, value in waits]
            eng.wait_ge(S["vector_ready"], 1)
            for sem, value in waits:
                eng.wait_ge(sem, value)

        def x_tile(t, n):
            return t[:, bass.ds(n * P, P), :].rearrange("b t d -> t b d")

        def run_bodies(eng, body):
            def live(t):
                return "".join(c for c, ahead in zip("ECMA", range(4)) if 0 <= t + ahead < NT)
            for t in range(-3, 1):
                body(t, live(t))
            with eng.Fori(1, NT - 4) as t:
                body(t, "ECMA")
            for t in range(NT - 4, NT):
                body(t, live(t))

        @block.sync
        def _(sp):
            loads = [
                (cT[:, :], d["cT"]), (wmod, d["wmod"]), (ln1w[:, :], d["ln1_w"]), (ln1b[:, :], d["ln1_b"]),
                (wp, d["in_projT"][:, 0:ZX]), (wdt[:, :], d["in_projT"][:, ZX:DP]), (convw[:, :, :], d["conv_w"]), (convb[:, :], d["conv_b"]),
                (dtb[:, :], d["dt_bias"].unsqueeze(0).to_broadcast([P, NH])),
                (A_row[:, :], d["A_log"].unsqueeze(0).to_broadcast([P, NH])),
                (Dcol[:, :], d["D_col"]), (normw[:, :], d["norm_w"]),
                (wout[:, :, :], d["out_projT"].rearrange("(j p) n -> p j n", p=P)),
                (ln2w[:, :], d["ln2_w"]), (ln2b[:, :], d["ln2_b"]), (w1m, d["mlp_w1T"]), (b1m[:, :], d["mlp_b1"]),
                (w2m[:, :, :], d["mlp_w2T"].rearrange("(q p) n -> p q n", p=P)),
                (b2row[:, :], d["mlp_b2"].unsqueeze(0).to_broadcast([P, D])),
                (wg[:, :], d["gateT"]), (wexp[:, :], d["moe_w1T"]), (b1e[:, :, :], d["moe_b1"]),
                (wo[:, :, :], d["moe_woT"].rearrange("(k p) n -> p k n", p=P)),
                (borow[:, :], d["moe_bo"].unsqueeze(0).to_broadcast([P, D])),
            ]
            assert len(loads) == N_LOADS
            for dst, src in loads:
                sp.dma_start(dst, src).then_inc(S["loads"], 16)

            def load_x(n):
                sp.wait_ge(S["xa_norm"], n)
                sp.dma_start(xt[:, :, :], x_tile(d["x"], n)).then_inc(S["x_loaded"], 16)

            def load_residual(n):
                sp.wait_ge(S["x4_ready"], n)
                sp.dma_start(xr[:, :, :], x_tile(d["x"], n)).then_inc(S["xr_loaded"], 16)

            def store(n):
                sp.wait_ge(S["o_ready"], n + 1)
                sp.dma_start(x_tile(out, n), o[:, :, :]).then_inc(S["stored"], 16)

            def body(t, live):
                if "C" in live:
                    load_residual(t + 1)
                if "A" in live:
                    if not isinstance(t, int) or t + 4 < NT:
                        load_x(t + 4)
                if "E" in live:
                    store(t)

            load_x(0)
            run_bodies(sp, body)
            sp.wait_ge(S["stored"], 16 * NT)

        @block.tensor
        def _(pe):
            def split3(o, ahi, alo, bhi, blo, start=True):
                pe.matmul(o, ahi, bhi, start=start, stop=False, skip_group_check=True)
                pe.matmul(o, ahi, blo, start=False, stop=False, skip_group_check=True)
                return pe.matmul(o, alo, bhi, start=False, stop=True, skip_group_check=True)

            def ring_free(name, n):
                reader = ring_reader(name, n)
                if reader is not None:
                    pe.wait_ge(*reader)

            def setup():
                pe.wait_ge(S["silu_rows_ready"], 1)
                for b in range(B):
                    for part, (c0, cols) in enumerate(((0, 3 * D), (5 * D, D))):
                        k = 2 * b + part
                        if k >= 3:
                            pe.wait_ge(S["mod_read"], k - 2)
                        pe.matmul(ring[k % 3][:, 0:cols], silu_row[:, b, :], wmod[:, c0:c0 + cols],
                                  start=True, stop=True).then_inc(S["mod_ps"], 1)
                pe.wait_ge(S["mod_read"], 2 * B - 2)
                for j in range(2):
                    m = pe.matmul(ring[2 * B % 3][:, j * B:(j + 1) * B], wmod[:, (3 + j) * D:(4 + j) * D], silu_c[:, :],
                                  start=(j == 0), stop=True, skip_group_check=True)
                m.then_inc(S["mod_ps"], 1)
                pe.wait_ge(S["mod_read"], 2 * B + 1)
                pe.wait_ge(S["gpsimd_ready"], 1)
                pe.wait_ge(S["scalar_ready"], 1)
                pe.wait_ge(S["vector_ready"], 1)

            def transposes(name, src):
                for b in range(B):
                    m = pe.transpose(slot(name)[:, bt(b)], src[:, b, :], ident[:, :])
                return m

            def stage_C(n, s):
                if s == 2:
                    ring_free("n2T", n)
                    pe.wait_ge(S["n2_ready"], n + 1)
                    transposes("n2T", x2).then_inc(S["n2T_ps"], 1)
                if s == 8:
                    pe.wait_ge(S["vhi_ready"], n + 1)
                    pe.wait_ge(S["vlo_ready"], n + 1)
                if s in (8, 9):
                    for q in (0, 1) if s == 8 else (2, 3):
                        ring_free(f"hid{q}", n)
                        cols = slice(q * P, (q + 1) * P)
                        split3(slot(f"hid{q}")[:, :], w1m_hi[:, cols], w1m_lo[:, cols], v_hi[:, :], v_lo[:, :])\
                            .then_inc(S["hid_ps"], 1)
                if s == 10:
                    ring_free("mlp", n)
                    pe.wait_ge(S["gelu_ready"], 4 * n + 4)
                    for b in range(B):
                        for q in range(MQ):
                            m = pe.matmul(slot("mlp")[:, bt(b)], gl[:, q, bt(b)], w2m[:, q, :],
                                          start=(b == 0 and q == 0), stop=(q == MQ - 1), skip_group_check=True)
                    m.then_inc(S["mlp_ps"], 1)
                if s == 13:
                    ring_free("n4T", n)
                    pe.wait_ge(S["n4_ready"], n + 1)
                    transposes("n4T", nrm4).then_inc(S["n4T_ps"], 1)
                if s == 14:
                    ring_free("logit", n)
                    pe.wait_ge(S["w_ready"], n + 1)
                    for b in range(B):
                        m = pe.matmul(slot("logit")[:, b * E:(b + 1) * E], w[:, bt(b)], wg[:, :], start=(b == 0), stop=True,
                                      skip_group_check=True)
                    m.then_inc(S["logit_ps"], 1)
                if s == 16:
                    ring_free("combT", n)
                    pe.wait_ge(S["comb_ready"], n + 1)
                    for b in range(B):
                        m = pe.transpose(slot("combT")[0:E, bt(b)], comb[:, b, :], ident[:, :])
                    m.then_inc(S["combT_ps"], 1)

            def stage_M(n, s):
                if s == 0:
                    pe.wait_ge(S["xs_silu"], n + 1)
                    for pair in range(2):
                        ring_free(f"xtm{pair}", n)
                        for q in range(2):
                            for j in range(DI // P):
                                m = pe.transpose(slot(f"xtm{pair}")[:, q * DI + j * P:q * DI + (j + 1) * P],
                                                 xs[:, j, bt(2 * pair + q)], ident[:, :])
                        m.then_inc(S["xtm_ps"], 1)
                    reader = ring_reader("btm", n)
                    wait_before(pe, (S["bc_silu"], n + 1), *([reader] if reader else []))
                    for b in range(B):
                        m = pe.transpose(slot("btm")[:, b * NS:(b + 1) * NS], Bc[:, bt(b)], ident[0:NS, 0:NS])
                    m.then_inc(S["btm_ps"], 1)
                    pe.wait_ge(S["a_ready"], n + 1)
                    ring_free("cum", n)
                    av = a[:, :, :].rearrange("p b h -> p (b h)")
                    for k, mask in enumerate((upto, after, ones)):
                        m = pe.matmul(slot("cum")[:, k * B * NH:(k + 1) * B * NH], mask[:, :], av, start=(k == 0),
                                      stop=True, skip_group_check=True)
                    m.then_inc(S["cum_ps"], 1)
                if s == 1:
                    ring_free("g", n)
                    for b in range(B):
                        m = pe.matmul(slot("g")[:, bt(b)], Bc[:, bt(b)], Cc[:, bt(b)], start=(b == 0), stop=True,
                                      skip_group_check=True)
                    m.then_inc(S["g_ps"], 1)
                if s in (2, 5):
                    pair = s // 3
                    for q in range(2):
                        b = 2 * pair + q
                        ring_free(f"seg{b}", n)
                        pe.wait_ge(S["m1a_ready"], 4 * n + b + 1)
                        pe.matmul(slot(f"seg{b}")[:, :], after[:, :],
                                  m1a[:, q, :, :].rearrange("p h t -> p (h t)"), start=True, stop=True).then_inc(S["seg_ps"], 1)
                if s in (3, 6):
                    pair = s // 4
                    inter = slot(f"int{pair}")
                    ring_free(f"int{pair}", n)
                    pe.wait_ge(S["H_ready"], 2 * n)
                    for q in range(2):
                        b = 2 * pair + q
                        m = pe.matmul(inter[:, q * DI:(q + 1) * DI], Cc[:, bt(b)], H[:, b, :], start=(q == 0), stop=True,
                                      skip_group_check=True)
                    m.then_inc(S["int_ps"], 1)
                if s in (4, 7):
                    pair = s // 5
                    intra = slot(f"intra{pair}")
                    ring_free(f"intra{pair}", n)
                    for q in range(2):
                        b = 2 * pair + q
                        for j in range(DI // P):
                            pe.matmul(intra[:, q * DI + j * P:q * DI + (j + 1) * P], xs[:, j, bt(b)], Ddiag[:, j, :],
                                      start=(q == 0 and j == 0), stop=False, skip_group_check=True)
                        pe.wait_ge(S["W_ready"], 4 * n + b + 1)
                        pe.wait_ge(S["xdt_ready"], 2 * n + pair + 1)
                        for hh in range(NH):
                            m = pe.matmul(intra[:, q * DI + hh * HD:q * DI + (hh + 1) * HD], Wt[:, q, hh, :],
                                          xdt[:, b, hh * HD:(hh + 1) * HD], start=False, stop=True,
                                          skip_group_check=True)
                    m.then_inc(S["yi_ps"], 1)
                if s == 9:
                    pe.wait_ge(S["btm_ready"], n + 1)
                    for pair in range(2):
                        ring_free(f"st{pair}", n)
                        pe.wait_ge(S["xde_ready"], 2 * n + pair + 1)
                        for q in range(2):
                            b = 2 * pair + q
                            m = pe.matmul(slot(f"st{pair}")[0:NS, q * DI:(q + 1) * DI], Btm[:, b, :], xde[:, b, :],
                                          start=(q == 0), stop=True, skip_group_check=True)
                        m.then_inc(S["st_ps"], 1)
                if s == 10:
                    pe.wait_ge(S["yz_ready"], 2 * n + 2)
                    for j in range(DI // P):
                        ring_free(f"yzT{j}", n)
                        for b in range(B):
                            m = pe.transpose(slot(f"yzT{j}")[:, bt(b)], yz[:, b, j * P:(j + 1) * P], ident[:, :])
                        m.then_inc(S["yzT_ps"], 1)
                if s == 11:
                    ring_free("op", n)
                    pe.wait_ge(S["yzT_ready"], 2 * n + 2)
                    for b in range(B):
                        for j in range(DI // P):
                            m = pe.matmul(slot("op")[:, bt(b)], yzT[:, j, bt(b)], wout[:, j, :],
                                          start=(b == 0 and j == 0), stop=(j == 1), skip_group_check=True)
                    m.then_inc(S["op_ps"], 1)

            def stage_A(n, s):
                if s == 3:
                    ring_free("n1T", n)
                    pe.wait_ge(S["n1_ready"], n + 1)
                    transposes("n1T", nrm).then_inc(S["n1T_ps"], 1)
                if s == 5:
                    ring_free("dt", n)
                    pe.wait_ge(S["u_ready"], n + 1)
                    for b in range(B):
                        m = pe.matmul(slot("dt")[:, b * NH:(b + 1) * NH], u[:, bt(b)], wdt[:, :],
                                      start=(b == 0), stop=True, skip_group_check=True)
                    m.then_inc(S["dt_ps"], 1)
                if s == 6:
                    pe.wait_ge(S["ulo_ready"], n + 1)
                    for j in range(CB):
                        ring_free(f"xbc{j}", n)
                        cols = slice(DI + j * P, DI + (j + 1) * P)
                        split3(slot(f"xbc{j}")[:, :], wp_hi[:, cols], wp_lo[:, cols], u_hi[:, :], u_lo[:, :])\
                            .then_inc(S["xbc_ps"], 1)
                if s == 12:
                    for pair in range(2):
                        ring_free(f"z{pair}", n)
                        for q in range(2):
                            m = split3(slot(f"z{pair}")[:, q * DI:(q + 1) * DI], u_hi[:, bt(2 * pair + q)],
                                       u_lo[:, bt(2 * pair + q)], wp_hi[:, 0:DI], wp_lo[:, 0:DI], start=(q == 0))
                        m.then_inc(S["z_ps"], 1)

            def expert_unit(n, un):
                e, k = divmod(un, HK)
                if un == 0:
                    pe.wait_ge(S["whi_ready"], n + 1)
                    pe.wait_ge(S["wlo_ready"], n + 1)
                pe.wait_ge(S["tanh_ready"], NU * n + max(un - 1, 0))
                pe.wait_ge(S["aw_ready"], NU * n + max(un - 1, 0))
                for half in range(2):
                    c0 = e * 2 * H2 + half * H2 + k * P
                    m = split3(ab[2 * (un % 2) + half][:, :], wexp_hi[:, c0:c0 + P], wexp_lo[:, c0:c0 + P],
                               w_hi[:, :], w_lo[:, :])
                m.then_inc(S["ab_ps"], 1)
                if k == 0:
                    if e == 0:
                        pe.wait_ge(S["combT_hi"], n + 1)
                        pe.wait_ge(S["combT_lo"], n + 1)
                    pe.wait_ge(S["combB_ready"], E * n + e)
                    pe.matmul(cbps[:, :], pick_r[:, e, :], combT[:, :], start=True, stop=True).then_inc(S["combB_ps"], 1)

            def expert_out(n):
                pe.wait_ge(S["acc_added"], (NU - HK) * n + NU - HK)
                ring_free("out", n)
                for b in range(B):
                    for k in range(HK):
                        m = pe.matmul(slot("out")[:, bt(b)], acc[:, k, bt(b)], wo[:, k, :], start=(b == 0 and k == 0),
                                      stop=(k == 1), skip_group_check=True)
                m.then_inc(S["wo_ps"], 1)

            def body(t, live):
                for s in range(NU + 1):
                    if "C" in live:
                        stage_C(t + 1, s)
                    if "M" in live:
                        stage_M(t + 2, s)
                    if "A" in live:
                        stage_A(t + 3, s)
                    if "E" in live and s < NU:
                        expert_unit(t, s)
                if "E" in live:
                    expert_out(t)

            setup()
            run_bodies(pe, body)

        @block.scalar
        def _(act):
            f = act.activation

            def setup():
                act.wait_ge(S["loads"], 16 * N_LOADS)
                f(silu_c[:, :], cT[:, :], ACT.Silu).then_inc(S["silu_c_ready"], 1)
                f(wp_hi[:, :], wp[:, 0:ZX], ACT.Copy).then_inc(S["split_hi"], 1)
                f(w1m_hi[:, :], w1m[:, :], ACT.Copy).then_inc(S["split_hi"], 1)
                f(wexp_hi[:, :], wexp[:, :], ACT.Copy).then_inc(S["split_hi"], 1)
                f(A_neg[:, :], A_row[:, :], ACT.Exp).then_inc(S["A_exp"], 1)
                act.wait_ge(S["split_hi"], 3)
                f(b1e_half[:, :, :], b1e[:, :, :], ACT.Copy, scale=0.5).then_inc(S["scalar_ready"], 1)
                act.wait_ge(S["scalar_ready"], 1)
                act.wait_ge(S["gpsimd_ready"], 1)
                act.wait_ge(S["vector_ready"], 1)

            def stage_C(n, s):
                if s == 2:
                    act.wait_ge(S["n2T_ps"], n + 1)
                    act.wait_ge(S["vlo_ready"], n)
                    f(v[:, :], slot("n2T")[:, :], ACT.Identity, bias=ln2b[:, 0:1], scale=ln2w[:, 0:1]).then_inc(S["v_ready"], 1)
                    act.wait_ge(S["v_ready"], n + 1)
                    act.wait_ge(S["hid_ps"], 4 * n)
                    f(v_hi[:, :], v[:, :], ACT.Copy).then_inc(S["vhi_ready"], 1)
                if s in (8, 9):
                    if s == 8:
                        act.wait_ge(S["mlp_ps"], n)
                    for q in (0, 1) if s == 8 else (2, 3):
                        act.wait_ge(S["hid_ps"], 4 * n + q + 1)
                        f(gl[:, q, :], slot(f"hid{q}")[:, :], ACT.Gelu, bias=b1m[:, q:q + 1]).then_inc(S["gelu_ready"], 1)
                if s == 13:
                    act.wait_ge(S["n4T_ps"], n + 1)
                    act.wait_ge(S["wlo_ready"], n)
                    act.wait_ge(S["logit_ps"], n)
                    for b in range(B):
                        m = f(w[:, bt(b)], slot("n4T")[:, bt(b)], ACT.Identity, bias=sbT[:, b:b + 1], scale=cb1T[:, b:b + 1])
                    m.then_inc(S["w_ready"], 1)
                if s == 15:
                    act.wait_ge(S["gate_chain"], GATE_STEPS * n + GATE_EXP)
                    f(ex[:, :, :], exs[:, :, :], ACT.Exp).then_inc(S["ex_ready"], 1)
                if s == 16:
                    act.wait_ge(S["w_ready"], n + 1)
                    act.wait_ge(S["ab_ps"], NU * n)
                    f(w_hi[:, :], w[:, :], ACT.Copy).then_inc(S["whi_ready"], 1)
                    act.wait_ge(S["combT_ps"], n + 1)
                    act.wait_ge(S["combB_ps"], E * n)
                    f(combT[0:E, :], slot("combT")[0:E, :], ACT.Copy).then_inc(S["combT_hi"], 1)

            def stage_M(n, s):
                if s == 0:
                    act.wait_ge(S["h_ready"], n + 1)
                    act.wait_ge(S["x2_ready"], n)
                    f(hk[:, :, :], h[:, :, :], ACT.Copy).then_inc(S["h_kept"], 1)
                    act.wait_ge(S["btm_ps"], n + 1)
                    act.wait_ge(S["st_ps"], 2 * n)
                    f(Btm[:, :, :], slot("btm")[:, 0:B * NS].rearrange("p (b s) -> p b s", b=B), ACT.Copy)\
                        .then_inc(S["btm_ready"], 1)
                    act.wait_ge(S["cum_ps"], n + 1)
                    act.wait_ge(S["yt_ready"], 2 * n)
                    act.wait_ge(S["xde_ready"], 2 * n)
                    act.wait_ge(S["Hd_ready"], 2 * n)
                    f(ecs[:, :, :, :].rearrange("p k b h -> p (k b h)"), slot("cum")[:, 0:3 * B * NH], ACT.Exp)\
                        .then_inc(S["ecs_ready"], 1)
                if s in (2, 5):
                    pair = s // 3
                    for q in range(2):
                        b = 2 * pair + q
                        act.wait_ge(S["seg_ps"], 4 * n + b + 1)
                        act.wait_ge(S["W_ready"], 4 * n + max(b - 1, 0))
                        f(L[:, q, :, :].rearrange("p h t -> p (h t)"), slot(f"seg{b}")[:, :], ACT.Exp)\
                            .then_inc(S["L_ready"], 1)
                if s == 10:
                    act.wait_ge(S["yz_ready"], 2 * n + 2)
                    for b in range(B):
                        m = f(yt[:, b, :], yz[:, b, :], ACT.Square, accum_out=ssq[:, b:b + 1])
                    m.then_inc(S["ssq_ready"], 1)
                    act.wait_ge(S["op_ps"], n)
                    for j in range(DI // P):
                        act.wait_ge(S["yzT_ps"], 2 * n + j + 1)
                        f(yzT[:, j, :], slot(f"yzT{j}")[:, :], ACT.Copy).then_inc(S["yzT_ready"], 1)

            def stage_A(n, s):
                if s == 3:
                    act.wait_ge(S["n1T_ps"], n + 1)
                    act.wait_ge(S["ulo_ready"], n)
                    act.wait_ge(S["dt_ps"], n)
                    f(u[:, :], slot("n1T")[:, :], ACT.Identity, bias=ln1b[:, 0:1], scale=ln1w[:, 0:1]).then_inc(S["u_ready"], 1)
                    act.wait_ge(S["u_ready"], n + 1)
                    act.wait_ge(S["z_ps"], 2 * n)
                    f(u_hi[:, :], u[:, :], ACT.Copy).then_inc(S["uhi_ready"], 1)
                if s == 6:
                    act.wait_ge(S["halo_saved"], n)
                    for j in range(CB):
                        act.wait_ge(S["xbc_ps"], CB * n + j + 1)
                        src = slot(f"xbc{j}")[:, :].rearrange("p (b t) -> p b t", b=B)
                        f(xbc[:, j, :, HALO:HALO + P], src, ACT.Copy)
                        f(cv[:, j, :, :], src, ACT.Identity, bias=convb[:, j:j + 1], scale=convw[:, j, HALO:HALO + 1])\
                            .then_inc(S["xbc_read"], 1)
                if s == 12:
                    act.wait_ge(S["yi_ps"], 2 * n)
                    for j in range(CB - 1):
                        act.wait_ge(S["conv_tap"], CB * HALO * n + HALO * (j + 1))
                        m = f(xs[:, j, :].rearrange("p (b t) -> p b t", b=B), cv[:, j, :, :], ACT.Silu)
                    m.then_inc(S["xs_silu"], 1)
                    act.wait_ge(S["conv_tap"], CB * HALO * (n + 1))
                    f(tok4(Bc), cv[0:NS, CB - 1, :, :], ACT.Silu)
                    f(tok4(Cc), cv[NS:2 * NS, CB - 1, :, :], ACT.Silu).then_inc(S["bc_silu"], 1)
                    act.wait_ge(S["yz_ready"], 2 * n)
                    for pair in range(2):
                        act.wait_ge(S["z_ps"], 2 * n + pair + 1)
                        f(sz[:, 2 * pair:2 * pair + 2, :], slot(f"z{pair}")[:, :].rearrange("p (b c) -> p b c", b=2),
                          ACT.Silu).then_inc(S["z_silu"], 1)
                if s == 13:
                    act.wait_ge(S["dt_chain"], DT_STEPS * n + 2)
                    f(ew[:, :, :], nab[:, :, :], ACT.Exp).then_inc(S["dt_exp"], 1)

            def expert_unit(n, un):
                e, k = divmod(un, HK)
                if un == 0:
                    act.wait_ge(S["x4_ready"], n + 1)
                    act.wait_ge(S["comb_ready"], n + 1)
                    act.wait_ge(S["o_ready"], n)
                    act.wait_ge(S["o_bias"], n)
                    f(x4k[:, :, :], x4[:, :, :], ACT.Copy)
                    f(csumk[:, :], csum[:, :], ACT.Copy).then_inc(S["kept"], 1)
                if k == 0:
                    act.wait_ge(S["combB_ps"], E * n + e + 1)
                    act.wait_ge(S["aw_ready"], NU * n + HK * max(e - 1, 0))
                    f(combB[:, e % 2, :], cbps[:, :], ACT.Copy).then_inc(S["combB_ready"], 1)
                act.wait_ge(S["ab_ps"], NU * n + un + 1)
                act.wait_ge(S["g_ready"], NU * n + max(un - 1, 0))
                f(tg[:, un % 2, :], ab[2 * (un % 2) + 1][:, :], ACT.Tanh, bias=b1e_half[:, e, HK + k:HK + k + 1], scale=0.5)\
                    .then_inc(S["tanh_ready"], 1)

            def body(t, live):
                for s in range(NU + 1):
                    if "C" in live:
                        stage_C(t + 1, s)
                    if "M" in live:
                        stage_M(t + 2, s)
                    if "A" in live:
                        stage_A(t + 3, s)
                    if "E" in live and s < NU:
                        expert_unit(t, s)

            setup()
            run_bodies(act, body)

        @block.vector
        def _(dve):
            tt, ts, stt = dve.tensor_tensor, dve.tensor_scalar, dve.scalar_tensor_tensor

            def setup():
                dve.memset(xbc[:, :, :, 0:HALO], 0.0)
                dve.memset(H[:, :, :], 0.0)
                dve.memset(top[:, :, :], PAD)
                dve.memset(lg[:, :, :], PAD)
                dve.memset(minus_half[:, :], -0.5)
                dve.wait_ge(S["silu_c_ready"], 1)
                dve.tensor_copy(silu_row[:, :, :], bcast(silu_c[:, :], 2, [P, B, P])).then_inc(S["silu_rows_ready"], 1)
                dve.wait_ge(S["gpsimd_ready"], 1)
                dve.tensor_copy(pick_r[:, :, :], pick[:, :, :])
                ts(combT[:, :], wexp[0:64, 0:W4], 0.0, None, ALU.mult)
                for j in range(DI // P):
                    ts(Ddiag[:, j, :], ident[:, :], Dcol[:, j:j + 1], None, ALU.mult)
                    ts(wout[:, j, :], wout[:, j, :], normw[:, j:j + 1], None, ALU.mult)
                for b in range(B):
                    dve.wait_ge(S["mod_ps"], 2 * b + 1)
                    dve.tensor_copy(sa[:, b, :], ring[2 * b % 3][:, 0:D])
                    ts(ca1[:, b, :], ring[2 * b % 3][:, D:2 * D], 1.0, None, ALU.add)
                    dve.tensor_copy(ga[:, b, :], ring[2 * b % 3][:, 2 * D:3 * D]).then_inc(S["mod_read"], 1)
                    dve.wait_ge(S["mod_ps"], 2 * b + 2)
                    dve.tensor_copy(gb[:, b, :], ring[(2 * b + 1) % 3][:, 0:D]).then_inc(S["mod_read"], 1)
                dve.wait_ge(S["mod_ps"], 2 * B + 1)
                dve.tensor_copy(sbT[:, :], ring[2 * B % 3][:, 0:B])
                ts(cb1T[:, :], ring[2 * B % 3][:, B:2 * B], 1.0, None, ALU.add).then_inc(S["mod_read"], 1)
                dve.wait_ge(S["split_hi"], 3)
                tt(wp_lo[:, :], wp[:, 0:ZX], wp_hi[:, :].bitcast(F32), ALU.subtract)
                tt(w1m_lo[:, :], w1m[:, :], w1m_hi[:, :].bitcast(F32), ALU.subtract)
                tt(wexp_lo[:, :], wexp[:, :], wexp_hi[:, :].bitcast(F32), ALU.subtract)
                steps = 0
                for g in (ga, gb):
                    dve.wait_ge(S["mod_read"], 2 * B + 1)
                    if steps:
                        dve.wait_ge(S["setup_chain"], steps)
                    ts(gsign[:, :, :], g[:, :, :], 0.0, 2.0, ALU.is_ge, ALU.mult).then_inc(S["setup_chain"], 1)
                    dve.wait_ge(S["setup_chain"], steps + 1)
                    stt(g[:, :, :], g[:, :, :], -1.0, g[:, :, :], ALU.mult, ALU.max).then_inc(S["setup_chain"], 1)
                    ts(gsign[:, :, :], gsign[:, :, :], -1.0, None, ALU.add).then_inc(S["setup_chain"], 1)
                    dve.wait_ge(S["setup_chain"], steps + 3)
                    stt(g[:, :, :], g[:, :, :], 0.25, gsign[:, :, :], ALU.max, ALU.mult).then_inc(S["setup_chain"], 1)
                    steps += 4
                dve.wait_ge(S["setup_chain"], steps)
                dve.wait_ge(S["A_exp"], 1)
                ts(A_neg[:, :], A_neg[:, :], -1.0, None, ALU.mult).then_inc(S["vector_ready"], 1)
                dve.wait_ge(S["vector_ready"], 1)
                dve.wait_ge(S["scalar_ready"], 1)

            def ln_stats(src, which, mv, n, stats_done, mv_done):
                for b in range(B):
                    m = dve.bn_stats(stats[:, which, b, :], src[:, b, :])
                m.then_inc(stats_done, 1)
                wait_before(dve, (stats_done, n + 1))
                for b in range(B):
                    m = dve.bn_aggr(mv[:, b, :], stats[:, which, b, :])
                m.then_inc(mv_done, 1)

            def ln_norm(dst, src, mv, r):
                for b in range(B):
                    m = ts(dst[:, b, :], src[:, b, :], mv[:, b, 0:1], r[:, b:b + 1], ALU.subtract, ALU.mult)
                return m

            def softplus_and_a(n):
                base = DT_STEPS * n
                dve.wait_ge(S["dt_exp"], n + 1)
                ts(den[:, :, :], ew[:, :, :], 2.0, None, ALU.add).then_inc(S["dt_chain"], 1)
                dve.wait_ge(S["dt_chain"], base + 3)
                dve.reciprocal(rden[:, :, :], den[:, :, :]).then_inc(S["dt_chain"], 1)
                dve.wait_ge(S["dt_chain"], base + 4)
                tt(sw[:, :, :], ew[:, :, :], rden[:, :, :], ALU.mult).then_inc(S["dt_chain"], 1)
                dve.wait_ge(S["dt_chain"], base + 5)
                tt(s2[:, :, :], sw[:, :, :], sw[:, :, :], ALU.mult).then_inc(S["dt_chain"], 1)
                dve.wait_ge(S["dt_chain"], base + 6)
                ts(pl[:, :, :], s2[:, :, :], 2.0 / ATANH[0], None, ALU.mult).then_inc(S["dt_chain"], 1)
                at = base + 7
                for c in ATANH[1:]:
                    dve.wait_ge(S["dt_chain"], at)
                    stt(pl[:, :, :], pl[:, :, :], 2.0 / c, s2[:, :, :], ALU.add, ALU.mult).then_inc(S["dt_chain"], 1)
                    at = at + 1
                dve.wait_ge(S["dt_chain"], at)
                stt(pl[:, :, :], pl[:, :, :], 2.0, sw[:, :, :], ALU.add, ALU.mult).then_inc(S["dt_chain"], 1)
                dve.wait_ge(S["dt_chain"], at + 1)
                dve.wait_ge(S["xdt_ready"], 2 * n)
                tt(dt[:, :, :], pl[:, :, :], relu[:, :, :], ALU.add).then_inc(S["dt_chain"], 1)
                dve.wait_ge(S["dt_chain"], at + 2)
                dve.wait_ge(S["m1a_ready"], 4 * n)
                dve.wait_ge(S["cum_ps"], n)
                tt(a[:, :, :], dt[:, :, :], bcast(A_neg[:, :], 1, [P, B, NH]), ALU.mult).then_inc(S["a_ready"], 1)

            def gate(n):
                base = GATE_STEPS * n
                wait_before(dve, (S["logit_ready"], n + 1))
                for b in range(B):
                    m = dve.max(mx[:, b, :], lg[:, b, 0:E])
                m.then_inc(S["gate_chain"], 1)
                dve.wait_ge(S["gate_chain"], base + 1)
                dve.tensor_copy(top[:, :, 0:2], mx[:, :, 0:2]).then_inc(S["gate_chain"], 1)
                tt(exs[:, :, :], lg[:, :, 0:E], mx[:, :, 0:1].to_broadcast([P, B, E]), ALU.subtract).then_inc(S["gate_chain"], 1)
                wait_before(dve, (S["gate_chain"], base + 3))
                for b in range(B):
                    m = dve.match_replace(rep[:, b, :], top[:, b, :], lg[:, b, :], TAKEN)
                m.then_inc(S["gate_chain"], 1)
                dve.wait_ge(S["ex_ready"], n + 1)
                dve.tensor_reduce(Z[:, :], ex[:, :, :], AX.X, ALU.add).then_inc(S["gate_chain"], 1)
                dve.wait_ge(S["gate_chain"], base + 5)
                stt(sel[:, :, :], rep[:, :, 0:E], TAKEN / 2, ex[:, :, :], ALU.is_gt, ALU.mult).then_inc(S["gate_chain"], 1)
                dve.wait_ge(S["gate_chain"], base + 6)
                dve.tensor_reduce(dsum[:, :], sel[:, :, :], AX.X, ALU.add).then_inc(S["gate_chain"], 1)
                dve.wait_ge(S["gate_chain"], base + 7)
                stt(deps[:, :], Z[:, :], TOPK_EPS, dsum[:, :], ALU.mult, ALU.add).then_inc(S["gate_chain"], 1)
                dve.wait_ge(S["gate_chain"], base + 8)
                dve.reciprocal(rinv[:, :], deps[:, :]).then_inc(S["gate_chain"], 1)
                dve.wait_ge(S["gate_chain"], base + 9)
                dve.wait_ge(S["kept"], n)
                dve.wait_ge(S["combT_ps"], n)
                tt(csum[:, :], dsum[:, :], rinv[:, :], ALU.mult)
                stt(comb[:, :, :], sel[:, :, :], 0.5, bcast(rinv[:, :], 2, [P, B, E]), ALU.mult, ALU.mult)\
                    .then_inc(S["comb_ready"], 1)

            def stage_C(n, s):
                if s == 0:
                    ln_stats(x2, 2, mv2, n, S["x2_stats"], S["x2_mv"])
                if s == 1:
                    dve.wait_ge(S["x2_rstd"], n + 1)
                    dve.wait_ge(S["x2b_ready"], n + 1)
                    ln_norm(x2, x2, mv2, r2).then_inc(S["n2_ready"], 1)
                if s == 3:
                    dve.wait_ge(S["vhi_ready"], n + 1)
                    dve.wait_ge(S["hid_ps"], 4 * n)
                    tt(v_lo[:, :], v[:, :], v_hi[:, :].bitcast(F32), ALU.subtract).then_inc(S["vlo_ready"], 1)
                if s == 10:
                    dve.wait_ge(S["mlp_ps"], n + 1)
                    dve.wait_ge(S["x2b_ready"], n + 1)
                    dve.wait_ge(S["x4_ready"], n)
                    tt(x3[:, :, :], tok4(slot("mlp")), x2b[:, :, :], ALU.add).then_inc(S["x3_ready"], 1)
                if s == 12:
                    dve.wait_ge(S["x4_ready"], n + 1)
                    ln_stats(x4, 3, mv4, n, S["x4_stats"], S["x4_mv"])
                if s == 13:
                    dve.wait_ge(S["x4_rstd"], n + 1)
                    dve.wait_ge(S["n4T_ps"], n)
                    ln_norm(nrm4, x4, mv4, r4).then_inc(S["n4_ready"], 1)
                if s == 15:
                    dve.wait_ge(S["logit_ps"], n + 1)
                    dve.tensor_copy(lg[:, :, 0:E], slot("logit")[:, 0:B * E].rearrange("p (b e) -> p b e", b=B))\
                        .then_inc(S["logit_ready"], 1)
                    gate(n)
                if s == 16:
                    dve.wait_ge(S["whi_ready"], n + 1)
                    dve.wait_ge(S["ab_ps"], NU * n)
                    tt(w_lo[:, :], w[:, :], w_hi[:, :].bitcast(F32), ALU.subtract).then_inc(S["wlo_ready"], 1)
                    dve.wait_ge(S["combT_hi"], n + 1)
                    dve.wait_ge(S["combB_ps"], E * n)
                    tt(combT[32:32 + E, :], slot("combT")[0:E, :], combT[0:E, :].bitcast(F32), ALU.subtract)\
                        .then_inc(S["combT_lo"], 1)

            def stage_M(n, s):
                if s == 0:
                    dve.wait_ge(S["yi_ps"], 2 * n)
                    dve.wait_ge(S["xde_ready"], 2 * n)
                    for pair in range(2):
                        bb = slice(2 * pair, 2 * pair + 2)
                        dve.wait_ge(S["xtm_ps"], 2 * n + pair + 1)
                        tt(heads(xdt[:, bb, :]), heads(slot(f"xtm{pair}")[:, :].rearrange("p (b c) -> p b c", b=2)),
                           over_q(dt[:, bb, :]), ALU.mult).then_inc(S["xdt_ready"], 1)
                if s == 1:
                    dve.wait_ge(S["g_ps"], n + 1)
                    tt(gm[:, :, :], tok4(slot("g")), bcast(upto[:, :], 1, [P, B, P]), ALU.mult).then_inc(S["gm_ready"], 1)
                if s in (2, 5):
                    pair = s // 3
                    dve.wait_ge(S["gm_ready"], n + 1)
                    dve.wait_ge(S["yi_ps"], 2 * n + pair)
                    for q in range(2):
                        b = 2 * pair + q
                        dve.wait_ge(S["L_ready"], 4 * n + b + 1)
                        tt(Wt[:, q, :, :], L[:, q, :, :], bcast(gm[:, b, :], 1, [P, NH, P]), ALU.mult).then_inc(S["W_ready"], 1)
                if s in (3, 6):
                    pair = s // 4
                    bb = slice(2 * pair, 2 * pair + 2)
                    dve.wait_ge(S["int_ps"], 2 * n + pair + 1)
                    dve.wait_ge(S["ecs_ready"], n + 1)
                    dve.wait_ge(S["ssq_ready"], n)
                    tt(heads(yt[:, bb, :]), heads(slot(f"int{pair}")[:, :].rearrange("p (b c) -> p b c", b=2)),
                       over_q(ecs[:, 0, bb, :]), ALU.mult).then_inc(S["yt_ready"], 1)
                if s in (4, 7):
                    pair = s // 5
                    bb = slice(2 * pair, 2 * pair + 2)
                    dve.wait_ge(S["yt_ready"], 2 * n + pair + 1)
                    dve.wait_ge(S["yi_ps"], 2 * n + pair + 1)
                    tt(yt[:, bb, :], slot(f"intra{pair}")[:, :].rearrange("p (b c) -> p b c", b=2), yt[:, bb, :], ALU.add)\
                        .then_inc(S["yi_read"], 1)
                    dve.wait_ge(S["yi_read"], 2 * n + pair + 1)
                    dve.wait_ge(S["z_silu"], 2 * n + pair + 1)
                    dve.wait_ge(S["yzT_ps"], 2 * n)
                    tt(yz[:, bb, :], yt[:, bb, :], sz[:, bb, :], ALU.mult).then_inc(S["yz_ready"], 1)
                if s == 9:
                    dve.wait_ge(S["int_ps"], 2 * n + 2)
                    for pair in range(2):
                        bb = slice(2 * pair, 2 * pair + 2)
                        dve.wait_ge(S["st_ps"], 2 * n + pair + 1)
                        dve.wait_ge(S["Hd_ready"], 2 * n + pair + 1)
                        tt(H[:, bb, :], slot(f"st{pair}")[0:NS, :].rearrange("p (b c) -> p b c", b=2), Hd[:, bb, :], ALU.add)\
                            .then_inc(S["H_ready"], 1)
                if s == 11:
                    dve.wait_ge(S["op_ps"], n + 1)
                    dve.wait_ge(S["y_rstd"], n + 1)
                    dve.wait_ge(S["h_kept"], n + 1)
                    dve.wait_ge(S["n2T_ps"], n)
                    for b in range(B):
                        m = stt(x2[:, b, :], slot("op")[:, bt(b)], ry[:, b:b + 1], hk[:, b, :], ALU.mult, ALU.add)
                    m.then_inc(S["x2_ready"], 1)
                    dve.wait_ge(S["x2_ready"], n + 1)

            def stage_A(n, s):
                if s == 0:
                    dve.wait_ge(S["x_loaded"], 16 * (n + 1))
                    ln_stats(xt, 0, mva, n, S["xa_stats"], S["xa_mv"])
                if s == 2:
                    dve.wait_ge(S["h_ready"], n + 1)
                    ln_stats(h, 1, mvh, n, S["h_stats"], S["h_mv"])
                if s == 3:
                    dve.wait_ge(S["h_rstd"], n + 1)
                    dve.wait_ge(S["n1T_ps"], n)
                    ln_norm(nrm, h, mvh, rh).then_inc(S["n1_ready"], 1)
                if s == 4:
                    dve.wait_ge(S["uhi_ready"], n + 1)
                    dve.wait_ge(S["z_ps"], 2 * n)
                    tt(u_lo[:, :], u[:, :], u_hi[:, :].bitcast(F32), ALU.subtract).then_inc(S["ulo_ready"], 1)
                if s == 5:
                    dve.wait_ge(S["dt_ps"], n + 1)
                    tt(dtv[:, :, :], slot("dt")[:, 0:B * NH].rearrange("p (b h) -> p b h", b=B),
                       bcast(dtb[:, :], 1, [P, B, NH]), ALU.add).then_inc(S["dt_chain"], 1)
                    dve.wait_ge(S["dt_chain"], DT_STEPS * n + 1)
                    ts(relu[:, :, :], dtv[:, :, :], 0.0, None, ALU.max)
                    stt(nab[:, :, :], dtv[:, :, :], -1.0, dtv[:, :, :], ALU.mult, ALU.min).then_inc(S["dt_chain"], 1)
                if s in (7, 8, 9):
                    j = s - 7
                    dve.wait_ge(S["xbc_read"], CB * n + j + 1)
                    for k in range(HALO):
                        if k > 0:
                            dve.wait_ge(S["conv_tap"], CB * HALO * n + HALO * j + k)
                        stt(cv[:, j, :, :], xbc[:, j, :, k:k + P], convw[:, j, k:k + 1], cv[:, j, :, :],
                            ALU.mult, ALU.add).then_inc(S["conv_tap"], 1)
                if s == 14:
                    softplus_and_a(n)

            def expert_unit(n, un):
                e, k = divmod(un, HK)
                dve.wait_ge(S["ab_ps"], NU * n + un + 1)
                dve.wait_ge(S["combB_ready"], E * n + e + 1)
                dve.wait_ge(S["g_ready"], NU * n + max(un - 1, 0))
                stt(aw[:, un % 2, :], ab[2 * (un % 2)][:, :], b1e[:, e, k:k + 1], combB[:, e % 2, :], ALU.add, ALU.mult)\
                    .then_inc(S["aw_ready"], 1)

            def expert_gate(n, un):
                e, k = divmod(un, HK)
                dve.wait_ge(S["aw_ready"], NU * n + un + 1)
                dve.wait_ge(S["tanh_ready"], NU * n + un + 1)
                if e == 0:
                    dve.wait_ge(S["wo_ps"], n)
                    dst = acc[:, k, :]
                else:
                    dve.wait_ge(S["acc_added"], (NU - HK) * n + max(un - 5, 0))
                    dst = gg[:, un % 4, :]
                stt(dst, tg[:, un % 2, :], 1.0, aw[:, un % 2, :], ALU.add, ALU.mult).then_inc(S["g_ready"], 1)

            def expert_out(n):
                dve.wait_ge(S["wo_ps"], n + 1)
                dve.wait_ge(S["kept"], n + 1)
                dve.wait_ge(S["stored"], 16 * n)
                for b in range(B):
                    m = stt(o[:, b, :], borow[:, :], csumk[:, b:b + 1], slot("out")[:, bt(b)], ALU.mult, ALU.add)
                m.then_inc(S["o_bias"], 1)

            def body(t, live):
                for s in range(NU + 1):
                    if "C" in live:
                        stage_C(t + 1, s)
                    if "M" in live:
                        stage_M(t + 2, s)
                    if "A" in live:
                        stage_A(t + 3, s)
                    if "E" in live:
                        if s < NU:
                            expert_unit(t, s)
                        if s > 0:
                            expert_gate(t, s - 1)
                if "E" in live:
                    expert_out(t)

            setup()
            run_bodies(dve, body)

        @block.gpsimd
        def _(pool):
            tt, ts = pool.tensor_tensor, pool.tensor_scalar

            def setup():
                pool.memset(ones[:, :], 1.0).then_inc(S["masks_filled"], 1)
                pool.memset(ident[:, :], 0.0).then_inc(S["masks_filled"], 1)
                pool.memset(pick[:, :, :], 0.0).then_inc(S["masks_filled"], 1)
                pool.wait_ge(S["masks_filled"], 3)
                pool.affine_select(out=ident[:, :], in_=ident[:, :], pattern=[[-1, P]], compare_op=ALU.not_equal, fill=1.0,
                                   base=0, channel_multiplier=1)
                pool.affine_select(out=upto[:, :], in_=ones[:, :], pattern=[[1, P]], compare_op=ALU.is_ge, fill=0.0,
                                   base=0, channel_multiplier=-1)
                pool.affine_select(out=after[:, :], in_=ones[:, :], pattern=[[-1, P]], compare_op=ALU.is_gt, fill=0.0,
                                   base=0, channel_multiplier=1)
                pool.affine_select(out=pick[:, :, :], in_=pick[:, :, :], pattern=[[-1, E], [0, P]],
                                   compare_op=ALU.not_equal, fill=1.0, base=0, channel_multiplier=1).then_inc(S["masks_made"], 1)
                pool.wait_ge(S["masks_made"], 1)
                pool.affine_select(out=pick[:, :, :], in_=pick[:, :, :], pattern=[[-1, E], [0, P]],
                                   compare_op=ALU.not_equal, fill=1.0, base=-32, channel_multiplier=1)\
                    .then_inc(S["gpsimd_ready"], 1)
                pool.wait_ge(S["gpsimd_ready"], 1)
                pool.wait_ge(S["vector_ready"], 1)

            def rstd(dst, which, var, scale, eps, var_done, rstd_done, n):
                ts(var_e[:, which, :], var, scale, eps, ALU.mult, ALU.add).then_inc(var_done, 1)
                pool.wait_ge(var_done, n + 1)
                tt(dst[:, :], var_e[:, which, :], minus_half[:, :], ALU.pow).then_inc(rstd_done, 1)

            def stage_C(n, s):
                if s == 0:
                    pool.wait_ge(S["x3_ready"], n)
                    pool.wait_ge(S["x2_ready"], n + 1)
                    tt(x2b[:, :, :], x2[:, :, :], bcast(b2row[:, :], 1, [P, B, D]), ALU.add).then_inc(S["x2b_ready"], 1)
                    wait_before(pool, (S["x2_mv"], n + 1))
                    rstd(r2, 2, mv2[:, :, 1], 1.0, LN_EPS, S["x2_var"], S["x2_rstd"], n)
                if s == 10:
                    pool.wait_ge(S["x3_ready"], n + 1)
                    tt(x3[:, :, :], x3[:, :, :], ga[:, :, :], ALU.mult).then_inc(S["x3_scaled"], 1)
                    pool.wait_ge(S["x3_scaled"], n + 1)
                    pool.wait_ge(S["xr_loaded"], 16 * (n + 1))
                    pool.wait_ge(S["kept"], n)
                    pool.wait_ge(S["n4_ready"], n)
                    tt(x4[:, :, :], x3[:, :, :], xr[:, :, :], ALU.add).then_inc(S["x4_ready"], 1)
                if s == 12:
                    wait_before(pool, (S["x4_mv"], n + 1))
                    rstd(r4, 3, mv4[:, :, 1], 1.0, LN_EPS, S["x4_var"], S["x4_rstd"], n)

            def stage_M(n, s):
                if s in (0, 3):
                    pair = s // 3
                    pool.wait_ge(S["a_ready"], n + 1)
                    for q in range(2):
                        b = 2 * pair + q
                        pool.wait_ge(S["seg_ps"], 4 * n + max(b - 1, 0))
                        tt(m1a[:, q, :, :], bcast(upto[:, :], 1, [P, NH, P]), bcast(a[:, b, :], 2, [P, NH, P]), ALU.mult)\
                            .then_inc(S["m1a_ready"], 1)
                if s == 5:
                    pool.wait_ge(S["ecs_ready"], n + 1)
                    pool.wait_ge(S["xdt_ready"], 2 * n + 2)
                    pool.wait_ge(S["st_ps"], 2 * n)
                    for pair in range(2):
                        bb = slice(2 * pair, 2 * pair + 2)
                        tt(heads(xde[:, bb, :]), heads(xdt[:, bb, :]), over_q(ecs[:, 1, bb, :]), ALU.mult)\
                            .then_inc(S["xde_ready"], 1)
                if s == 7:
                    pool.wait_ge(S["H_ready"], 2 * n)
                    for pair in range(2):
                        bb = slice(2 * pair, 2 * pair + 2)
                        tt(heads(Hd[:, bb, :]), heads(H[:, bb, :]), over_q(ecs[0:NS, 2, bb, :]), ALU.mult)\
                            .then_inc(S["Hd_ready"], 1)
                if s == 10:
                    wait_before(pool, (S["ssq_ready"], n + 1))
                    rstd(ry, 4, ssq[:, :], 1.0 / DI, LN_EPS, S["y_var"], S["y_rstd"], n)

            def stage_A(n, s):
                if s == 1:
                    wait_before(pool, (S["xa_mv"], n + 1))
                    rstd(ra, 0, mva[:, :, 1], 1.0, LN_EPS, S["xa_var"], S["xa_rstd"], n)
                    wait_before(pool, (S["xa_rstd"], n + 1), (S["h_kept"], n), (S["n1_ready"], n))
                    for b in range(B):
                        m = ts(h[:, b, :], xt[:, b, :], mva[:, b, 0:1], ra[:, b:b + 1], ALU.subtract, ALU.mult)
                    m.then_inc(S["xa_norm"], 1)
                    pool.wait_ge(S["xa_norm"], n + 1)
                    tt(h[:, :, :], h[:, :, :], ca1[:, :, :], ALU.mult).then_inc(S["xa_scaled"], 1)
                    pool.wait_ge(S["xa_scaled"], n + 1)
                    tt(h[:, :, :], h[:, :, :], sa[:, :, :], ALU.add).then_inc(S["h_ready"], 1)
                if s == 2:
                    wait_before(pool, (S["h_mv"], n + 1))
                    rstd(rh, 1, mvh[:, :, 1], 1.0, LN_EPS, S["h_var"], S["h_rstd"], n)
                if s == 10:
                    wait_before(pool, (S["conv_tap"], CB * HALO * (n + 1)))
                    pool.tensor_copy(xbc[:, :, :, 0:HALO], xbc[:, :, :, P:P + HALO]).then_inc(S["halo_saved"], 1)

            def expert_add(n, un):
                e, k = divmod(un, HK)
                if e == 0:
                    return
                pool.wait_ge(S["g_ready"], NU * n + un + 1)
                pool.wait_ge(S["acc_added"], (NU - HK) * n + max(un - 3, 0))
                tt(acc[:, k, :], acc[:, k, :], gg[:, un % 4, :], ALU.add).then_inc(S["acc_added"], 1)

            def expert_out(n):
                pool.wait_ge(S["o_bias"], n + 1)
                tt(o[:, :, :], o[:, :, :], gb[:, :, :], ALU.mult).then_inc(S["o_scaled"], 1)
                pool.wait_ge(S["o_scaled"], n + 1)
                pool.wait_ge(S["kept"], n + 1)
                tt(o[:, :, :], o[:, :, :], x4k[:, :, :], ALU.add).then_inc(S["o_ready"], 1)

            def body(t, live):
                for s in range(NU + 1):
                    if "C" in live:
                        stage_C(t + 1, s)
                    if "M" in live:
                        stage_M(t + 2, s)
                    if "A" in live:
                        stage_A(t + 3, s)
                    if "E" in live and s > 0:
                        expert_add(t, s - 1)
                if "E" in live:
                    expert_out(t)

            setup()
            run_bodies(pool, body)


def kernel(**inputs):
    import numpy as np
    import concourse.bacc as bacc
    from concourse.bass_utils import run_bass_kernel_spmd

    def per_partition(v, rows=1):
        return np.moveaxis(v.reshape(v.shape[:-1] + (rows, P)), -1, 0)

    L = {k: np.asarray(v) for k, v in inputs.items()}
    n_heads = L["L0_attn_D"].shape[0]
    inner = L["L0_attn_norm_w"].shape[0]
    arrays = {
        "x": L["L0_attn_x"], "ln1_w": per_partition(L["L0_attn_ln1_w"]), "ln1_b": per_partition(L["L0_attn_ln1_b"]),
        "ln2_w": per_partition(L["L0_attn_ln2_w"]), "ln2_b": per_partition(L["L0_attn_ln2_b"]),
        "in_projT": L["L0_attn_in_proj_w"].T,
        "conv_w": np.moveaxis(L["L0_attn_conv_w"].reshape(-1, P, 4), 0, 1),
        "conv_b": per_partition(L["L0_attn_conv_b"], 3),
        "dt_bias": L["L0_attn_dt_bias"], "A_log": L["L0_attn_A_log"],
        "D_col": per_partition(np.repeat(L["L0_attn_D"], inner // n_heads), inner // P),
        "norm_w": per_partition(L["L0_attn_norm_w"], inner // P), "out_projT": L["L0_attn_out_proj_w"].T,
        "mlp_w1T": L["L0_attn_mlp_w1"].T, "mlp_b1": per_partition(L["L0_attn_mlp_b1"], 4),
        "mlp_w2T": L["L0_attn_mlp_w2"].T, "mlp_b2": L["L0_attn_mlp_b2"], "gateT": L["L0_ffn_Wg"].T,
        "moe_w1T": np.moveaxis(L["L0_ffn_W1"], 2, 0).reshape(P, -1), "moe_b1": per_partition(L["L0_ffn_b1"], 4),
        "moe_woT": L["L0_ffn_Wo"].T, "moe_bo": L["L0_ffn_bo"], "cT": L["L0_c"].T, "wmod": L["L0_wmod"],
    }
    arrays = {k: np.ascontiguousarray(v) for k, v in arrays.items()}
    nc = bacc.Bacc("TRN2", target_bir_lowering=False, num_devices=1)
    d = {k: nc.dram_tensor("in_" + k, v.shape, mybir.dt.from_np(v.dtype), kind="ExternalInput").ap() for k, v in arrays.items()}
    out = nc.dram_tensor("out", arrays["x"].shape, F32, kind="ExternalOutput").ap()
    build(nc, d, out)
    r = run_bass_kernel_spmd(nc, [{"in_" + k: v for k, v in arrays.items()}], core_ids=[0])
    return r.results[0]["out"]
```

```python
from contextlib import ExitStack

import concourse.bass as bass
from concourse import mybir

F32 = mybir.dt.float32
F32R = mybir.dt.float32r
ALU = mybir.AluOpType
ACT = mybir.ActivationFunctionType
AX = mybir.AxisListType

P = 128
LN_EPS = 1e-5
TOPK_EPS = 1e-9
PAD = -3.0e38
TAKEN = 3.0e38
ATANH = (13, 11, 9, 7, 5, 3)
DT_STEPS = 8 + len(ATANH)
SP_OPS = 7 + len(ATANH)
GATE_STEPS = 9
N_MOD, N_FRONT, N_LATE = 2, 8, 13
GATE_EXP = 3

EVENTS = """
x_loaded xa_stats xa_mv xa_var xa_rstd xa_norm xa_scaled h_ready xr_loaded h_kept
h_stats h_mv h_var h_rstd n1_ready n1T_ps u_ready uhi_ready ulo_ready
dt_ps dt_chain dt_exp a_ready xbc_ps xbc_read conv_tap halo_saved z_ps z_silu xs_silu bc_silu
xtm_ps xdt_ready btm_ps btm_ready cum_ps ecs_ready g_ps gm_ready
m1a_ready seg_ps L_ready W_ready int_ps yt_ready yi_ps yi_read yz_ready
x2_seeded ssq_ready y_var y_rstd xde_ready st_ps Hd_ready H_ready
yzT_ps yzT_ready op_ps x2_ready
x2_stats x2_mv x2_var x2_rstd n2_ready n2T_ps v_ready vhi_ready vlo_ready x2b_ready
hid_ps gelu_ready mlp_ps x3_ready x3_scaled x4_ready
x4_stats x4_mv x4_var x4_rstd n4_ready n4T_ps w_ready whi_ready wlo_ready
logit_ps logit_ready gate_chain ex_ready comb_ready combT_ps combT_hi combT_lo
kept combB_ps combB_ready ab_ps tanh_ready aw_ready g_ready acc_added
wo_ps o_bias o_scaled o_ready o_free
""".split()
SETUP = "loads_mod loads_front loads_late late_hi late_vector late_scalar silu_c_ready silu_rows_ready mod_ps mod_read masks_filled masks_made split_hi vector_ready gpsimd_ready A_exp setup_chain".split()


def bcast(ap, where, shape):
    return ap.unsqueeze(where).to_broadcast(shape)


def build(nc, d, out):
    B, T, D = d["x"].shape
    NT = T // P
    E = d["moe_b1"].shape[1]
    DI = d["out_projT"].shape[0]
    NH = d["A_log"].shape[0]
    HD = DI // NH
    NS = (d["conv_w"].shape[1] * P - DI) // 2
    MH = d["mlp_w1T"].shape[1]
    MQ = MH // P
    H2 = d["moe_woT"].shape[0]
    HK = H2 // P
    CB = d["conv_w"].shape[1]
    TAPS = d["conv_w"].shape[2]
    HALO = TAPS - 1
    NU = E * HK
    DP = d["in_projT"].shape[1]
    ZX = DP - NH
    W4 = B * P
    assert D == P and B == 4 and NH == 4 and E == 8 and CB == 3 and HK == 2

    with ExitStack() as ctx:
        def sb(name, shape, dt=F32):
            return ctx.enter_context(nc.sbuf_tensor(name, shape, dt))

        wdt = sb("wdt", [P, NH]); wp_hi = sb("wp_hi", [P, ZX], F32R); wp_lo = sb("wp_lo", [P, ZX], F32R)
        w1m_hi = sb("w1m_hi", [P, MH], F32R); w1m_lo = sb("w1m_lo", [P, MH], F32R)
        w2m = sb("w2m", [P, MQ, D])
        wexp_hi = sb("wexp_hi", [P, E * 2 * H2], F32R); wexp_lo = sb("wexp_lo", [P, E * 2 * H2], F32R)
        wo = sb("wo", [P, HK, D]); wout = sb("wout", [P, DI // P, D]); wg = sb("wg", [P, E])
        ln1w = sb("ln1w", [P, 1]); ln1b = sb("ln1b", [P, 1]); ln2w = sb("ln2w", [P, 1]); ln2b = sb("ln2b", [P, 1])
        convw = sb("convw", [P, CB, TAPS]); convb = sb("convb", [P, CB])
        dtb = sb("dtb", [P, NH]); A_row = sb("A_row", [P, NH]); A_neg = sb("A_neg", [P, NH])
        Dcol = sb("Dcol", [P, DI // P]); Ddiag = sb("Ddiag", [P, DI // P, P])
        normw = sb("normw", [P, DI // P]); b1m = sb("b1m", [P, MQ]); b2row = sb("b2row", [P, D])
        b1e = sb("b1e", [P, E, 2 * HK]); b1e_half = sb("b1e_half", [P, E, 2 * HK]); borow = sb("borow", [P, D])
        cT = sb("cT", [P, B]); silu_c = sb("silu_c", [P, B])
        ones = sb("ones", [P, P]); ident = sb("ident", [P, P])
        upto = sb("upto", [P, P])
        after = sb("after", [P, P])
        pick_r = sb("pick_r", [64, E, P], F32R)
        minus_half = sb("minus_half", [P, B])
        sa = sb("sa", [P, B, D]); ca1 = sb("ca1", [P, B, D]); ga = sb("ga", [P, B, D]); gb = sb("gb", [P, B, D])
        sbT = sb("sbT", [P, B]); cb1T = sb("cb1T", [P, B])

        xt = sb("xt", [P, B, D]); xr = sb("xr", [P, B, D]); stats = sb("stats", [P, 4, B, 6])
        mva = sb("mva", [P, B, 2]); mvh = sb("mvh", [P, B, 2]); mv2 = sb("mv2", [P, B, 2]); mv4 = sb("mv4", [P, B, 2])
        var_e = sb("var_e", [P, 5, B]); nmean = sb("nmean", [P, 4, B]); shift = sb("shift", [P, 4, B]); ra = sb("ra", [P, B]); rh = sb("rh", [P, B]); r2 = sb("r2", [P, B]); r4 = sb("r4", [P, B])
        h = sb("h", [P, B, D]); hk = sb("hk", [P, B, D]); nrm = sb("nrm", [P, B, D]); nrm4 = sb("nrm4", [P, B, D])
        u = sb("u", [P, W4]); u_hi = sb("u_hi", [P, W4], F32R); u_lo = sb("u_lo", [P, W4], F32R)
        dtv = sb("dtv", [P, B, NH]); nab = sb("nab", [P, B, NH]); ew = sb("ew", [P, B, NH]); den = sb("den", [P, B, NH])
        rden = sb("rden", [P, B, NH]); sw = sb("sw", [P, B, NH]); s2 = sb("s2", [P, B, NH]); pl = sb("pl", [P, B, NH])
        relu = sb("relu", [P, B, NH]); dt = sb("dt", [P, B, NH]); a = sb("a", [P, B, NH])
        xbc = sb("xbc", [P, CB, B, HALO + P]); cv = sb("cv", [P, CB, B, P])
        xs = sb("xs", [P, DI // P, W4]); Bc = sb("Bc", [NS, W4]); Cc = sb("Cc", [NS, W4])
        sz = sb("sz", [P, B, DI]); xdt = sb("xdt", [P, B, DI]); xde = sb("xde", [P, B, DI]); Btm = sb("Btm", [P, B, NS])
        ecs = sb("ecs", [P, 3, B, NH])
        gm = sb("gm", [P, B, P]); m1a = sb("m1a", [P, 2, NH, P]); L = sb("L", [P, 2, NH, P]); Wt = sb("Wt", [P, 2, NH, P])
        yt = sb("yt", [P, B, DI]); yz = sb("yz", [P, B, DI])
        ssq = sb("ssq", [P, B]); ry = sb("ry", [P, B])
        H = sb("H", [NS, B, DI]); Hd = sb("Hd", [NS, B, DI])
        yzT = sb("yzT", [P, DI // P, W4]); x2 = sb("x2", [P, B, D]); x2b = sb("x2b", [P, B, D]); x3 = x2b
        v = sb("v", [P, W4]); v_hi = sb("v_hi", [P, W4], F32R); v_lo = sb("v_lo", [P, W4], F32R)
        gl = sb("gl", [P, MQ, W4]); x4 = sb("x4", [P, B, D])
        w = sb("w", [P, W4]); w_hi = sb("w_hi", [P, W4], F32R); w_lo = sb("w_lo", [P, W4], F32R)
        NP_ = E + 6
        lg = sb("lg", [P, B, NP_]); mx = sb("mx", [P, B, 8]); top = sb("top", [P, B, 8]); rep = sb("rep", [P, B, NP_])
        exs = sb("exs", [P, B, E]); ex = sb("ex", [P, B, E]); Z = sb("Z", [P, B]); sel = sb("sel", [P, B, E])
        dsum = sb("dsum", [P, B]); deps = sb("deps", [P, B]); rinv = sb("rinv", [P, B]); csum = sb("csum", [P, B])
        comb = sb("comb", [P, B, E]); combT = sb("combT", [64, W4], F32R)
        csumk = sb("csumk", [P, B]); combB = sb("combB", [P, 2, W4])
        aw = sb("aw", [P, 2, W4]); acc = sb("acc", [P, HK, W4])
        late = sb("late", [P, 8 * W4])
        gg = late[:, 0:4 * W4].rearrange("p (q w) -> p q w", q=4)
        tg = late[:, 4 * W4:6 * W4].rearrange("p (q w) -> p q w", q=2)
        x4k, o = (late[:, (6 + q) * W4:(7 + q) * W4].rearrange("p (b d) -> p b d", b=B) for q in range(2))
        wexp = late
        raw = gl[:, :, :].rearrange("p q w -> p (q w)")
        wp, w1m = raw[:, 0:ZX], raw[:, ZX:ZX + MH]
        wmod = xde[:, :, :].rearrange("p b c -> p (b c)")[:, 0:6 * D]
        silu_row, gsign = yz[:, 0:2, :].rearrange("p b (c d) -> p (b c) d", d=D), x2
        pick = combB[0:64, :, :].rearrange("p a (e w) -> p (a e) w", w=P)

        ring = [ctx.enter_context(nc.psum_tensor(f"ring{i}", [P, W4], F32)) for i in range(3)]
        ab = [ctx.enter_context(nc.psum_tensor(f"ab{i}", [P, W4], F32)) for i in range(4)]
        cbps = ctx.enter_context(nc.psum_tensor("cbps", [P, W4], F32))
        S = {e: ctx.enter_context(nc.semaphore(e)) for e in SETUP + EVENTS}
        block = ctx.enter_context(nc.Block())

        uses = {
            "hid0": (1, "gelu_ready", 4, 1), "hid1": (1, "gelu_ready", 4, 2), "out": (-1, "o_bias", 1, 1),
            "hid2": (1, "gelu_ready", 4, 3), "hid3": (1, "gelu_ready", 4, 4),
            "btm": (2, "btm_ready", 1, 1), "g": (2, "gm_ready", 1, 1), "cum": (2, "ecs_ready", 1, 1),
            "seg0": (2, "L_ready", 4, 1), "seg1": (2, "L_ready", 4, 2), "n1T": (3, "u_ready", 1, 1),
            "int0": (2, "yt_ready", 2, 1), "dt": (3, "dt_chain", DT_STEPS, 1), "intra0": (2, "yi_read", 2, 1),
            "xbc0": (3, "xbc_read", CB, 1), "mlp": (1, "x3_ready", 1, 1),
            "seg2": (2, "L_ready", 4, 3), "seg3": (2, "L_ready", 4, 4), "int1": (2, "yt_ready", 2, 2),
            "xbc1": (3, "xbc_read", CB, 2), "intra1": (2, "yi_read", 2, 2), "xbc2": (3, "xbc_read", CB, 3), "n4T": (1, "w_ready", 1, 1),
            "st0": (2, "H_ready", 2, 1), "st1": (2, "H_ready", 2, 2), "logit": (1, "logit_ready", 1, 1),
            "yzT0": (2, "yzT_ready", 2, 1), "yzT1": (2, "yzT_ready", 2, 2), "op": (2, "x2_ready", 1, 1),
            "z0": (3, "z_silu", 2, 1), "z1": (3, "z_silu", 2, 2), "xtm0": (3, "xdt_ready", 2, 1),
            "combT": (1, "combT_lo", 1, 1), "n2T": (2, "v_ready", 1, 1), "xtm1": (3, "xdt_ready", 2, 2), "spare": None,
        }
        order = list(uses)
        assert len(order) % 3 == 0
        slot = lambda name: ring[order.index(name) % 3]

        def ring_reader(name, n):
            t, at, first = n - uses[name][0], order.index(name), isinstance(n, int)
            while True:
                at -= 3
                if at < 0:
                    at, t = at + len(order), t - 1
                if uses[order[at]] is None:
                    continue
                ahead, sem, per, count = uses[order[at]]
                if not first or 0 <= t + ahead < NT:
                    return S[sem], per * (t + ahead) + count
                if t < -6:
                    return None

        bt = lambda b: slice(b * P, (b + 1) * P)
        tok4 = lambda t: t[:, :].rearrange("p (b d) -> p b d", b=B)
        heads = lambda t: t.rearrange("p b (h q) -> p b h q", h=NH)
        over_q = lambda t: t.unsqueeze(3).to_broadcast([t.shape[0], t.shape[1], NH, HD])

        def wait_before(eng, *waits):
            waits = [(sem, value if isinstance(value, int) else eng.to_reg(value)) for sem, value in waits]
            eng.wait_ge(S["vector_ready"], 1)
            for sem, value in waits:
                eng.wait_ge(sem, value)

        def x_tile(t, n):
            return t[:, bass.ds(n * P, P), :].rearrange("b t d -> t b d")

        def run_bodies(eng, body):
            def live(t):
                stages = "".join(c for c, ahead in zip("OECMAX", range(-1, 5)) if 0 <= t + ahead < NT)
                return stages + "S" if t == -3 else stages
            for t in range(-4, 1):
                body(t, live(t))
            with eng.Fori(1, NT - 4) as t:
                body(t, "OECMAX")
            for t in range(NT - 4, NT + 1):
                body(t, live(t))

        @block.sync
        def _(sp):
            loads_mod = [(cT[:, :], d["cT"]), (wmod, d["wmod"])]
            loads_front = [
                (wp, d["in_projT"][:, 0:ZX]), (ln1w[:, :], d["ln1_w"]), (ln1b[:, :], d["ln1_b"]),
                (wdt[:, :], d["in_projT"][:, ZX:DP]), (convw[:, :, :], d["conv_w"]), (convb[:, :], d["conv_b"]),
                (dtb[:, :], d["dt_bias"].unsqueeze(0).to_broadcast([P, NH])),
                (A_row[:, :], d["A_log"].unsqueeze(0).to_broadcast([P, NH])),
            ]
            loads_late = [
                (Dcol[:, :], d["D_col"]), (normw[:, :], d["norm_w"]),
                (wout[:, :, :], d["out_projT"].rearrange("(j p) n -> p j n", p=P)),
                (w1m, d["mlp_w1T"]), (wexp[:, :], d["moe_w1T"]), (b1e[:, :, :], d["moe_b1"]),
                (ln2w[:, :], d["ln2_w"]), (ln2b[:, :], d["ln2_b"]), (b1m[:, :], d["mlp_b1"]),
                (w2m[:, :, :], d["mlp_w2T"].rearrange("(q p) n -> p q n", p=P)),
                (b2row[:, :], d["mlp_b2"].unsqueeze(0).to_broadcast([P, D])), (wg[:, :], d["gateT"]),
                (wo[:, :, :], d["moe_woT"].rearrange("(k p) n -> p k n", p=P)),
            ]
            assert (len(loads_mod), len(loads_front), len(loads_late)) == (N_MOD, N_FRONT, N_LATE)

            def load_x(n):
                sp.wait_ge(S["xa_norm"], n)
                sp.dma_start(xt[:, :, :], x_tile(d["x"], n)).then_inc(S["x_loaded"], 16)

            def load_residual(n):
                sp.wait_ge(S["x4_ready"], n)
                sp.dma_start(xr[:, :, :], x_tile(d["x"], n)).then_inc(S["xr_loaded"], 16)

            def store(n):
                sp.wait_ge(S["o_ready"], n + 1)
                sp.dma_start(x_tile(out, n), o[:, :, :]).then_inc(S["o_free"], 16)

            def body(t, live):
                if "X" in live and not (isinstance(t, int) and t == -4):
                    load_x(t + 4)
                if "C" in live:
                    load_residual(t + 1)
                if "O" in live:
                    store(t - 1)

            for dst, src in loads_mod:
                sp.dma_start(dst, src).then_inc(S["loads_mod"], 16)
            sp.dma_start(xt[:, :, :], x_tile(d["x"], 0)).then_inc(S["x_loaded"], 16)
            for dst, src in loads_front:
                sp.dma_start(dst, src).then_inc(S["loads_front"], 16)
            for dst, src in loads_late:
                sp.dma_start(dst, src).then_inc(S["loads_late"], 16)
            sp.dma_start(borow[:, :], d["moe_bo"].unsqueeze(0).to_broadcast([P, D])).then_inc(S["o_free"], 16)
            run_bodies(sp, body)
            sp.wait_ge(S["o_free"], 16 * (NT + 1))

        @block.tensor
        def _(pe):
            def split3(o, ahi, alo, bhi, blo, start=True):
                pe.matmul(o, ahi, bhi, start=start, stop=False, skip_group_check=True)
                pe.matmul(o, ahi, blo, start=False, stop=False, skip_group_check=True)
                return pe.matmul(o, alo, bhi, start=False, stop=True, skip_group_check=True)

            def ring_free(name, n):
                reader = ring_reader(name, n)
                if reader is not None:
                    pe.wait_ge(*reader)

            def setup():
                pe.wait_ge(S["silu_rows_ready"], 1)
                for b in range(B):
                    for part, (c0, cols) in enumerate(((0, 3 * D), (5 * D, D))):
                        k = 2 * b + part
                        if k >= 3:
                            pe.wait_ge(S["mod_read"], k - 2)
                        pe.matmul(ring[k % 3][:, 0:cols], silu_row[:, b, :], wmod[:, c0:c0 + cols],
                                  start=True, stop=True).then_inc(S["mod_ps"], 1)
                pe.wait_ge(S["mod_read"], 2 * B - 2)
                for j in range(2):
                    m = pe.matmul(ring[2 * B % 3][:, j * B:(j + 1) * B], wmod[:, (3 + j) * D:(4 + j) * D], silu_c[:, :],
                                  start=(j == 0), stop=True, skip_group_check=True)
                m.then_inc(S["mod_ps"], 1)
                pe.wait_ge(S["mod_read"], 2 * B + 1)
                pe.wait_ge(S["gpsimd_ready"], 1)
                pe.wait_ge(S["loads_front"], 16 * N_FRONT)
                pe.wait_ge(S["split_hi"], 1)
                pe.wait_ge(S["vector_ready"], 1)

            def transposes(name, src):
                for b in range(B):
                    m = pe.transpose(slot(name)[:, bt(b)], src[:, b, :], ident[:, :])
                return m

            def hidden(q, n):
                ring_free(f"hid{q}", n)
                cols = slice(q * P, (q + 1) * P)
                split3(slot(f"hid{q}")[:, :], w1m_hi[:, cols], w1m_lo[:, cols], v_hi[:, :], v_lo[:, :])\
                    .then_inc(S["hid_ps"], 1)

            def stage_C(n, s):
                if s == 0:
                    pe.wait_ge(S["vhi_ready"], n + 1)
                    pe.wait_ge(S["vlo_ready"], n + 1)
                if s in (0, 1):
                    hidden(2 * s, n)
                    hidden(2 * s + 1, n)
                if s in (4.5, 5):
                    if s == 4.5:
                        ring_free("mlp", n)
                        pe.wait_ge(S["gelu_ready"], 4 * n + 4)
                    for b in (0, 1) if s == 4.5 else (2, 3):
                        for q in range(MQ):
                            m = pe.matmul(slot("mlp")[:, bt(b)], gl[:, q, bt(b)], w2m[:, q, :],
                                          start=(b == 0 and q == 0), stop=(q == MQ - 1), skip_group_check=True)
                    if s == 5:
                        m.then_inc(S["mlp_ps"], 1)
                if s == 9:
                    ring_free("n4T", n)
                    pe.wait_ge(S["n4_ready"], n + 1)
                    transposes("n4T", nrm4).then_inc(S["n4T_ps"], 1)
                if s == 10:
                    ring_free("logit", n)
                    pe.wait_ge(S["w_ready"], n + 1)
                    for b in range(B):
                        m = pe.matmul(slot("logit")[:, b * E:(b + 1) * E], w[:, bt(b)], wg[:, :], start=(b == 0), stop=True,
                                      skip_group_check=True)
                    m.then_inc(S["logit_ps"], 1)
                if s == 15:
                    ring_free("combT", n)
                    pe.wait_ge(S["comb_ready"], n + 1)
                    for b in range(B):
                        m = pe.transpose(slot("combT")[0:E, bt(b)], comb[:, b, :], ident[:, :])
                    m.then_inc(S["combT_ps"], 1)

            def stage_M(n, s):
                if s == 1:
                    reader = ring_reader("btm", n)
                    wait_before(pe, (S["bc_silu"], n + 1), *([reader] if reader else []))
                    for b in range(B):
                        m = pe.transpose(slot("btm")[:, b * NS:(b + 1) * NS], Bc[:, bt(b)], ident[0:NS, 0:NS])
                    m.then_inc(S["btm_ps"], 1)
                    ring_free("g", n)
                    for b in range(B):
                        m = pe.matmul(slot("g")[:, bt(b)], Bc[:, bt(b)], Cc[:, bt(b)], start=(b == 0), stop=True,
                                      skip_group_check=True)
                    m.then_inc(S["g_ps"], 1)
                    pe.wait_ge(S["a_ready"], n + 1)
                    ring_free("cum", n)
                    av = a[:, :, :].rearrange("p b h -> p (b h)")
                    for k, mask in enumerate((upto, after, ones)):
                        m = pe.matmul(slot("cum")[:, k * B * NH:(k + 1) * B * NH], mask[:, :], av, start=(k == 0),
                                      stop=True, skip_group_check=True)
                    m.then_inc(S["cum_ps"], 1)
                if s in (2, 5):
                    pair = s // 3
                    for q in range(2):
                        b = 2 * pair + q
                        ring_free(f"seg{b}", n)
                        pe.wait_ge(S["m1a_ready"], 4 * n + b + 1)
                        pe.matmul(slot(f"seg{b}")[:, :], after[:, :],
                                  m1a[:, q, :, :].rearrange("p h t -> p (h t)"), start=True, stop=True).then_inc(S["seg_ps"], 1)
                if s in (3, 6):
                    pair = s // 4
                    inter = slot(f"int{pair}")
                    ring_free(f"int{pair}", n)
                    pe.wait_ge(S["H_ready"], 2 * n)
                    for q in range(2):
                        b = 2 * pair + q
                        m = pe.matmul(inter[:, q * DI:(q + 1) * DI], Cc[:, bt(b)], H[:, b, :], start=(q == 0), stop=True,
                                      skip_group_check=True)
                    m.then_inc(S["int_ps"], 1)
                if s in (4, 7):
                    pair = s // 5
                    intra = slot(f"intra{pair}")
                    ring_free(f"intra{pair}", n)
                    for q in range(2):
                        b = 2 * pair + q
                        for j in range(DI // P):
                            pe.matmul(intra[:, q * DI + j * P:q * DI + (j + 1) * P], xs[:, j, bt(b)], Ddiag[:, j, :],
                                      start=(q == 0 and j == 0), stop=False, skip_group_check=True)
                        pe.wait_ge(S["W_ready"], 4 * n + b + 1)
                        pe.wait_ge(S["xdt_ready"], 2 * n + pair + 1)
                        for hh in range(NH):
                            m = pe.matmul(intra[:, q * DI + hh * HD:q * DI + (hh + 1) * HD], Wt[:, q, hh, :],
                                          xdt[:, b, hh * HD:(hh + 1) * HD], start=False, stop=True,
                                          skip_group_check=True)
                    m.then_inc(S["yi_ps"], 1)
                if s == 9:
                    pe.wait_ge(S["btm_ready"], n + 1)
                    for pair in range(2):
                        ring_free(f"st{pair}", n)
                        pe.wait_ge(S["xde_ready"], 2 * n + pair + 1)
                        for q in range(2):
                            b = 2 * pair + q
                            m = pe.matmul(slot(f"st{pair}")[0:NS, q * DI:(q + 1) * DI], Btm[:, b, :], xde[:, b, :],
                                          start=(q == 0), stop=True, skip_group_check=True)
                        m.then_inc(S["st_ps"], 1)
                if s == 10:
                    pe.wait_ge(S["yz_ready"], 2 * n + 2)
                    for j in range(DI // P):
                        ring_free(f"yzT{j}", n)
                        for b in range(B):
                            m = pe.transpose(slot(f"yzT{j}")[:, bt(b)], yz[:, b, j * P:(j + 1) * P], ident[:, :])
                        m.then_inc(S["yzT_ps"], 1)
                if s == 11:
                    ring_free("op", n)
                    pe.wait_ge(S["yzT_ready"], 2 * n + 2)
                    for b in range(B):
                        for j in range(DI // P):
                            m = pe.matmul(slot("op")[:, bt(b)], yzT[:, j, bt(b)], wout[:, j, :],
                                          start=(b == 0 and j == 0), stop=(j == 1), skip_group_check=True)
                    m.then_inc(S["op_ps"], 1)
                if s == 15:
                    ring_free("n2T", n)
                    pe.wait_ge(S["n2_ready"], n + 1)
                    transposes("n2T", x2).then_inc(S["n2T_ps"], 1)

            def stage_A(n, s):
                if s == 2:
                    ring_free("n1T", n)
                    pe.wait_ge(S["n1_ready"], n + 1)
                    transposes("n1T", nrm).then_inc(S["n1T_ps"], 1)
                if s == 3:
                    ring_free("dt", n)
                    pe.wait_ge(S["u_ready"], n + 1)
                    for b in range(B):
                        m = pe.matmul(slot("dt")[:, b * NH:(b + 1) * NH], u[:, bt(b)], wdt[:, :],
                                      start=(b == 0), stop=True, skip_group_check=True)
                    m.then_inc(S["dt_ps"], 1)
                if s in (4, 6, 7):
                    if s == 4:
                        pe.wait_ge(S["uhi_ready"], n + 1)
                        pe.wait_ge(S["ulo_ready"], n + 1)
                    j = (4, 6, 7).index(s)
                    ring_free(f"xbc{j}", n)
                    cols = slice(DI + j * P, DI + (j + 1) * P)
                    split3(slot(f"xbc{j}")[:, :], wp_hi[:, cols], wp_lo[:, cols], u_hi[:, :], u_lo[:, :])\
                        .then_inc(S["xbc_ps"], 1)
                if s in (12, 13):
                    pair = s - 12
                    ring_free(f"z{pair}", n)
                    for q in range(2):
                        m = split3(slot(f"z{pair}")[:, q * DI:(q + 1) * DI], u_hi[:, bt(2 * pair + q)],
                                   u_lo[:, bt(2 * pair + q)], wp_hi[:, 0:DI], wp_lo[:, 0:DI], start=(q == 0))
                    m.then_inc(S["z_ps"], 1)
                if s in (14.5, 16):
                    pair = 0 if s == 14.5 else 1
                    pe.wait_ge(S["xs_silu"], n + 1)
                    ring_free(f"xtm{pair}", n)
                    for q in range(2):
                        for j in range(DI // P):
                            m = pe.transpose(slot(f"xtm{pair}")[:, q * DI + j * P:q * DI + (j + 1) * P],
                                             xs[:, j, bt(2 * pair + q)], ident[:, :])
                    m.then_inc(S["xtm_ps"], 1)

            def expert_weight(n, e):
                if e == 0:
                    pe.wait_ge(S["combT_hi"], n + 1)
                    pe.wait_ge(S["combT_lo"], n + 1)
                pe.wait_ge(S["combB_ready"], E * n + e)
                pe.matmul(cbps[:, :], pick_r[:, e, :], combT[:, :], start=True, stop=True).then_inc(S["combB_ps"], 1)

            def expert_unit(n, un):
                e, k = divmod(un, HK)
                if un == 0:
                    pe.wait_ge(S["whi_ready"], n + 1)
                    pe.wait_ge(S["wlo_ready"], n + 1)
                pe.wait_ge(S["tanh_ready"], NU * n + max(un - 1, 0))
                pe.wait_ge(S["aw_ready"], NU * n + max(un - 1, 0))
                if un == 0:
                    expert_weight(n, 0)
                for half in range(2):
                    c0 = e * 2 * H2 + half * H2 + k * P
                    m = split3(ab[2 * (un % 2) + half][:, :], wexp_hi[:, c0:c0 + P], wexp_lo[:, c0:c0 + P],
                               w_hi[:, :], w_lo[:, :])
                m.then_inc(S["ab_ps"], 1)
                if k == 1 and e + 1 < E:
                    expert_weight(n, e + 1)

            def expert_out(n):
                pe.wait_ge(S["acc_added"], (NU - HK) * n + NU - HK)
                ring_free("out", n)
                for b in range(B):
                    for k in range(HK):
                        m = pe.matmul(slot("out")[:, bt(b)], acc[:, k, bt(b)], wo[:, k, :], start=(b == 0 and k == 0),
                                      stop=(k == 1), skip_group_check=True)
                m.then_inc(S["wo_ps"], 1)

            def body(t, live):
                for s in range(NU + 1):
                    if "E" in live and s < NU:
                        expert_unit(t, s)
                    if "C" in live:
                        stage_C(t + 1, s)
                    if "M" in live:
                        stage_M(t + 2, s)
                    if "A" in live:
                        stage_A(t + 3, s)
                    if "C" in live:
                        stage_C(t + 1, s + 0.5)
                    if "A" in live:
                        stage_A(t + 3, s + 0.5)
                    if "O" in live and s == 0:
                        expert_out(t - 1)
                if "S" in live:
                    pe.wait_ge(S["loads_late"], 16 * N_LATE)
                    pe.wait_ge(S["late_scalar"], 1)
                    pe.wait_ge(S["late_vector"], 1)

            setup()
            run_bodies(pe, body)

        @block.scalar
        def _(act):
            f = act.activation

            def setup():
                act.wait_ge(S["loads_mod"], 16 * N_MOD)
                f(silu_c[:, :], cT[:, :], ACT.Silu).then_inc(S["silu_c_ready"], 1)
                act.wait_ge(S["loads_front"], 16 * N_FRONT)
                f(wp_hi[:, :], wp[:, 0:ZX], ACT.Copy).then_inc(S["split_hi"], 1)
                f(A_neg[:, :], A_row[:, :], ACT.Exp).then_inc(S["A_exp"], 1)
                act.wait_ge(S["gpsimd_ready"], 1)
                act.wait_ge(S["vector_ready"], 1)

            def setup_late(s):
                if s == 0:
                    act.wait_ge(S["loads_late"], 16 * N_LATE)
                    f(w1m_hi[:, :], w1m[:, :], ACT.Copy).then_inc(S["late_hi"], 1)
                if 1 <= s <= 8:
                    piece = slice((s - 1) * W4, s * W4)
                    f(wexp_hi[:, piece], wexp[:, piece], ACT.Copy).then_inc(S["late_hi"], 1)
                if s == 9:
                    act.wait_ge(S["late_hi"], 9)
                    f(b1e_half[:, :, :], b1e[:, :, :], ACT.Copy, scale=0.5).then_inc(S["late_scalar"], 1)
                    act.wait_ge(S["late_scalar"], 1)

            def gelu(q, n):
                act.wait_ge(S["hid_ps"], 4 * n + q + 1)
                if q == 0:
                    act.wait_ge(S["mlp_ps"], n)
                f(gl[:, q, :], slot(f"hid{q}")[:, :], ACT.Gelu, bias=b1m[:, q:q + 1]).then_inc(S["gelu_ready"], 1)

            def norm(dst, src, r, which):
                for b in range(B):
                    m = f(dst[:, b, :], src[:, b, :], ACT.Identity, bias=shift[:, which, b:b + 1], scale=r[:, b:b + 1])
                return m

            def stage_C(n, s):
                if s == 8:
                    act.wait_ge(S["x4_rstd"], 2 * n + 2)
                    act.wait_ge(S["n4T_ps"], n)
                    norm(nrm4, x4, r4, 3).then_inc(S["n4_ready"], 1)
                if s in (0, 1):
                    gelu(2 * s, n)
                    gelu(2 * s + 1, n)
                if s == 9:
                    act.wait_ge(S["n4T_ps"], n + 1)
                    act.wait_ge(S["wlo_ready"], n)
                    act.wait_ge(S["logit_ps"], n)
                    for b in range(B):
                        m = f(w[:, bt(b)], slot("n4T")[:, bt(b)], ACT.Identity, bias=sbT[:, b:b + 1], scale=cb1T[:, b:b + 1])
                    m.then_inc(S["w_ready"], 1)
                if s == 11:
                    act.wait_ge(S["gate_chain"], GATE_STEPS * n + GATE_EXP)
                    f(ex[:, :, :], exs[:, :, :], ACT.Exp).then_inc(S["ex_ready"], 1)
                if s == 15:
                    act.wait_ge(S["w_ready"], n + 1)
                    act.wait_ge(S["ab_ps"], NU * n)
                    f(w_hi[:, :], w[:, :], ACT.Copy).then_inc(S["whi_ready"], 1)
                    act.wait_ge(S["combT_ps"], n + 1)
                    act.wait_ge(S["combB_ps"], E * n)
                    f(combT[0:E, :], slot("combT")[0:E, :], ACT.Copy).then_inc(S["combT_hi"], 1)

            def stage_M(n, s):
                if s == 1:
                    act.wait_ge(S["btm_ps"], n + 1)
                    act.wait_ge(S["st_ps"], 2 * n)
                    f(Btm[:, :, :], slot("btm")[:, 0:B * NS].rearrange("p (b s) -> p b s", b=B), ACT.Copy)\
                        .then_inc(S["btm_ready"], 1)
                    act.wait_ge(S["cum_ps"], n + 1)
                    act.wait_ge(S["yt_ready"], 2 * n)
                    act.wait_ge(S["xde_ready"], 2 * n)
                    act.wait_ge(S["Hd_ready"], 2 * n)
                    f(ecs[:, :, :, :].rearrange("p k b h -> p (k b h)"), slot("cum")[:, 0:3 * B * NH], ACT.Exp)\
                        .then_inc(S["ecs_ready"], 1)
                if s == 2:
                    act.wait_ge(S["h_kept"], n + 1)
                    act.wait_ge(S["n2T_ps"], n)
                    f(x2[:, :, :], hk[:, :, :], ACT.Copy).then_inc(S["x2_seeded"], 1)
                if s in (2, 5):
                    pair = s // 3
                    for q in range(2):
                        b = 2 * pair + q
                        act.wait_ge(S["seg_ps"], 4 * n + b + 1)
                        act.wait_ge(S["W_ready"], 4 * n + max(b - 1, 0))
                        f(L[:, q, :, :].rearrange("p h t -> p (h t)"), slot(f"seg{b}")[:, :], ACT.Exp)\
                            .then_inc(S["L_ready"], 1)
                if s == 9:
                    act.wait_ge(S["yz_ready"], 2 * n + 2)
                    for b in range(B):
                        m = f(yt[:, b, :], yz[:, b, :], ACT.Square, accum_out=ssq[:, b:b + 1])
                    m.then_inc(S["ssq_ready"], 1)
                if s == 10:
                    act.wait_ge(S["op_ps"], n)
                    for j in range(DI // P):
                        act.wait_ge(S["yzT_ps"], 2 * n + j + 1)
                        f(yzT[:, j, :], slot(f"yzT{j}")[:, :], ACT.Copy).then_inc(S["yzT_ready"], 1)
                if s == 14:
                    act.wait_ge(S["x2_rstd"], 2 * n + 2)
                    act.wait_ge(S["x2b_ready"], n + 1)
                    norm(x2, x2, r2, 2).then_inc(S["n2_ready"], 1)
                if s == 16:
                    act.wait_ge(S["n2T_ps"], n + 1)
                    act.wait_ge(S["vlo_ready"], n)
                    f(v[:, :], slot("n2T")[:, :], ACT.Identity, bias=ln2b[:, 0:1], scale=ln2w[:, 0:1]).then_inc(S["v_ready"], 1)
                    act.wait_ge(S["v_ready"], n + 1)
                    act.wait_ge(S["hid_ps"], 4 * n)
                    f(v_hi[:, :], v[:, :], ACT.Copy).then_inc(S["vhi_ready"], 1)

            def stage_A(n, s):
                if s == 1:
                    act.wait_ge(S["h_rstd"], 2 * n + 2)
                    act.wait_ge(S["n1T_ps"], n)
                    norm(nrm, h, rh, 1).then_inc(S["n1_ready"], 1)
                if s == 2:
                    act.wait_ge(S["n1T_ps"], n + 1)
                    act.wait_ge(S["ulo_ready"], n)
                    act.wait_ge(S["dt_ps"], n)
                    f(u[:, :], slot("n1T")[:, :], ACT.Identity, bias=ln1b[:, 0:1], scale=ln1w[:, 0:1]).then_inc(S["u_ready"], 1)
                    act.wait_ge(S["u_ready"], n + 1)
                    act.wait_ge(S["z_ps"], 2 * n)
                    f(u_hi[:, :], u[:, :], ACT.Copy).then_inc(S["uhi_ready"], 1)
                if s in (4, 6, 7):
                    j = (4, 6, 7).index(s)
                    if s == 4:
                        act.wait_ge(S["halo_saved"], n)
                    act.wait_ge(S["xbc_ps"], CB * n + j + 1)
                    src = slot(f"xbc{j}")[:, :].rearrange("p (b t) -> p b t", b=B)
                    f(xbc[:, j, :, HALO:HALO + P], src, ACT.Copy)
                    f(cv[:, j, :, :], src, ACT.Identity, bias=convb[:, j:j + 1], scale=convw[:, j, HALO:HALO + 1])\
                        .then_inc(S["xbc_read"], 1)
                if s == 3:
                    act.wait_ge(S["dt_chain"], DT_STEPS * n + 2)
                    f(ew[:, :, :], nab[:, :, :], ACT.Exp).then_inc(S["dt_exp"], 1)
                if s == 3:
                    act.wait_ge(S["h_ready"], n + 1)
                    act.wait_ge(S["x2_seeded"], n)
                    f(hk[:, :, :], h[:, :, :], ACT.Copy).then_inc(S["h_kept"], 1)
                if s == 12:
                    act.wait_ge(S["yi_ps"], 2 * n)
                    for j in range(CB - 1):
                        act.wait_ge(S["conv_tap"], CB * HALO * n + HALO * (j + 1))
                        m = f(xs[:, j, :].rearrange("p (b t) -> p b t", b=B), cv[:, j, :, :], ACT.Silu)
                    m.then_inc(S["xs_silu"], 1)
                if s in (12, 13):
                    pair = s - 12
                    act.wait_ge(S["z_ps"], 2 * n + pair + 1)
                    act.wait_ge(S["yz_ready"], 2 * n)
                    f(sz[:, 2 * pair:2 * pair + 2, :], slot(f"z{pair}")[:, :].rearrange("p (b c) -> p b c", b=2),
                      ACT.Silu).then_inc(S["z_silu"], 1)
                if s == 14:
                    act.wait_ge(S["conv_tap"], CB * HALO * (n + 1))
                    f(tok4(Bc), cv[0:NS, CB - 1, :, :], ACT.Silu)
                    f(tok4(Cc), cv[NS:2 * NS, CB - 1, :, :], ACT.Silu).then_inc(S["bc_silu"], 1)

            def stage_X(n, s):
                if s == 5:
                    act.wait_ge(S["xa_rstd"], 2 * n + 2)
                    act.wait_ge(S["h_kept"], n)
                    act.wait_ge(S["n1_ready"], n)
                    norm(h, xt, ra, 0).then_inc(S["xa_norm"], 1)

            def expert_weight(n, e):
                act.wait_ge(S["combB_ps"], E * n + e + 1)
                act.wait_ge(S["aw_ready"], NU * n + HK * max(e - 1, 0))
                f(combB[:, e % 2, :], cbps[:, :], ACT.Copy).then_inc(S["combB_ready"], 1)

            def expert_unit(n, un):
                e, k = divmod(un, HK)
                if un == 3:
                    act.wait_ge(S["x4_ready"], n + 1)
                    act.wait_ge(S["comb_ready"], n + 1)
                    act.wait_ge(S["o_ready"], n)
                    act.wait_ge(S["o_bias"], n)
                    f(x4k[:, :, :], x4[:, :, :], ACT.Copy)
                    f(csumk[:, :], csum[:, :], ACT.Copy).then_inc(S["kept"], 1)
                if un == 0:
                    expert_weight(n, 0)
                act.wait_ge(S["ab_ps"], NU * n + un + 1)
                act.wait_ge(S["g_ready"], NU * n + max(un - 1, 0))
                f(tg[:, un % 2, :], ab[2 * (un % 2) + 1][:, :], ACT.Tanh, bias=b1e_half[:, e, HK + k:HK + k + 1], scale=0.5)\
                    .then_inc(S["tanh_ready"], 1)
                if k == 1 and e + 1 < E:
                    expert_weight(n, e + 1)

            def body(t, live):
                for s in range(NU + 1):
                    if "E" in live and s < NU:
                        expert_unit(t, s)
                    if "C" in live:
                        stage_C(t + 1, s)
                    if "M" in live:
                        stage_M(t + 2, s)
                    if "A" in live:
                        stage_A(t + 3, s)
                    if "X" in live:
                        stage_X(t + 4, s)
                    if "S" in live:
                        setup_late(s)

            setup()
            run_bodies(act, body)

        @block.vector
        def _(dve):
            tt, ts, stt = dve.tensor_tensor, dve.tensor_scalar, dve.scalar_tensor_tensor

            def setup():
                dve.memset(xbc[:, :, :, 0:HALO], 0.0)
                dve.memset(H[:, :, :], 0.0)
                dve.memset(top[:, :, :], PAD)
                dve.memset(lg[:, :, :], PAD)
                dve.memset(minus_half[:, :], -0.5)
                dve.wait_ge(S["silu_c_ready"], 1)
                dve.tensor_copy(silu_row[:, :, :], bcast(silu_c[:, :], 2, [P, B, P])).then_inc(S["silu_rows_ready"], 1)
                for b in range(B):
                    dve.wait_ge(S["mod_ps"], 2 * b + 1)
                    dve.tensor_copy(sa[:, b, :], ring[2 * b % 3][:, 0:D])
                    ts(ca1[:, b, :], ring[2 * b % 3][:, D:2 * D], 1.0, None, ALU.add)
                    dve.tensor_copy(ga[:, b, :], ring[2 * b % 3][:, 2 * D:3 * D]).then_inc(S["mod_read"], 1)
                    dve.wait_ge(S["mod_ps"], 2 * b + 2)
                    dve.tensor_copy(gb[:, b, :], ring[(2 * b + 1) % 3][:, 0:D]).then_inc(S["mod_read"], 1)
                dve.wait_ge(S["mod_ps"], 2 * B + 1)
                dve.tensor_copy(sbT[:, :], ring[2 * B % 3][:, 0:B])
                ts(cb1T[:, :], ring[2 * B % 3][:, B:2 * B], 1.0, None, ALU.add).then_inc(S["mod_read"], 1)
                dve.wait_ge(S["loads_front"], 16 * N_FRONT)
                dve.wait_ge(S["split_hi"], 1)
                tt(wp_lo[:, :], wp[:, 0:ZX], wp_hi[:, :].bitcast(F32), ALU.subtract)
                dve.wait_ge(S["A_exp"], 1)
                ts(A_neg[:, :], A_neg[:, :], -1.0, None, ALU.mult).then_inc(S["vector_ready"], 1)
                dve.wait_ge(S["vector_ready"], 1)
                dve.wait_ge(S["gpsimd_ready"], 1)

            def gain(g, k, at):
                if at:
                    dve.wait_ge(S["setup_chain"], at)
                if k == 0:
                    m = ts(gsign[:, :, :], g[:, :, :], 0.0, 2.0, ALU.is_ge, ALU.mult)
                if k == 1:
                    m = stt(g[:, :, :], g[:, :, :], -1.0, g[:, :, :], ALU.mult, ALU.max)
                if k == 2:
                    m = ts(gsign[:, :, :], gsign[:, :, :], -1.0, None, ALU.add)
                if k == 3:
                    m = stt(g[:, :, :], g[:, :, :], 0.25, gsign[:, :, :], ALU.max, ALU.mult)
                m.then_inc(S["setup_chain"], 1)

            def setup_late(s):
                if s == 0:
                    dve.wait_ge(S["loads_late"], 16 * N_LATE)
                    dve.tensor_copy(pick_r[:, :, :], pick[:, :, :])
                    ts(combT[:, :], wexp[0:64, 0:W4], 0.0, None, ALU.mult)
                if s == 2:
                    dve.wait_ge(S["late_hi"], 1)
                    tt(w1m_lo[:, :], w1m[:, :], w1m_hi[:, :].bitcast(F32), ALU.subtract)
                if 3 <= s <= 10:
                    gain(ga if s < 7 else gb, (s - 3) % 4, s - 3)
                    piece = slice((s - 3) * W4, (s - 2) * W4)
                    dve.wait_ge(S["late_hi"], s - 1)
                    tt(wexp_lo[:, piece], wexp[:, piece], wexp_hi[:, piece].bitcast(F32), ALU.subtract)
                if s == 11:
                    dve.wait_ge(S["setup_chain"], 8)
                    for j in range(DI // P):
                        ts(Ddiag[:, j, :], ident[:, :], Dcol[:, j:j + 1], None, ALU.mult)
                        m = ts(wout[:, j, :], wout[:, j, :], normw[:, j:j + 1], None, ALU.mult)
                    m.then_inc(S["late_vector"], 1)
                    dve.wait_ge(S["late_vector"], 1)

            def ln_stats(src, which, mv, n, stats_done, mv_done):
                for b in range(B):
                    m = dve.bn_stats(stats[:, which, b, :], src[:, b, :])
                m.then_inc(stats_done, 1)
                wait_before(dve, (stats_done, n + 1))
                for b in range(B):
                    m = dve.bn_aggr(mv[:, b, :], stats[:, which, b, :])
                m.then_inc(mv_done, 1)

            def softplus(n, k):
                if k == 0:
                    dve.wait_ge(S["dt_exp"], n + 1)
                    m = ts(den[:, :, :], ew[:, :, :], 2.0, None, ALU.add)
                else:
                    dve.wait_ge(S["dt_chain"], DT_STEPS * n + 2 + k)
                if k == 1:
                    m = dve.reciprocal(rden[:, :, :], den[:, :, :])
                if k == 2:
                    m = tt(sw[:, :, :], ew[:, :, :], rden[:, :, :], ALU.mult)
                if k == 3:
                    m = tt(s2[:, :, :], sw[:, :, :], sw[:, :, :], ALU.mult)
                if k == 4:
                    m = ts(pl[:, :, :], s2[:, :, :], 2.0 / ATANH[0], None, ALU.mult)
                if 5 <= k < SP_OPS - 3:
                    m = stt(pl[:, :, :], pl[:, :, :], 2.0 / ATANH[k - 4], s2[:, :, :], ALU.add, ALU.mult)
                if k == SP_OPS - 3:
                    m = stt(pl[:, :, :], pl[:, :, :], 2.0, sw[:, :, :], ALU.add, ALU.mult)
                if k == SP_OPS - 2:
                    dve.wait_ge(S["xdt_ready"], 2 * n)
                    m = tt(dt[:, :, :], pl[:, :, :], relu[:, :, :], ALU.add)
                if k == SP_OPS - 1:
                    dve.wait_ge(S["m1a_ready"], 4 * n)
                    dve.wait_ge(S["cum_ps"], n)
                    tt(a[:, :, :], dt[:, :, :], bcast(A_neg[:, :], 1, [P, B, NH]), ALU.mult).then_inc(S["a_ready"], 1)
                else:
                    m.then_inc(S["dt_chain"], 1)

            def conv_taps(n, first, last):
                for i in range(first, last):
                    j, k = divmod(i, HALO)
                    dve.wait_ge(S["xbc_read"], CB * n + j + 1)
                    if k > 0:
                        dve.wait_ge(S["conv_tap"], CB * HALO * n + i)
                    stt(cv[:, j, :, :], xbc[:, j, :, k:k + P], convw[:, j, k:k + 1], cv[:, j, :, :],
                        ALU.mult, ALU.add).then_inc(S["conv_tap"], 1)

            def gate_choice(n):
                base = GATE_STEPS * n
                wait_before(dve, (S["logit_ready"], n + 1))
                for b in range(B):
                    m = dve.max(mx[:, b, :], lg[:, b, 0:E])
                m.then_inc(S["gate_chain"], 1)
                dve.wait_ge(S["gate_chain"], base + 1)
                dve.tensor_copy(top[:, :, 0:2], mx[:, :, 0:2]).then_inc(S["gate_chain"], 1)
                tt(exs[:, :, :], lg[:, :, 0:E], mx[:, :, 0:1].to_broadcast([P, B, E]), ALU.subtract).then_inc(S["gate_chain"], 1)
                wait_before(dve, (S["gate_chain"], base + 3))
                for b in range(B):
                    m = dve.match_replace(rep[:, b, :], top[:, b, :], lg[:, b, :], TAKEN)
                m.then_inc(S["gate_chain"], 1)

            def gate_weights(n):
                base = GATE_STEPS * n
                dve.wait_ge(S["ex_ready"], n + 1)
                dve.wait_ge(S["gate_chain"], base + 4)
                dve.tensor_reduce(Z[:, :], ex[:, :, :], AX.X, ALU.add).then_inc(S["gate_chain"], 1)
                dve.wait_ge(S["gate_chain"], base + 5)
                stt(sel[:, :, :], rep[:, :, 0:E], TAKEN / 2, ex[:, :, :], ALU.is_gt, ALU.mult).then_inc(S["gate_chain"], 1)
                dve.wait_ge(S["gate_chain"], base + 6)
                dve.tensor_reduce(dsum[:, :], sel[:, :, :], AX.X, ALU.add).then_inc(S["gate_chain"], 1)
                dve.wait_ge(S["gate_chain"], base + 7)
                stt(deps[:, :], Z[:, :], TOPK_EPS, dsum[:, :], ALU.mult, ALU.add).then_inc(S["gate_chain"], 1)
                dve.wait_ge(S["gate_chain"], base + 8)
                dve.reciprocal(rinv[:, :], deps[:, :]).then_inc(S["gate_chain"], 1)
                dve.wait_ge(S["gate_chain"], base + 9)
                dve.wait_ge(S["kept"], n)
                dve.wait_ge(S["combT_ps"], n)
                tt(csum[:, :], dsum[:, :], rinv[:, :], ALU.mult)
                stt(comb[:, :, :], sel[:, :, :], 0.5, bcast(rinv[:, :], 2, [P, B, E]), ALU.mult, ALU.mult)\
                    .then_inc(S["comb_ready"], 1)

            def stage_C(n, s):
                if s == 6:
                    dve.wait_ge(S["mlp_ps"], n + 1)
                    dve.wait_ge(S["x2b_ready"], n + 1)
                    tt(x3[:, :, :], tok4(slot("mlp")), x2b[:, :, :], ALU.add).then_inc(S["x3_ready"], 1)
                if s == 7.5:
                    dve.wait_ge(S["x4_ready"], n + 1)
                    ln_stats(x4, 3, mv4, n, S["x4_stats"], S["x4_mv"])
                if s == 11:
                    dve.wait_ge(S["logit_ps"], n + 1)
                    dve.tensor_copy(lg[:, :, 0:E], slot("logit")[:, 0:B * E].rearrange("p (b e) -> p b e", b=B))\
                        .then_inc(S["logit_ready"], 1)
                    gate_choice(n)
                if s == 12.5:
                    gate_weights(n)
                if s == 15.5:
                    dve.wait_ge(S["whi_ready"], n + 1)
                    dve.wait_ge(S["ab_ps"], NU * n)
                    tt(w_lo[:, :], w[:, :], w_hi[:, :].bitcast(F32), ALU.subtract).then_inc(S["wlo_ready"], 1)
                    dve.wait_ge(S["combT_hi"], n + 1)
                    dve.wait_ge(S["combB_ps"], E * n)
                    tt(combT[32:32 + E, :], slot("combT")[0:E, :], combT[0:E, :].bitcast(F32), ALU.subtract)\
                        .then_inc(S["combT_lo"], 1)

            def stage_M(n, s):
                if s == 2:
                    dve.wait_ge(S["g_ps"], n + 1)
                    tt(gm[:, :, :], tok4(slot("g")), bcast(upto[:, :], 1, [P, B, P]), ALU.mult).then_inc(S["gm_ready"], 1)
                if s in (3, 6):
                    pair = s // 4
                    dve.wait_ge(S["gm_ready"], n + 1)
                    dve.wait_ge(S["yi_ps"], 2 * n + pair)
                    for q in range(2):
                        b = 2 * pair + q
                        dve.wait_ge(S["L_ready"], 4 * n + b + 1)
                        tt(Wt[:, q, :, :], L[:, q, :, :], bcast(gm[:, b, :], 1, [P, NH, P]), ALU.mult).then_inc(S["W_ready"], 1)
                if s in (4, 7):
                    pair = s // 5
                    bb = slice(2 * pair, 2 * pair + 2)
                    dve.wait_ge(S["int_ps"], 2 * n + pair + 1)
                    dve.wait_ge(S["ecs_ready"], n + 1)
                    dve.wait_ge(S["ssq_ready"], n)
                    tt(heads(yt[:, bb, :]), heads(slot(f"int{pair}")[:, :].rearrange("p (b c) -> p b c", b=2)),
                       over_q(ecs[:, 0, bb, :]), ALU.mult).then_inc(S["yt_ready"], 1)
                if s in (5, 8):
                    pair = s // 6
                    bb = slice(2 * pair, 2 * pair + 2)
                    dve.wait_ge(S["yt_ready"], 2 * n + pair + 1)
                    dve.wait_ge(S["yi_ps"], 2 * n + pair + 1)
                    tt(yt[:, bb, :], slot(f"intra{pair}")[:, :].rearrange("p (b c) -> p b c", b=2), yt[:, bb, :], ALU.add)\
                        .then_inc(S["yi_read"], 1)
                    dve.wait_ge(S["yi_read"], 2 * n + pair + 1)
                    dve.wait_ge(S["z_silu"], 2 * n + pair + 1)
                    dve.wait_ge(S["yzT_ps"], 2 * n)
                    tt(yz[:, bb, :], yt[:, bb, :], sz[:, bb, :], ALU.mult).then_inc(S["yz_ready"], 1)
                if s == 10:
                    dve.wait_ge(S["int_ps"], 2 * n + 2)
                    for pair in range(2):
                        bb = slice(2 * pair, 2 * pair + 2)
                        dve.wait_ge(S["st_ps"], 2 * n + pair + 1)
                        dve.wait_ge(S["Hd_ready"], 2 * n + pair + 1)
                        tt(H[:, bb, :], slot(f"st{pair}")[0:NS, :].rearrange("p (b c) -> p b c", b=2), Hd[:, bb, :], ALU.add)\
                            .then_inc(S["H_ready"], 1)
                if s == 11.5:
                    dve.wait_ge(S["op_ps"], n + 1)
                    dve.wait_ge(S["y_rstd"], n + 1)
                    dve.wait_ge(S["x2_seeded"], n + 1)
                    for b in range(B):
                        m = stt(x2[:, b, :], slot("op")[:, bt(b)], ry[:, b:b + 1], x2[:, b, :], ALU.mult, ALU.add)
                    m.then_inc(S["x2_ready"], 1)
                if s == 13:
                    dve.wait_ge(S["x2_ready"], n + 1)
                    ln_stats(x2, 2, mv2, n, S["x2_stats"], S["x2_mv"])
                if s == 16:
                    dve.wait_ge(S["vhi_ready"], n + 1)
                    dve.wait_ge(S["hid_ps"], 4 * n)
                    tt(v_lo[:, :], v[:, :], v_hi[:, :].bitcast(F32), ALU.subtract).then_inc(S["vlo_ready"], 1)

            def stage_A(n, s):
                if s == 3.5:
                    dve.wait_ge(S["uhi_ready"], n + 1)
                    dve.wait_ge(S["z_ps"], 2 * n)
                    tt(u_lo[:, :], u[:, :], u_hi[:, :].bitcast(F32), ALU.subtract).then_inc(S["ulo_ready"], 1)
                if s == 4:
                    dve.wait_ge(S["dt_ps"], n + 1)
                    tt(dtv[:, :, :], slot("dt")[:, 0:B * NH].rearrange("p (b h) -> p b h", b=B),
                       bcast(dtb[:, :], 1, [P, B, NH]), ALU.add).then_inc(S["dt_chain"], 1)
                    dve.wait_ge(S["dt_chain"], DT_STEPS * n + 1)
                    ts(relu[:, :, :], dtv[:, :, :], 0.0, None, ALU.max)
                    stt(nab[:, :, :], dtv[:, :, :], -1.0, dtv[:, :, :], ALU.mult, ALU.min).then_inc(S["dt_chain"], 1)
                if s >= 5.5 and int(2 * s - 11) < SP_OPS:
                    softplus(n, int(2 * s - 11))
                taps = {5: (0, 1), 6.5: (1, 2), 7: (2, 3), 8: (3, 4), 9: (4, 5), 9.5: (5, 6), 10.5: (6, 7),
                        11.5: (7, 8), 13.5: (8, 9)}
                if s in taps:
                    conv_taps(n, *taps[s])
                if s in (15, 16):
                    pair = s - 15
                    bb = slice(2 * pair, 2 * pair + 2)
                    dve.wait_ge(S["yi_ps"], 2 * n)
                    dve.wait_ge(S["xde_ready"], 2 * n)
                    dve.wait_ge(S["xtm_ps"], 2 * n + pair + 1)
                    tt(heads(xdt[:, bb, :]), heads(slot(f"xtm{pair}")[:, :].rearrange("p (b c) -> p b c", b=2)),
                       over_q(dt[:, bb, :]), ALU.mult).then_inc(S["xdt_ready"], 1)

            def stage_X(n, s):
                if s == 1.5:
                    dve.wait_ge(S["x_loaded"], 16 * (n + 1))
                    ln_stats(xt, 0, mva, n, S["xa_stats"], S["xa_mv"])
                if s == 15.5:
                    dve.wait_ge(S["h_ready"], n + 1)
                    ln_stats(h, 1, mvh, n, S["h_stats"], S["h_mv"])

            def expert_unit(n, un):
                e, k = divmod(un, HK)
                dve.wait_ge(S["ab_ps"], NU * n + un + 1)
                dve.wait_ge(S["combB_ready"], E * n + e + 1)
                dve.wait_ge(S["g_ready"], NU * n + max(un - 1, 0))
                stt(aw[:, un % 2, :], ab[2 * (un % 2)][:, :], b1e[:, e, k:k + 1], combB[:, e % 2, :], ALU.add, ALU.mult)\
                    .then_inc(S["aw_ready"], 1)

            def expert_gate(n, un):
                e, k = divmod(un, HK)
                dve.wait_ge(S["aw_ready"], NU * n + un + 1)
                dve.wait_ge(S["tanh_ready"], NU * n + un + 1)
                if e == 0:
                    dve.wait_ge(S["wo_ps"], n)
                    dst = acc[:, k, :]
                else:
                    dve.wait_ge(S["acc_added"], (NU - HK) * n + max(un - 5, 0))
                    dst = gg[:, un % 4, :]
                stt(dst, tg[:, un % 2, :], 1.0, aw[:, un % 2, :], ALU.add, ALU.mult).then_inc(S["g_ready"], 1)

            def expert_out(n):
                dve.wait_ge(S["wo_ps"], n + 1)
                dve.wait_ge(S["kept"], n + 1)
                dve.wait_ge(S["o_free"], 16 * (n + 1))
                for b in range(B):
                    m = stt(o[:, b, :], borow[:, :], csumk[:, b:b + 1], slot("out")[:, bt(b)], ALU.mult, ALU.add)
                m.then_inc(S["o_bias"], 1)

            def stages(t, live, s):
                if "O" in live and s == 1:
                    expert_out(t - 1)
                if "C" in live:
                    stage_C(t + 1, s)
                if "M" in live:
                    stage_M(t + 2, s)
                if "A" in live:
                    stage_A(t + 3, s)
                if "X" in live:
                    stage_X(t + 4, s)

            def body(t, live):
                for s in range(NU + 1):
                    stages(t, live, s)
                    if "E" in live and s < NU:
                        expert_unit(t, s)
                    if "E" in live and s > 0:
                        expert_gate(t, s - 1)
                    stages(t, live, s + 0.5)
                    if "S" in live:
                        setup_late(s)

            setup()
            run_bodies(dve, body)

        @block.gpsimd
        def _(pool):
            tt, ts = pool.tensor_tensor, pool.tensor_scalar

            def setup():
                pool.memset(ones[:, :], 1.0).then_inc(S["masks_filled"], 1)
                pool.memset(ident[:, :], 0.0).then_inc(S["masks_filled"], 1)
                pool.memset(pick[:, :, :], 0.0).then_inc(S["masks_filled"], 1)
                pool.wait_ge(S["masks_filled"], 3)
                pool.affine_select(out=ident[:, :], in_=ident[:, :], pattern=[[-1, P]], compare_op=ALU.not_equal, fill=1.0,
                                   base=0, channel_multiplier=1)
                pool.affine_select(out=upto[:, :], in_=ones[:, :], pattern=[[1, P]], compare_op=ALU.is_ge, fill=0.0,
                                   base=0, channel_multiplier=-1)
                pool.affine_select(out=after[:, :], in_=ones[:, :], pattern=[[-1, P]], compare_op=ALU.is_gt, fill=0.0,
                                   base=0, channel_multiplier=1)
                pool.affine_select(out=pick[:, :, :], in_=pick[:, :, :], pattern=[[-1, E], [0, P]],
                                   compare_op=ALU.not_equal, fill=1.0, base=0, channel_multiplier=1).then_inc(S["masks_made"], 1)
                pool.wait_ge(S["masks_made"], 1)
                pool.affine_select(out=pick[:, :, :], in_=pick[:, :, :], pattern=[[-1, E], [0, P]],
                                   compare_op=ALU.not_equal, fill=1.0, base=-32, channel_multiplier=1)\
                    .then_inc(S["gpsimd_ready"], 1)
                pool.wait_ge(S["gpsimd_ready"], 1)
                pool.wait_ge(S["vector_ready"], 1)

            def rstd(dst, which, var, scale, eps, var_done, rstd_done, n):
                ts(var_e[:, which, :], var, scale, eps, ALU.mult, ALU.add).then_inc(var_done, 1)
                pool.wait_ge(var_done, n + 1)
                tt(dst[:, :], var_e[:, which, :], minus_half[:, :], ALU.pow).then_inc(rstd_done, 1)

            def rstd_shift(dst, which, mv, var_done, rstd_done, n):
                wait_before(pool, (rstd_done, 2 * n))
                ts(nmean[:, which, :], mv[:, :, 0], -1.0, None, ALU.mult)
                ts(var_e[:, which, :], mv[:, :, 1], 1.0, LN_EPS, ALU.mult, ALU.add).then_inc(var_done, 1)
                pool.wait_ge(var_done, n + 1)
                tt(dst[:, :], var_e[:, which, :], minus_half[:, :], ALU.pow).then_inc(rstd_done, 1)
                pool.wait_ge(rstd_done, 2 * n + 1)
                tt(shift[:, which, :], nmean[:, which, :], dst[:, :], ALU.mult).then_inc(rstd_done, 1)

            def stage_C(n, s):
                if s == 6:
                    pool.wait_ge(S["x3_ready"], n + 1)
                    tt(x3[:, :, :], x3[:, :, :], ga[:, :, :], ALU.mult).then_inc(S["x3_scaled"], 1)
                    pool.wait_ge(S["x3_scaled"], n + 1)
                    pool.wait_ge(S["xr_loaded"], 16 * (n + 1))
                    pool.wait_ge(S["kept"], n)
                    pool.wait_ge(S["n4_ready"], n)
                    tt(x4[:, :, :], x3[:, :, :], xr[:, :, :], ALU.add).then_inc(S["x4_ready"], 1)
                if s == 8:
                    wait_before(pool, (S["x4_mv"], n + 1))
                    rstd_shift(r4, 3, mv4, S["x4_var"], S["x4_rstd"], n)

            def stage_M(n, s):
                if s in (0, 3):
                    pair = s // 3
                    pool.wait_ge(S["a_ready"], n + 1)
                    for q in range(2):
                        b = 2 * pair + q
                        pool.wait_ge(S["seg_ps"], 4 * n + max(b - 1, 0))
                        tt(m1a[:, q, :, :], bcast(upto[:, :], 1, [P, NH, P]), bcast(a[:, b, :], 2, [P, NH, P]), ALU.mult)\
                            .then_inc(S["m1a_ready"], 1)
                if s == 4:
                    pool.wait_ge(S["ecs_ready"], n + 1)
                    pool.wait_ge(S["xdt_ready"], 2 * n + 2)
                    pool.wait_ge(S["st_ps"], 2 * n)
                    for pair in range(2):
                        bb = slice(2 * pair, 2 * pair + 2)
                        tt(heads(xde[:, bb, :]), heads(xdt[:, bb, :]), over_q(ecs[:, 1, bb, :]), ALU.mult)\
                            .then_inc(S["xde_ready"], 1)
                if s == 7:
                    pool.wait_ge(S["H_ready"], 2 * n)
                    for pair in range(2):
                        bb = slice(2 * pair, 2 * pair + 2)
                        tt(heads(Hd[:, bb, :]), heads(H[:, bb, :]), over_q(ecs[0:NS, 2, bb, :]), ALU.mult)\
                            .then_inc(S["Hd_ready"], 1)
                if s == 9:
                    wait_before(pool, (S["ssq_ready"], n + 1))
                    rstd(ry, 4, ssq[:, :], 1.0 / DI, LN_EPS, S["y_var"], S["y_rstd"], n)
                if s == 12:
                    pool.wait_ge(S["x4_ready"], n)
                    pool.wait_ge(S["x2_ready"], n + 1)
                    tt(x2b[:, :, :], x2[:, :, :], bcast(b2row[:, :], 1, [P, B, D]), ALU.add).then_inc(S["x2b_ready"], 1)
                if s == 13:
                    wait_before(pool, (S["x2_mv"], n + 1))
                    rstd_shift(r2, 2, mv2, S["x2_var"], S["x2_rstd"], n)

            def stage_A(n, s):
                if s == 15:
                    wait_before(pool, (S["conv_tap"], CB * HALO * (n + 1)))
                    pool.tensor_copy(xbc[:, :, :, 0:HALO], xbc[:, :, :, P:P + HALO]).then_inc(S["halo_saved"], 1)

            def stage_X(n, s):
                if s == 16:
                    wait_before(pool, (S["h_mv"], n + 1))
                    rstd_shift(rh, 1, mvh, S["h_var"], S["h_rstd"], n)
                if s == 4:
                    wait_before(pool, (S["xa_mv"], n + 1))
                    rstd_shift(ra, 0, mva, S["xa_var"], S["xa_rstd"], n)
                if s == 10:
                    pool.wait_ge(S["xa_norm"], n + 1)
                    tt(h[:, :, :], h[:, :, :], ca1[:, :, :], ALU.mult).then_inc(S["xa_scaled"], 1)
                    pool.wait_ge(S["xa_scaled"], n + 1)
                    tt(h[:, :, :], h[:, :, :], sa[:, :, :], ALU.add).then_inc(S["h_ready"], 1)

            def expert_add(n, un):
                e, k = divmod(un, HK)
                if e == 0:
                    return
                pool.wait_ge(S["g_ready"], NU * n + un + 1)
                pool.wait_ge(S["acc_added"], (NU - HK) * n + max(un - 3, 0))
                tt(acc[:, k, :], acc[:, k, :], gg[:, un % 4, :], ALU.add).then_inc(S["acc_added"], 1)

            def expert_out(n):
                pool.wait_ge(S["o_bias"], n + 1)
                tt(o[:, :, :], o[:, :, :], gb[:, :, :], ALU.mult).then_inc(S["o_scaled"], 1)
                pool.wait_ge(S["o_scaled"], n + 1)
                pool.wait_ge(S["kept"], n + 1)
                tt(o[:, :, :], o[:, :, :], x4k[:, :, :], ALU.add).then_inc(S["o_ready"], 1)

            def body(t, live):
                for s in range(NU + 1):
                    if "O" in live and s == 2:
                        expert_out(t - 1)
                    if "C" in live:
                        stage_C(t + 1, s)
                    if "M" in live:
                        stage_M(t + 2, s)
                    if "A" in live:
                        stage_A(t + 3, s)
                    if "X" in live:
                        stage_X(t + 4, s)
                    if "E" in live and s > 0:
                        expert_add(t, s - 1)
                if "S" in live:
                    pool.wait_ge(S["loads_late"], 16 * N_LATE)
                    pool.wait_ge(S["late_vector"], 1)

            setup()
            run_bodies(pool, body)


def kernel(**inputs):
    import numpy as np
    import concourse.bacc as bacc
    from concourse.bass_utils import run_bass_kernel_spmd

    def per_partition(v, rows=1):
        return np.moveaxis(v.reshape(v.shape[:-1] + (rows, P)), -1, 0)

    L = {k: np.asarray(v) for k, v in inputs.items()}
    n_heads = L["L0_attn_D"].shape[0]
    inner = L["L0_attn_norm_w"].shape[0]
    arrays = {
        "x": L["L0_attn_x"], "ln1_w": per_partition(L["L0_attn_ln1_w"]), "ln1_b": per_partition(L["L0_attn_ln1_b"]),
        "ln2_w": per_partition(L["L0_attn_ln2_w"]), "ln2_b": per_partition(L["L0_attn_ln2_b"]),
        "in_projT": L["L0_attn_in_proj_w"].T,
        "conv_w": np.moveaxis(L["L0_attn_conv_w"].reshape(-1, P, 4), 0, 1),
        "conv_b": per_partition(L["L0_attn_conv_b"], 3),
        "dt_bias": L["L0_attn_dt_bias"], "A_log": L["L0_attn_A_log"],
        "D_col": per_partition(np.repeat(L["L0_attn_D"], inner // n_heads), inner // P),
        "norm_w": per_partition(L["L0_attn_norm_w"], inner // P), "out_projT": L["L0_attn_out_proj_w"].T,
        "mlp_w1T": L["L0_attn_mlp_w1"].T, "mlp_b1": per_partition(L["L0_attn_mlp_b1"], 4),
        "mlp_w2T": L["L0_attn_mlp_w2"].T, "mlp_b2": L["L0_attn_mlp_b2"], "gateT": L["L0_ffn_Wg"].T,
        "moe_w1T": np.moveaxis(L["L0_ffn_W1"], 2, 0).reshape(P, -1), "moe_b1": per_partition(L["L0_ffn_b1"], 4),
        "moe_woT": L["L0_ffn_Wo"].T, "moe_bo": L["L0_ffn_bo"], "cT": L["L0_c"].T, "wmod": L["L0_wmod"],
    }
    arrays = {k: np.ascontiguousarray(v) for k, v in arrays.items()}
    nc = bacc.Bacc("TRN2", target_bir_lowering=False, num_devices=1)
    d = {k: nc.dram_tensor("in_" + k, v.shape, mybir.dt.from_np(v.dtype), kind="ExternalInput").ap() for k, v in arrays.items()}
    out = nc.dram_tensor("out", arrays["x"].shape, F32, kind="ExternalOutput").ap()
    build(nc, d, out)
    r = run_bass_kernel_spmd(nc, [{"in_" + k: v for k, v in arrays.items()}], core_ids=[0])
    return r.results[0]["out"]
```
